# Optimizing a Trainium2 kernel written in Bass

```python
import numpy as np
import jax
import jax.numpy as jnp

def _softmax(x, axis=-1):
    return jax.nn.softmax(x, axis=axis)

def _gelu(x):
    return jax.nn.gelu(x, approximate=True)

def _silu(x):
    return jax.nn.silu(x)

def _sigmoid(x):
    return jax.nn.sigmoid(x)

def _layernorm(x, axis=-1, eps=1e-05):
    m = jnp.mean(x, axis=axis, keepdims=True)
    v = jnp.var(x, axis=axis, keepdims=True)
    return (x - m) / jnp.sqrt(v + eps)

def _scatter_add(tgt, idx, src, axis=0):
    return tgt.at[idx].add(src)

def _segment_sum(src, seg, n):
    return jax.ops.segment_sum(src, seg, n)
kernel_name = 'mk_xattn_ffn_d2_seqx_r2_65d3b3'

def setup_inputs(seed: int=0):
    np.random.seed(seed)
    _w = jnp.asarray

    def _rec_inputs():
        import jax
        import jax.numpy as jnp
        _rk = jax.random.key(seed)
        x = -0.0002928 + 1 * jax.random.normal(jax.random.fold_in(_rk, 1), (16, 100, 512), jnp.float32)
        _lenS = 100 - jax.random.randint(jax.random.fold_in(_rk, 7), (16,), 0, max(1, 100 // 4) + 1, jnp.int32)
        _lenS2 = 722 - jax.random.randint(jax.random.fold_in(_rk, 8), (16,), 0, max(1, 722 // 4) + 1, jnp.int32)
        _ctx_1024P = jax.random.normal(jax.random.fold_in(_rk, 11), (16, 16, 512), jnp.float32)
        _ctx_1024c = jax.random.dirichlet(jax.random.fold_in(_rk, 511), 0.3 * jnp.ones((16,), jnp.float32), (16, 722))
        _ctx_1024t = jnp.einsum('bsk,bkd->bsd', _ctx_1024c, _ctx_1024P)
        _ctx_1024t = _ctx_1024t * jax.lax.rsqrt(jnp.mean(jnp.square(_ctx_1024t)) + 1e-12) * 0.953939
        ctx_1024 = -1.39393e-06 + 0.999914 * (_ctx_1024t + 0.3 * jax.random.normal(jax.random.fold_in(_rk, 611), (16, 722, 512), jnp.float32))
        _validS = jnp.arange(100)[None, :] < _lenS[:, None]
        _validS2 = jnp.arange(722)[None, :] < _lenS2[:, None]
        _causal = jnp.tril(jnp.ones((100, 100), dtype=bool))
        mask_BxS2_bf0 = jnp.logical_not(jnp.ones((16, 722), dtype=bool))
        mask_BxS2_bk1 = jnp.broadcast_to(_validS2[:, :], (16, 722))
        return (x, ctx_1024, mask_BxS2_bf0, mask_BxS2_bk1)
    x, ctx_1024, mask_BxS2_bf0, mask_BxS2_bk1 = _rec_inputs()

    def _L0_xattn_setup():
        import jax, jax.numpy as jnp
        import numpy as np
        DIM = 512
        HEADS = 16
        HEAD_DIM = DIM // HEADS
        SCALE = HEAD_DIM ** (-0.5)
        key = jax.random.key(seed)
        ks = jax.random.split(key, 7)
        b, n = (2, 1024)
        x1 = jax.random.normal(ks[0], (b, n, DIM), dtype=jnp.float32)
        x2 = jax.random.normal(ks[1], (b, n, DIM), dtype=jnp.float32)
        s = DIM ** (-0.5)
        wq = jax.random.normal(ks[2], (DIM, DIM), dtype=jnp.float32) * s
        wk = jax.random.normal(ks[3], (DIM, DIM), dtype=jnp.float32) * s
        wv = jax.random.normal(ks[4], (DIM, DIM), dtype=jnp.float32) * s
        wo = jax.random.normal(ks[5], (DIM, DIM), dtype=jnp.float32) * s
        bo = jax.random.normal(ks[6], (DIM,), dtype=jnp.float32) * 0.01
        return {'x1': x1, 'x2': x2, 'wq': wq, 'wk': wk, 'wv': wv, 'wo': wo, 'bo': bo}
    _L0_xattn_all = _L0_xattn_setup()
    _L0_xattn_in = {k: v for k, v in _L0_xattn_all.items() if k in ('wq', 'wk', 'wv', 'wo', 'bo')}
    del _L0_xattn_all

    def _L0_ffn_setup():
        import jax, jax.numpy as jnp
        import numpy as np
        B, S, D = (2, 512, 512)
        E, K, I = (8, 2, 512)
        LIMIT = 7.0
        ALPHA = 1.702

        def _swiglu(t, limit):
            glu = jnp.minimum(t[..., ::2], limit)
            lin = jnp.clip(t[..., 1::2], -limit, limit)
            return glu * jax.nn.sigmoid(ALPHA * glu) * (lin + 1.0)
        key = jax.random.key(seed)
        k0, k1, k2, k3 = jax.random.split(key, 4)
        return {'x': jax.random.normal(k0, (B, S, D), jnp.float32), 'norm_w': jnp.ones((D,), jnp.float32), 'gate_w': jax.random.normal(k1, (E, D), jnp.float32) / np.sqrt(D).astype(np.float32), 'gate_b': jnp.zeros((E,), jnp.float32), 'mlp1_w': jax.random.normal(k2, (E, 2 * I, D), jnp.float32) / np.sqrt(D).astype(np.float32), 'mlp1_b': jnp.zeros((E, 2 * I), jnp.float32), 'mlp2_w': jax.random.normal(k3, (E, D, I), jnp.float32) / np.sqrt(I).astype(np.float32), 'mlp2_b': jnp.zeros((E, D), jnp.float32)}
    _L0_ffn_all = _L0_ffn_setup()
    _L0_ffn_in = {k: v for k, v in _L0_ffn_all.items() if k in ('norm_w', 'gate_w', 'gate_b', 'mlp1_w', 'mlp1_b', 'mlp2_w', 'mlp2_b')}
    del _L0_ffn_all

    def _L1_xattn_setup():
        import jax, jax.numpy as jnp
        import numpy as np
        key = jax.random.key(seed)
        ks = jax.random.split(key, 6)
        B, P, Q, D_IN, D_H = (8, 1024, 1024, 512, 512)
        passage = jax.random.normal(ks[0], (B, P, D_IN), dtype=jnp.float32)
        question = jax.random.normal(ks[1], (B, Q, D_IN), dtype=jnp.float32)
        rep = jax.random.normal(ks[2], (B, Q, D_H), dtype=jnp.float32)
        p_mask = jnp.zeros((B, P), dtype=bool)
        q_mask = jax.random.randint(ks[3], (B, Q), 0, 2).astype(bool)
        limit = np.sqrt(6.0 / (D_IN + D_H))
        U_w = jax.random.uniform(ks[4], (D_H, D_IN), dtype=jnp.float32, minval=-limit, maxval=limit)
        D_param = jnp.ones((1, D_H), dtype=jnp.float32)
        return {'passage': passage, 'p_mask': p_mask, 'question': question, 'q_mask': q_mask, 'rep': rep, 'U_w': U_w, 'D_param': D_param}
    _L1_xattn_all = _L1_xattn_setup()
    _L1_xattn_in = {k: v for k, v in _L1_xattn_all.items() if k in ('U_w', 'D_param')}
    del _L1_xattn_all

    def _L1_ffn_setup():
        import jax, jax.numpy as jnp
        import numpy as np
        CAPACITY_FACTOR = 1.25
        key = jax.random.key(seed)
        k1, k2, k3, k4 = jax.random.split(key, 4)
        B, T, D, F, E = (4, 2048, 512, 2048, 8)
        s = 0.02
        return {'x': jax.random.normal(k1, (B, T, D), dtype=jnp.float32), 'wg': jax.random.normal(k2, (D, E), dtype=jnp.float32) * s, 'W1': jax.random.normal(k3, (E, D, F), dtype=jnp.float32) * s, 'b1': jnp.zeros((E, F), dtype=jnp.float32), 'W2': jax.random.normal(k4, (E, F, D), dtype=jnp.float32) * s, 'b2': jnp.zeros((E, D), dtype=jnp.float32)}
    _L1_ffn_all = _L1_ffn_setup()
    _L1_ffn_in = {k: v for k, v in _L1_ffn_all.items() if k in ('wg', 'W1', 'b1', 'W2', 'b2')}
    del _L1_ffn_all
    return {'x': x, 'ctx_1024': ctx_1024, 'mask_BxS2_bf0': mask_BxS2_bf0, 'mask_BxS2_bk1': mask_BxS2_bk1, 'L0_xattn_wq': _L0_xattn_in['wq'], 'L0_xattn_wk': _L0_xattn_in['wk'], 'L0_xattn_wv': _L0_xattn_in['wv'], 'L0_xattn_wo': _L0_xattn_in['wo'], 'L0_xattn_bo': _L0_xattn_in['bo'], 'L0_ffn_norm_w': _L0_ffn_in['norm_w'], 'L0_ffn_gate_w': _L0_ffn_in['gate_w'], 'L0_ffn_gate_b': _L0_ffn_in['gate_b'], 'L0_ffn_mlp1_w': _L0_ffn_in['mlp1_w'], 'L0_ffn_mlp1_b': _L0_ffn_in['mlp1_b'], 'L0_ffn_mlp2_w': _L0_ffn_in['mlp2_w'], 'L0_ffn_mlp2_b': _L0_ffn_in['mlp2_b'], 'L1_xattn_U_w': _L1_xattn_in['U_w'], 'L1_xattn_D_param': _L1_xattn_in['D_param'], 'L1_ffn_wg': _L1_ffn_in['wg'], 'L1_ffn_W1': _L1_ffn_in['W1'], 'L1_ffn_b1': _L1_ffn_in['b1'], 'L1_ffn_W2': _L1_ffn_in['W2'], 'L1_ffn_b2': _L1_ffn_in['b2']}

def reference(x, ctx_1024, mask_BxS2_bf0, mask_BxS2_bk1, L0_xattn_wq, L0_xattn_wk, L0_xattn_wv, L0_xattn_wo, L0_xattn_bo, L0_ffn_norm_w, L0_ffn_gate_w, L0_ffn_gate_b, L0_ffn_mlp1_w, L0_ffn_mlp1_b, L0_ffn_mlp2_w, L0_ffn_mlp2_b, L1_xattn_U_w, L1_xattn_D_param, L1_ffn_wg, L1_ffn_W1, L1_ffn_b1, L1_ffn_W2, L1_ffn_b2):
    import jax
    import jax.numpy as jnp

    def _L0_xattn_ref(x1, x2, wq, wk, wv, wo, bo):
        import jax, jax.numpy as jnp
        import numpy as np
        DIM = 512
        HEADS = 16
        HEAD_DIM = DIM // HEADS
        SCALE = HEAD_DIM ** (-0.5)
        b, n, _ = x1.shape
        m = x2.shape[1]
        q = (x1 @ wq.T).reshape(b, n, HEADS, HEAD_DIM).transpose(0, 2, 1, 3)
        k = (x2 @ wk.T).reshape(b, m, HEADS, HEAD_DIM).transpose(0, 2, 1, 3)
        v = (x2 @ wv.T).reshape(b, m, HEADS, HEAD_DIM).transpose(0, 2, 1, 3)
        dots = jnp.einsum('bhnd,bhmd->bhnm', q, k) * SCALE
        attn = jax.nn.softmax(dots, axis=-1)
        out = jnp.einsum('bhnm,bhmd->bhnd', attn, v)
        out = out.transpose(0, 2, 1, 3).reshape(b, n, DIM)
        return out @ wo.T + bo

    def _L0_ffn_ref(x, norm_w, gate_w, gate_b, mlp1_w, mlp1_b, mlp2_w, mlp2_b):
        import jax, jax.numpy as jnp
        import numpy as np
        B, S, D = (2, 512, 512)
        E, K, I = (8, 2, 512)
        LIMIT = 7.0
        ALPHA = 1.702

        def _swiglu(t, limit):
            glu = jnp.minimum(t[..., ::2], limit)
            lin = jnp.clip(t[..., 1::2], -limit, limit)
            return glu * jax.nn.sigmoid(ALPHA * glu) * (lin + 1.0)
        eps = jnp.finfo(x.dtype).eps
        h = x * jax.lax.rsqrt(jnp.mean(x * x, axis=-1, keepdims=True) + eps) * norm_w
        flat = h.reshape(-1, D)
        logits = flat @ gate_w.T + gate_b
        vals, idx = jax.lax.top_k(logits, K)
        wts = jax.nn.softmax(vals, axis=-1)
        t1 = jnp.einsum('td,efd->tef', flat, mlp1_w) + mlp1_b
        act = _swiglu(t1, LIMIT)
        y = jnp.einsum('tei,edi->ted', act, mlp2_w) + mlp2_b
        sel = jnp.take_along_axis(y, idx[:, :, None], axis=1)
        out = jnp.sum(sel * wts[:, :, None], axis=1).reshape(x.shape)
        return x + out

    def _L1_xattn_ref(passage, p_mask, question, q_mask, rep, U_w, D_param):
        import jax, jax.numpy as jnp
        import numpy as np
        Up = jax.nn.relu(jnp.einsum('bpi,hi->bph', passage, U_w))
        Uq = jax.nn.relu(jnp.einsum('bqi,hi->bqh', question, U_w))
        Uq = D_param[0] * Uq
        scores = jnp.einsum('bph,bqh->bpq', Up, Uq)
        scores = jnp.where(q_mask[:, None, :], -jnp.inf, scores)
        alpha = jax.nn.softmax(scores, axis=2)
        return jnp.einsum('bpq,bqh->bph', alpha, rep)

    def _L1_ffn_ref(x, wg, W1, b1, W2, b2):
        import jax, jax.numpy as jnp
        import numpy as np
        CAPACITY_FACTOR = 1.25
        B, T, D = x.shape
        E = wg.shape[1]
        N = B * T
        capacity = int(N / E * CAPACITY_FACTOR) + 1
        xf = x.reshape(N, D)
        logits = xf @ wg
        scores = jax.nn.softmax(logits, axis=-1)
        top1 = jnp.argmax(scores, axis=-1)
        combine_w = jnp.take_along_axis(scores, top1[:, None], axis=1)[:, 0]
        oh = jax.nn.one_hot(top1, E, dtype=jnp.int32)
        rank = jnp.take_along_axis(jnp.cumsum(oh, axis=0), top1[:, None], axis=1)[:, 0] - 1
        valid = rank < capacity
        trash = E * capacity
        slot = jnp.where(valid, top1 * capacity + rank, trash)
        buf = jnp.zeros((E * capacity + 1, D), dtype=x.dtype).at[slot].set(xf)
        eb = buf[:E * capacity].reshape(E, capacity, D)
        h = jax.nn.gelu(jnp.einsum('ecd,edf->ecf', eb, W1) + b1[:, None, :], approximate=False)
        y = jnp.einsum('ecf,efd->ecd', h, W2) + b2[:, None, :]
        yf = y.reshape(E * capacity, D)
        gathered = yf[jnp.minimum(slot, E * capacity - 1)]
        out_flat = jnp.where(valid[:, None], gathered, 0.0) * combine_w[:, None]
        return out_flat.reshape(B, T, D)
    x = x + _L0_xattn_ref(_layernorm(x, axis=-1), ctx_1024, L0_xattn_wq, L0_xattn_wk, L0_xattn_wv, L0_xattn_wo, L0_xattn_bo)
    x = x + _L0_ffn_ref(_layernorm(x, axis=-1), L0_ffn_norm_w, L0_ffn_gate_w, L0_ffn_gate_b, L0_ffn_mlp1_w, L0_ffn_mlp1_b, L0_ffn_mlp2_w, L0_ffn_mlp2_b)
    x = x + _L1_xattn_ref(_layernorm(x, axis=-1), mask_BxS2_bf0, ctx_1024, mask_BxS2_bk1, ctx_1024, L1_xattn_U_w, L1_xattn_D_param)
    x = x + _L1_ffn_ref(_layernorm(x, axis=-1), L1_ffn_wg, L1_ffn_W1, L1_ffn_b1, L1_ffn_W2, L1_ffn_b2)
    return x

_drawn_inputs = setup_inputs


def setup_inputs(seed=0):
    import zlib

    import numpy as np

    out = dict(_drawn_inputs(seed))
    spreads = {'L0_ffn_norm_w': (1.0, 0.2),
     'L0_ffn_gate_b': (0.0, 0.1),
     'L0_ffn_mlp1_b': (0.0, 0.1),
     'L0_ffn_mlp2_b': (0.0, 0.1),
     'L1_xattn_D_param': (1.0, 0.2),
     'L1_ffn_b1': (0.0, 0.8),
     'L1_ffn_b2': (0.0, 0.8)}
    factors = {'L1_ffn_wg': 2.759, 'L1_ffn_W1': 2.942, 'L1_ffn_W2': 2.753}
    for name, (base, spread) in spreads.items():
        noise = np.random.default_rng([zlib.crc32(name.encode()), seed]).standard_normal(out[name].shape)
        drawn = base * np.exp(spread * noise) if base else spread * noise
        out[name] = jnp.asarray(drawn.astype(out[name].dtype))
    for name, factor in factors.items():
        out[name] = (out[name] * factor).astype(out[name].dtype)
    return out
```

```python
from contextlib import ExitStack

import numpy as np

import concourse.bass as bass
from concourse import mybir

F32 = mybir.dt.float32
I32 = mybir.dt.int32
U8 = mybir.dt.uint8
ALU = mybir.AluOpType
ACT = mybir.ActivationFunctionType
AX = mybir.AxisListType

P = 128
BATCH, Q, D = 16, 100, 512
KEYS = 722
KH = KEYS // 2
KTILES = -(-KEYS // P)
KLAST = KEYS - (KTILES - 1) * P
DC = D // P
HEADS, HD = 16, 32
HPC = P // HD
TOKENS = BATCH * Q
GROUPS = 4
GT = TOKENS // GROUPS
BPG = BATCH // GROUPS
E = 8
INNER0 = 512
F1 = 2048
BLK = 256
TOP0 = 2
BLOCKS0 = E + (TOP0 * TOKENS - E) // BLK
SLOTS0 = BLOCKS0 * BLK
COUNTS0 = -(-TOKENS // BLK)
CAP1 = int(TOKENS / E * 1.25) + 1
SLOTS1 = E * BLK
LN_EPS = 1e-5
RMS_EPS = float(np.finfo(np.float32).eps)
SCALE = HD ** -0.5
LIMIT, ALPHA = 7.0, 1.702
LOWEST = -3.0e38
FLOOR = -1.0e38
NW = -(-INNER0 // P)


class Chain:

    def __init__(self, eng, sem):
        self.eng, self.sem, self.value = eng, sem, 0

    def __call__(self, ins):
        self.value += 1
        ins.then_inc(self.sem, 1)
        self.eng.wait_ge(self.sem, self.value)


class Scope(ExitStack):

    def __init__(self, nc, name):
        super().__init__()
        self.nc, self.stage = nc, name

    def sb(self, name, shape, dt=F32):
        return self.enter_context(self.nc.sbuf_tensor(f"{self.stage}_{name}", shape, dt))

    def ps(self, name, shape, dt=F32):
        return self.enter_context(self.nc.psum_tensor(f"{self.stage}_{name}", shape, dt))

    def sem(self, name):
        return self.enter_context(self.nc.semaphore(f"{self.stage}_{name}"))

    def sems(self, name, n):
        return [self.sem(f"{name}{i}") for i in range(n)]


def load_constants(nc, io, k):
    with Scope(nc, "const") as s:
        loaded = s.sem("loaded")
        zeroed = s.sem("zeroed")
        pool_made = s.sem("pool_made")
        with nc.Block() as block:
            @block.sync
            def _(sp):
                sp.dma_start(k.x[:, :, :], io["x"]).then_inc(loaded, 16)
                sp.dma_start(k.scale_row[:, :], io["d_param"]).then_inc(loaded, 16)
                sp.wait_ge(loaded, 32)

            @block.gpsimd
            def _(pool):
                step = Chain(pool, pool_made)
                step(pool.memset(k.ident[:, :], 1.0))
                step(pool.affine_select(out=k.ident[:, :], in_=k.ident[:, :], compare_op=ALU.is_equal, fill=0.0,
                                        base=0, pattern=[[-1, P]], channel_multiplier=1))
                step(pool.memset(k.ones[:, :], 1.0))
                step(pool.affine_select(out=k.before[:, :], in_=k.ones[:, :], compare_op=ALU.is_gt, fill=0.0,
                                        base=0, pattern=[[1, P]], channel_multiplier=-1))
                step(pool.iota(k.ramp_i[:, :], [[1, P]], base=0, channel_multiplier=0))
                step(pool.affine_select(out=k.expert_before[:, :, :],
                                        in_=k.ones[:, 0:E * E].rearrange("p (e f) -> p e f", e=E),
                                        compare_op=ALU.is_gt, fill=0.0, base=0,
                                        pattern=[[1, E], [-1, E]], channel_multiplier=0))

            @block.vector
            def _(dve):
                dve.wait_ge(pool_made, 6)
                dve.tensor_copy(k.ramp[:, :], k.ramp_i[:, :]).then_inc(zeroed, 1)
                dve.wait_ge(zeroed, 1)


def layer_norm_stats(dve, step, x, tmp, stats_done):
    with dve.Fori(0, BATCH) as b:
        dve.bn_stats(tmp.stats[:, bass.ds(b, 1), :].rearrange("p a s -> p (a s)"),
                     x[:, bass.ds(b, 1), :].rearrange("p a d -> p (a d)")).then_inc(stats_done, 1)
    dve.wait_ge(stats_done, BATCH)
    even_mean, even_m2 = tmp.stats[:, :, 1], tmp.stats[:, :, 2]
    odd_mean, odd_m2 = tmp.stats[:, :, 4], tmp.stats[:, :, 5]
    step(dve.tensor_tensor(tmp.mean[:, :], even_mean, odd_mean, ALU.add))
    step(dve.tensor_scalar(tmp.mean[:, :], tmp.mean[:, :], 0.5, None, ALU.mult))
    step(dve.tensor_tensor(tmp.a[:, :], even_mean, odd_mean, ALU.subtract))
    step(dve.tensor_tensor(tmp.a[:, :], tmp.a[:, :], tmp.a[:, :], ALU.mult))
    step(dve.tensor_tensor(tmp.var[:, :], even_m2, odd_m2, ALU.add))
    step(dve.tensor_scalar(tmp.var[:, :], tmp.var[:, :], 1.0 / D, None, ALU.mult))
    step(dve.scalar_tensor_tensor(tmp.var[:, :], tmp.a[:, :], 0.25, tmp.var[:, :], ALU.mult, ALU.add))


def inverse_root(dve, step, act_ready, act_done, act_count, root, value, inv, tmp):
    dve.nop().then_inc(act_ready, 1)
    dve.wait_ge(act_done, act_count)
    step(dve.reciprocal(inv[:, :], root[:, :]))
    step(dve.tensor_tensor(tmp[:, :], inv[:, :], inv[:, :], ALU.mult))
    step(dve.tensor_tensor(tmp[:, :], tmp[:, :], value[:, :], ALU.mult))
    step(dve.tensor_scalar(tmp[:, :], tmp[:, :], -0.5, 1.5, ALU.mult, ALU.add))
    step(dve.tensor_tensor(inv[:, :], inv[:, :], tmp[:, :], ALU.mult))


class NormBuffers:
    def __init__(self, s):
        self.stats = s.sb("stats", [Q, BATCH, 6])
        self.mean = s.sb("mean", [Q, BATCH])
        self.var = s.sb("var", [Q, BATCH])
        self.a = s.sb("a", [Q, BATCH])
        self.root = s.sb("root", [Q, BATCH])
        self.inv = s.sb("inv", [Q, BATCH])
        self.value = s.sb("value", [Q, BATCH])
        self.inv2 = s.sb("inv2", [Q, BATCH])
        self.mul2 = s.sb("mul2", [Q, BATCH])


def norm_and_project(nc, io, k, name, weight, out_t, finish):
    with Scope(nc, name) as s:
        n = NormBuffers(s)
        w = s.sb("w", [P, DC, D])
        rows = s.sb("rows", [Q, 2, D])
        rows_t = s.sb("rows_t", [P, DC, TOKENS])
        turned = s.ps("turned", [P, 2, D])
        acc = s.ps("acc", [P, DC, D])
        w_loaded, stats_done, own = s.sem("w_loaded"), s.sem("stats_done"), s.sem("own")
        root_ask, root_done = s.sem("root_ask"), s.sem("root_done")
        norm_done, turn_done = s.sem("norm_done"), s.sem("turn_done")
        turned_free = s.sem("turned_free")
        proj_done, acc_free = s.sem("proj_done"), s.sem("acc_free")
        with nc.Block() as block:
            @block.sync
            def _(sp):
                sp.dma_start(w[:, :, :], io[weight]).then_inc(w_loaded, 16)

            @block.vector
            def _(dve):
                step = Chain(dve, own)
                layer_norm_stats(dve, step, k.x, n, stats_done)
                step(dve.tensor_scalar(n.value[:, :], n.var[:, :], LN_EPS, None, ALU.add))
                inverse_root(dve, step, root_ask, root_done, 1, n.root, n.value, n.inv, n.a)
                with dve.Fori(0, BATCH // 2) as i:
                    for half in range(2):
                        b = 2 * i + half
                        dve.wait_ge(turn_done, b + 1)
                        dve.tensor_scalar(rows[:, half, :], row(k.x, b), n.mean[:, bass.ds(b, 1)],
                                          n.inv[:, bass.ds(b, 1)], ALU.subtract, ALU.mult).then_inc(norm_done, 1)
                dve.sem_inc(acc_free, DC)
                with dve.Fori(0, GROUPS) as g:
                    for m in range(DC):
                        dve.wait_ge(proj_done, g * DC + (m + 1))
                        finish(dve, out_t[:, m, bass.ds(g * GT, GT)], acc[:, m, 0:GT], m).then_inc(acc_free, 1)
                dve.wait_ge(acc_free, DC + GROUPS * DC)

            @block.scalar
            def _(act):
                act.wait_ge(root_ask, 1)
                act.activation(n.root[:, :], n.value[:, :], ACT.Sqrt).then_inc(root_done, 1)
                act.sem_inc(turned_free, 2)
                with act.Fori(0, BATCH // 2) as i:
                    for half in range(2):
                        b = 2 * i + half
                        act.wait_ge(turn_done, b + 3)
                        act.activation(rows_t[:, :, bass.ds(b * Q, Q)],
                                       turned[:, half, 0:DC * Q].rearrange("p (c q) -> p c q", c=DC),
                                       ACT.Copy).then_inc(turned_free, 1)

            @block.tensor
            def _(pe):
                pe.sem_inc(turn_done, 2)
                with pe.Fori(0, BATCH // 2) as i:
                    for half in range(2):
                        b = 2 * i + half
                        pe.wait_ge(norm_done, b + 1)
                        pe.wait_ge(turned_free, b + 1)
                        for c in range(DC):
                            mm = pe.transpose(turned[:, half, c * Q:(c + 1) * Q],
                                              rows[:, half, c * P:(c + 1) * P], k.ident[0:Q, 0:Q])
                        mm.then_inc(turn_done, 1)
                pe.wait_ge(w_loaded, 16)
                with pe.Fori(0, GROUPS) as g:
                    pe.wait_ge(turned_free, 2 + BPG + g * BPG)
                    for m in range(DC):
                        pe.wait_ge(acc_free, g * DC + (m + 1))
                        for c in range(DC):
                            mm = pe.matmul(acc[:, m, 0:GT], w[:, c, m * P:(m + 1) * P],
                                           rows_t[:, c, bass.ds(g * GT, GT)], start=(c == 0), stop=(c == DC - 1))
                        mm.then_inc(proj_done, 1)


def row(t, b):
    return t[:, bass.ds(b, 1), :].rearrange("p a d -> p (a d)")


def first_attention(nc, io, k, q_t):
    K_CHUNKS = 2 * DC
    CHUNKS = K_CHUNKS + KTILES
    assert CHUNKS <= HEADS - 2
    PER = CHUNKS + 1
    with Scope(nc, "xattn0") as s:
        wk, wv, wo = (s.sb(n, [P, DC, D]) for n in ("wk", "wv", "wo"))
        bo = s.sb("bo", [Q, D])
        zeros = s.sb("zeros", [P, 4 * D])
        ctx_t = s.sb("ctx_t", [P, 2, DC, KEYS])
        keys_t = s.sb("keys_t", [P, 2, DC, KEYS])
        vals = s.sb("vals", [P, 2, KTILES, D])
        q_head = s.sb("q_head", [P, 2, HEADS, Q])
        neg_max = s.sb("neg_max", [Q, 2])
        total = s.sb("total", [Q, 2])
        inv_total = s.sb("inv_total", [Q, 2])
        probs = s.sb("probs", [Q, 2, KEYS])
        probs_t = s.sb("probs_t", [P, 2, KTILES, Q])
        out_t = s.sb("out_t", [P, DC, Q])
        out_rows = s.sb("out_rows", [Q, D])
        scores = s.ps("scores", [P, 2, 2, D])
        turned = s.ps("turned", [P, 2, D])
        heads_out = s.ps("heads_out", [P, D])
        proj = s.ps("proj", [P, D])
        w_loaded = s.sem("w_loaded")
        ctx_loaded = s.sems("ctx_loaded", 2)
        proj_done, proj_out = s.sem("proj_done"), s.sem("proj_out")
        q_ready, scores_done, max_ready = s.sem("q_ready"), s.sem("scores_done"), s.sem("max_ready")
        exp_done, inv_done, probs_ready = s.sem("exp_done"), s.sem("inv_done"), s.sem("probs_ready")
        turn_done, probs_t_ready, values_done = s.sem("turn_done"), s.sem("probs_t_ready"), s.sem("values_done")
        out_t_ready, x_added, prepared, zero_q = s.sem("out_t_ready"), s.sem("x_added"), s.sem("prepared"), s.sem("zero_q")
        prepared_psum = s.sem("prepared_psum")
        slots_zeroed = s.sem("slots_zeroed")

        def chunks_before(b):
            return CHUNKS + PER * b

        with nc.Block() as block:
            @block.sync
            def _(sp):
                def load(b, half):
                    sp.dma_start(ctx_t[:, half, :, :], io["ctx_t"][bass.ds(b, 1)].rearrange("a p c n -> p (a c) n"))\
                      .then_inc(ctx_loaded[half], 16)

                sp.dma_start(wk[:, :, :], io["wk"]).then_inc(w_loaded, 16)
                load(0, 0)
                sp.dma_start(wv[:, :, :], io["wv"]).then_inc(w_loaded, 16)
                load(1, 1)
                sp.dma_start(wo[:, :, :], io["wo"]).then_inc(w_loaded, 16)
                sp.dma_start(bo[:, :], io["bo"].partition_broadcast(Q)).then_inc(w_loaded, 16)
                sp.wait_ge(prepared_psum, 2)
                for dst, n in ((io["slots0"], SLOTS0), (io["slots1"][0:SLOTS1, :], SLOTS1)):
                    flat = dst.rearrange("(p r) d -> p (r d)", p=P)
                    for c in range(n * D // P // zeros.shape[1]):
                        w = zeros.shape[1]
                        sp.dma_start(flat[:, c * w:(c + 1) * w], zeros[:, :]).then_inc(slots_zeroed, 16)
                with sp.Fori(0, BATCH // 2 - 1) as i:
                    for half in range(2):
                        b = 2 * i + half
                        sp.wait_ge(proj_done, b * PER + CHUNKS)
                        load(b + 2, half)
                sp.wait_ge(slots_zeroed, 16 * ((SLOTS0 + SLOTS1) * D // P // zeros.shape[1]))

            @block.gpsimd
            def _(pool):
                def place_heads(b, half):
                    for j in range(HPC):
                        rows32 = slice(HD * j, HD * (j + 1))
                        dst = q_head[rows32, half, :, :].rearrange("p (m j) q -> p j m q", j=HPC)[:, j, :, :]
                        pool.tensor_copy(dst, q_t[rows32, :, bass.ds(b * Q, Q)]).then_inc(q_ready, 1)
                        pool.wait_ge(q_ready, b * HPC + (j + 1))

                pool.memset(q_head[:, :, :, :], 0.0).then_inc(zero_q, 1)
                pool.wait_ge(zero_q, 1)
                place_heads(0, 0)
                place_heads(1, 1)
                pool.wait_ge(w_loaded, 64)
                with pool.Fori(0, BATCH) as b:
                    pool.tensor_tensor(row(k.x, b), row(k.x, b), bo[:, :], ALU.add).then_inc(prepared, 1)
                pool.wait_ge(prepared, BATCH)

                def batch(b, half, more, last=False):
                    if more:
                        pool.wait_ge(scores_done, b * HEADS + HEADS)
                        place_heads(b + 2, half)
                    before = b * PER + CHUNKS + (0 if last else CHUNKS)
                    pool.wait_ge(proj_out, before + 2)
                    pool.tensor_tensor(row(k.x, b), row(k.x, b), out_rows[:, :], ALU.add).then_inc(x_added, 1)

                pool.sem_inc(x_added, 1)
                with pool.Fori(0, BATCH // 2 - 1) as i:
                    for half in range(2):
                        batch(2 * i + half, half, True)
                batch(BATCH - 2, 0, False)
                batch(BATCH - 1, 1, False, last=True)
                pool.wait_ge(x_added, 1 + BATCH)

            @block.tensor
            def _(pe):
                def make_chunk(c, before, half):
                    pe.wait_ge(proj_out, before + 1)
                    if c < K_CHUNKS:
                        m, side = divmod(c, 2)
                        for d in range(DC):
                            mm = pe.matmul(proj[:, 0:KH], wk[:, d, m * P:(m + 1) * P],
                                           ctx_t[:, half, d, side * KH:(side + 1) * KH],
                                           start=(d == 0), stop=(d == DC - 1))
                    else:
                        t = c - K_CHUNKS
                        n = P if t < KTILES - 1 else KLAST
                        for d in range(DC):
                            mm = pe.matmul(proj[0:n, :], ctx_t[:, half, d, t * P:t * P + n], wv[:, d, :],
                                           start=(d == 0), stop=(d == DC - 1))
                    mm.then_inc(proj_done, 1)

                def make_scores(g, h, half):
                    for side in range(2):
                        mm = pe.matmul(scores[0:Q, h % 2, side, 0:KH], q_head[:, half, h, :],
                                       keys_t[:, half, h // HPC, side * KH:(side + 1) * KH], start=True, stop=True)
                    mm.then_inc(scores_done, 1)

                def turn(g, h):
                    pe.wait_ge(probs_ready, g + 1)
                    pe.wait_ge(probs_t_ready, g + 1)
                    for t in range(KTILES):
                        n = P if t < KTILES - 1 else KLAST
                        mm = pe.transpose(turned[0:n, t // 3, t % 3 * Q:(t % 3 + 1) * Q],
                                          probs[:, h % 2, t * P:t * P + n], k.ident[0:Q, 0:Q])
                    mm.then_inc(turn_done, 1)

                def times_values(g, h, half):
                    pe.wait_ge(probs_t_ready, g + 2)
                    m, j = divmod(h, HPC)
                    for t in range(KTILES):
                        n = P if t < KTILES - 1 else KLAST
                        mm = pe.matmul(heads_out[HD * j:HD * (j + 1), m * Q:(m + 1) * Q],
                                       vals[0:n, half, t, h * HD:(h + 1) * HD], probs_t[0:n, h % 2, t, :],
                                       start=(t == 0), stop=(t == KTILES - 1), tile_position=(0, HD * j))
                    mm.then_inc(values_done, 1)

                def batch(b, half, more):
                    for h in range(1, HEADS + 1):
                        g = b * HEADS + h
                        if h <= HEADS - 2:
                            pe.wait_ge(exp_done, g)
                            make_scores(g + 1, h + 1, half)
                        elif more:
                            if h == HEADS - 1:
                                pe.wait_ge(proj_out, b * PER + 1 + CHUNKS + K_CHUNKS)
                                pe.wait_ge(q_ready, b * HPC + 2 * HPC)
                            pe.wait_ge(exp_done, g)
                            make_scores(g + 1, h + 1 - HEADS, 1 - half)
                        if more and h <= CHUNKS:
                            if h == 1:
                                pe.wait_ge(ctx_loaded[1 - half], (b + 1 - (1 - half)) * 8 + 16)
                            make_chunk(h - 1, b * PER + CHUNKS + (h - 1), 1 - half)
                        if h < HEADS or more:
                            turn(g, h % HEADS)
                        if h == 1:
                            pe.wait_ge(out_t_ready, b + 1)
                        times_values(g - 1, h - 1, half)
                    pe.wait_ge(out_t_ready, b + 2)
                    before = b * PER + CHUNKS + (CHUNKS if more else 0)
                    pe.wait_ge(proj_out, before + 1)
                    for c in range(DC):
                        mm = pe.matmul(proj[0:Q, :], out_t[:, c, :], wo[:, c, :], start=(c == 0), stop=(c == DC - 1))
                    mm.then_inc(proj_done, 1)

                pe.sem_inc(turn_done, 2)
                pe.sem_inc(values_done, 2)
                pe.wait_ge(prepared_psum, 2)
                pe.wait_ge(w_loaded, 64)
                pe.wait_ge(ctx_loaded[0], 16)
                for c in range(CHUNKS):
                    make_chunk(c, c, 0)
                pe.wait_ge(proj_out, 1 + CHUNKS)
                pe.wait_ge(q_ready, HPC)
                make_scores(0, 0, 0)
                make_scores(1, 1, 0)
                turn(0, 0)
                with pe.Fori(0, BATCH // 2 - 1) as i:
                    for half in range(2):
                        batch(2 * i + half, half, True)
                batch(BATCH - 2, 0, True)
                batch(BATCH - 1, 1, False)

            @block.scalar
            def _(act):
                def take_chunk(c, before, half):
                    act.wait_ge(proj_done, before + 1)
                    if c < K_CHUNKS:
                        m, side = divmod(c, 2)
                        dst, src = keys_t[:, half, m, side * KH:(side + 1) * KH], proj[:, 0:KH]
                    else:
                        t = c - K_CHUNKS
                        n = P if t < KTILES - 1 else KLAST
                        dst, src = vals[0:n, half, t, :], proj[0:n, :]
                    act.activation(dst, src, ACT.Copy).then_inc(proj_out, 1)

                def exponentials(g, h):
                    act.wait_ge(max_ready, g + 1)
                    act.wait_ge(turn_done, g + 1)
                    act.activation(probs[:, h % 2, :].rearrange("p (s n) -> p s n", s=2), scores[0:Q, h % 2, :, 0:KH],
                                   ACT.Exp, bias=neg_max[:, h % 2:h % 2 + 1],
                                   accum_out=total[:, h % 2:h % 2 + 1]).then_inc(exp_done, 1)

                def batch(b, half, more):
                    for h in range(1, HEADS + 1):
                        if h <= HEADS - 2 or more:
                            exponentials(b * HEADS + (h + 1), (h + 1) % HEADS)
                        if more and h <= CHUNKS:
                            take_chunk(h - 1, b * PER + CHUNKS + (h - 1), 1 - half)
                    before = b * PER + CHUNKS + (CHUNKS if more else 0)
                    act.wait_ge(proj_done, before + 1)
                    act.wait_ge(x_added, b + 1)
                    act.activation(out_rows[:, :], proj[0:Q, :], ACT.Copy).then_inc(proj_out, 1)

                act.sem_inc(proj_out, 1)
                for c in range(CHUNKS):
                    take_chunk(c, c, 0)
                exponentials(0, 0)
                exponentials(1, 1)
                with act.Fori(0, BATCH // 2 - 1) as i:
                    for half in range(2):
                        batch(2 * i + half, half, True)
                batch(BATCH - 2, 0, True)
                batch(BATCH - 1, 1, False)

            @block.vector
            def _(dve):
                def maximum(g, h):
                    dve.wait_ge(scores_done, g + 1)
                    dve.tensor_reduce(neg_max[:, h % 2:h % 2 + 1], scores[0:Q, h % 2, :, 0:KH], AX.XY, ALU.max,
                                      negate=True).then_inc(max_ready, 1)

                def divide(g, h):
                    one = slice(h % 2, h % 2 + 1)
                    dve.wait_ge(exp_done, g + 1)
                    dve.reciprocal(inv_total[:, one], total[:, one]).then_inc(inv_done, 1)
                    dve.wait_ge(inv_done, g + 1)
                    dve.tensor_scalar(probs[:, h % 2, :], probs[:, h % 2, :], inv_total[:, one], None,
                                      ALU.mult).then_inc(probs_ready, 1)

                def copy_turned(g, h):
                    dve.wait_ge(turn_done, g + 3)
                    dve.wait_ge(values_done, g + 1)
                    dve.tensor_copy(probs_t[:, h % 2, :, :].rearrange("p (s t) q -> p s (t q)", s=2),
                                    turned[:, :, 0:3 * Q]).then_inc(probs_t_ready, 1)

                def batch(b, half, more):
                    for h in range(1, HEADS + 1):
                        g = b * HEADS + h
                        if h <= HEADS - 2 or more:
                            maximum(g + 1, (h + 1) % HEADS)
                            divide(g + 1, (h + 1) % HEADS)
                        if h < HEADS or more:
                            copy_turned(g, h % HEADS)
                    dve.wait_ge(values_done, b * HEADS + HEADS + 2)
                    dve.tensor_copy(out_t[:, :, :], heads_out[:, 0:DC * Q].rearrange("p (c q) -> p c q", c=DC))\
                       .then_inc(out_t_ready, 1)

                dve.sem_inc(probs_t_ready, 1)
                dve.sem_inc(out_t_ready, 1)
                dve.memset(turned[:, :, :], 0.0).then_inc(prepared_psum, 1)
                dve.memset(zeros[:, :], 0.0).then_inc(prepared_psum, 1)
                dve.wait_ge(prepared_psum, 2)
                maximum(0, 0)
                divide(0, 0)
                maximum(1, 1)
                divide(1, 1)
                copy_turned(0, 0)
                with dve.Fori(0, BATCH // 2 - 1) as i:
                    for half in range(2):
                        batch(2 * i + half, half, True)
                batch(BATCH - 2, 0, True)
                batch(BATCH - 1, 1, False)


def norm_and_route(nc, io, k, name, h_all, logits, gate, rms):
    with Scope(nc, name) as s:
        n = NormBuffers(s)
        w = s.sb("w", [P, DC, E])
        rows = s.sb("rows", [Q, 2, D])
        h = s.sb("h", [Q, 2, D]) if rms else rows
        weight = s.sb("weight", [Q, D])
        rows_t = s.sb("rows_t", [P, 2, DC, Q])
        turned = s.ps("turned", [P, 2, D])
        acc = s.ps("acc", [P, 2, D])
        w_loaded, stats_done, own = s.sem("w_loaded"), s.sem("stats_done"), s.sem("own")
        root_ask, root_done = s.sem("root_ask"), s.sem("root_done")
        norm_done, h_done, turn_done = s.sem("norm_done"), s.sem("h_done"), s.sem("turn_done")
        turned_out, logits_done, logits_out, kept = (
            s.sem("turned_out"), s.sem("logits_done"), s.sem("logits_out"), s.sem("kept"))
        x_added = s.sem("x_added")
        with nc.Block() as block:
            @block.sync
            def _(sp):
                sp.dma_start(w[:, :, :], io[gate]).then_inc(w_loaded, 16)
                sp.dma_start(weight[:, :], io["norm_w"].partition_broadcast(Q)).then_inc(w_loaded, 16)

            @block.vector
            def _(dve):
                step = Chain(dve, own)
                layer_norm_stats(dve, step, k.x, n, stats_done)
                step(dve.tensor_scalar(n.value[:, :], n.var[:, :], LN_EPS, None, ALU.add))
                inverse_root(dve, step, root_ask, root_done, 1, n.root, n.value, n.inv, n.a)
                if rms:
                    step(dve.tensor_tensor(n.a[:, :], n.inv[:, :], n.inv[:, :], ALU.mult))
                    step(dve.tensor_tensor(n.value[:, :], n.a[:, :], n.var[:, :], ALU.mult))
                    step(dve.tensor_scalar(n.value[:, :], n.value[:, :], RMS_EPS, None, ALU.add))
                    inverse_root(dve, step, root_ask, root_done, 2, n.root, n.value, n.inv2, n.a)
                dve.wait_ge(w_loaded, 32)
                dve.sem_inc(logits_out, 2)

                def take_logits(b, half):
                    dve.wait_ge(logits_done, b + 3)
                    dve.tensor_copy(logits[:, bass.ds(b, 1), :].rearrange("p a e -> p (a e)"),
                                    acc[0:Q, half, 0:E]).then_inc(logits_out, 1)

                with dve.Fori(0, BATCH // 2) as i:
                    for half in range(2):
                        b = 2 * i + half
                        dve.wait_ge(turn_done, b + 1)
                        dve.wait_ge(kept, b + 1)
                        dve.tensor_scalar(rows[:, half, :], row(k.x, b), n.mean[:, bass.ds(b, 1)],
                                          n.inv[:, bass.ds(b, 1)], ALU.subtract, ALU.mult).then_inc(norm_done, 1)
                        if rms:
                            dve.wait_ge(norm_done, b + 1)
                            dve.scalar_tensor_tensor(h[:, half, :], rows[:, half, :], n.inv2[:, bass.ds(b, 1)],
                                                     weight[:, :], ALU.mult, ALU.mult).then_inc(h_done, 1)
                    for half in range(2):
                        take_logits(2 * i + half, half)
                dve.wait_ge(logits_out, 2 + BATCH)

            @block.gpsimd
            def _(pool):
                pool.sem_inc(kept, 2)
                with pool.Fori(0, BATCH // 2) as i:
                    for half in range(2):
                        b = 2 * i + half
                        if rms:
                            pool.wait_ge(norm_done, b + 1)
                            pool.tensor_tensor(row(k.x, b), row(k.x, b), rows[:, half, :], ALU.add).then_inc(x_added, 1)
                            pool.wait_ge(x_added, b + 1)
                            pool.wait_ge(h_done, b + 1)
                        else:
                            pool.wait_ge(norm_done, b + 1)
                        pool.tensor_copy(row(h_all, b), h[:, half, :]).then_inc(kept, 1)
                pool.wait_ge(kept, 2 + BATCH)

            @block.scalar
            def _(act):
                act.wait_ge(root_ask, 1)
                act.activation(n.root[:, :], n.value[:, :], ACT.Sqrt).then_inc(root_done, 1)
                if rms:
                    act.wait_ge(root_ask, 2)
                    act.activation(n.root[:, :], n.value[:, :], ACT.Sqrt).then_inc(root_done, 1)
                act.sem_inc(turned_out, 2)
                with act.Fori(0, BATCH // 2) as i:
                    for half in range(2):
                        b = 2 * i + half
                        act.wait_ge(turn_done, b + 3)
                        act.wait_ge(logits_done, b + 1)
                        act.activation(rows_t[:, half, :, :],
                                       turned[:, half, 0:DC * Q].rearrange("p (c q) -> p c q", c=DC),
                                       ACT.Copy).then_inc(turned_out, 1)

            @block.tensor
            def _(pe):
                pe.sem_inc(turn_done, 2)
                pe.sem_inc(logits_done, 2)
                pe.wait_ge(w_loaded, 32)

                def turn(b, half):
                    pe.wait_ge(h_done if rms else norm_done, b + 1)
                    pe.wait_ge(turned_out, b + 1)
                    for c in range(DC):
                        mm = pe.transpose(turned[:, half, c * Q:(c + 1) * Q], h[:, half, c * P:(c + 1) * P],
                                          k.ident[0:Q, 0:Q])
                    mm.then_inc(turn_done, 1)

                def dot_gate(b, half):
                    pe.wait_ge(turned_out, b + 3)
                    pe.wait_ge(logits_out, b + 1)
                    for c in range(DC):
                        mm = pe.matmul(acc[0:Q, half, 0:E], rows_t[:, half, c, :], w[:, c, :],
                                       start=(c == 0), stop=(c == DC - 1))
                    mm.then_inc(logits_done, 1)

                with pe.Fori(0, BATCH // 2) as i:
                    for half in range(2):
                        turn(2 * i + half, half)
                    for half in range(2):
                        dot_gate(2 * i + half, half)


class Routing:

    def __init__(self, s, top):
        self.logits = s.sb("logits", [Q, BATCH, E])
        self.hot = [s.sb(f"hot{i}", [Q, BATCH, E]) for i in range(top)]
        self.weight = [s.sb(f"weight{i}", [Q, BATCH]) for i in range(top)]
        self.slot = [s.sb(f"slot{i}", [Q, BATCH], I32) for i in range(top)]
        self.send = [s.sb(f"send{i}", [Q, BATCH], I32) for i in range(top)]
        self.share = s.sb("share", [Q, BATCH, E])
        self.block_expert = s.sb("block_expert", [1, BLOCKS0], I32)


def along(v, n):
    return v.unsqueeze(2).to_broadcast([v.shape[0], v.shape[1], n])


def between(v, n):
    return v.unsqueeze(1).to_broadcast([v.shape[0], n, v.shape[1]])


def route(nc, io, k, r, name, top, bias):
    with Scope(nc, name) as s:
        gate_bias = s.sb("gate_bias", [Q, E])
        left = s.sb("left", [Q, BATCH, E])
        same = s.sb("same", [Q, BATCH, E])
        peak = [s.sb(f"peak{i}", [Q, BATCH]) for i in range(2)]
        first = s.sb("first", [Q, BATCH])
        t = s.sb("t", [Q, BATCH, E])
        both = s.sb("both", [Q, BATCH, E])
        earlier = s.sb("earlier", [Q, BATCH + 1, E])
        count = s.sb("count", [Q, E])
        blocks = s.sb("blocks", [Q, E])
        start = s.sb("start", [Q, E])
        cover = s.sb("cover", [Q, E, COUNTS0])
        pairs = s.sb("pairs", [Q, E, E])
        owner = s.sb("owner", [Q, BLOCKS0, E])
        owner_of = s.sb("owner_of", [Q, BLOCKS0])
        a, b_, c_ = (s.sb(f"v{i}", [Q, BATCH]) for i in range(3))
        token_i = s.sb("token_i", [Q, BATCH], I32)
        token = s.sb("token", [Q, BATCH])
        rank = s.ps("rank", [P, D])
        totals = s.ps("totals", [P, D])
        loaded, own, ask_exp, exp_done = s.sem("loaded"), s.sem("own"), s.sem("ask_exp"), s.sem("exp_done")
        hot_ready, ranked, token_made = s.sem("hot_ready"), s.sem("ranked"), s.sem("token_made")
        with nc.Block() as block:
            @block.sync
            def _(sp):
                if bias is not None:
                    sp.dma_start(gate_bias[:, :], io[bias].partition_broadcast(Q)).then_inc(loaded, 16)

            @block.gpsimd
            def _(pool):
                pool.iota(token_i[:, :], [[Q, BATCH]], base=0, channel_multiplier=1).then_inc(token_made, 1)

            @block.tensor
            def _(pe):
                pe.wait_ge(hot_ready, 1)
                flat = both[:, :, :].rearrange("p b e -> p (b e)")
                before = earlier[:, 0:BATCH, :].rearrange("p b e -> p (b e)")
                pe.matmul(rank[0:Q, 0:BATCH * E], k.before[0:Q, 0:Q], flat, start=True, stop=False)
                pe.matmul(rank[0:Q, 0:BATCH * E], k.ones[0:Q, 0:Q], before, start=False, stop=True)
                pe.matmul(totals[0:Q, 0:E], k.ones[0:Q, 0:Q], earlier[:, BATCH, :],
                          start=True, stop=True).then_inc(ranked, 1)

            @block.scalar
            def _(act):
                act.wait_ge(ask_exp, 1)
                if top == 2:
                    act.activation(a[:, :], b_[:, :], ACT.Exp).then_inc(exp_done, 1)
                else:
                    act.activation(t[:, :, :], left[:, :, :], ACT.Exp).then_inc(exp_done, 1)

            @block.vector
            def _(dve):
                step = Chain(dve, own)
                if bias is not None:
                    dve.wait_ge(loaded, 16)
                    step(dve.tensor_tensor(r.logits[:, :, :], r.logits[:, :, :], between(gate_bias[:, :], BATCH), ALU.add))
                dve.wait_ge(token_made, 1)
                step(dve.tensor_copy(token[:, :], token_i[:, :]))
                step(dve.tensor_copy(left[:, :, :], r.logits[:, :, :]))
                experts = between(k.ramp[0:Q, 0:E], BATCH)
                for i in range(top):
                    step(dve.tensor_reduce(peak[i][:, :], left[:, :, :], AX.X, ALU.max))
                    step(dve.tensor_tensor(same[:, :, :], left[:, :, :], along(peak[i][:, :], E), ALU.is_equal))
                    step(dve.tensor_scalar(t[:, :, :], same[:, :, :], -float(E), float(E), ALU.mult, ALU.add))
                    step(dve.tensor_tensor(same[:, :, :], same[:, :, :], experts, ALU.mult))
                    step(dve.tensor_tensor(t[:, :, :], t[:, :, :], same[:, :, :], ALU.add))
                    step(dve.tensor_reduce(first[:, :], t[:, :, :], AX.X, ALU.min))
                    step(dve.scalar_tensor_tensor(first[:, :], first[:, :], float(E), first[:, :], ALU.is_lt, ALU.mult))
                    step(dve.tensor_tensor(r.hot[i][:, :, :], experts, along(first[:, :], E), ALU.is_equal))
                    if i + 1 < top:
                        step(dve.scalar_tensor_tensor(left[:, :, :], r.hot[i][:, :, :], LOWEST, left[:, :, :],
                                                      ALU.mult, ALU.add))
                if top == 2:
                    step(dve.tensor_tensor(both[:, :, :], r.hot[0][:, :, :], r.hot[1][:, :, :], ALU.add))
                else:
                    step(dve.tensor_copy(both[:, :, :], r.hot[0][:, :, :]))
                step(dve.memset(earlier[:, 0, :], 0.0))
                for i in range(BATCH):
                    step(dve.tensor_tensor(earlier[:, i + 1, :], earlier[:, i, :], both[:, i, :], ALU.add))
                dve.nop().then_inc(hot_ready, 1)
                if top == 2:
                    step(dve.tensor_tensor(b_[:, :], peak[1][:, :], peak[0][:, :], ALU.subtract))
                    dve.nop().then_inc(ask_exp, 1)
                    dve.wait_ge(exp_done, 1)
                    step(dve.tensor_scalar(c_[:, :], a[:, :], 1.0, None, ALU.add))
                    step(dve.reciprocal(r.weight[0][:, :], c_[:, :]))
                    step(dve.tensor_tensor(r.weight[1][:, :], r.weight[0][:, :], a[:, :], ALU.mult))
                else:
                    step(dve.tensor_tensor(left[:, :, :], r.logits[:, :, :], along(peak[0][:, :], E), ALU.subtract))
                    dve.nop().then_inc(ask_exp, 1)
                    dve.wait_ge(exp_done, 1)
                    step(dve.tensor_reduce(a[:, :], t[:, :, :], AX.X, ALU.add))
                    step(dve.reciprocal(r.weight[0][:, :], a[:, :]))
                dve.wait_ge(ranked, 1)
                ranks = rank[0:Q, 0:BATCH * E].rearrange("p (b e) -> p b e", e=E)
                if top == 2:
                    step(dve.tensor_copy(count[:, :], totals[0:Q, 0:E]))
                    step(dve.tensor_scalar(blocks[:, :], k.ramp[0:Q, 0:E], float(BLK), None, ALU.mult))
                    step(dve.tensor_tensor(cover[:, :, :], along(count[:, :], COUNTS0),
                                           between(blocks[:, 0:COUNTS0], E), ALU.is_gt))
                    step(dve.tensor_reduce(blocks[:, :], cover[:, :, :], AX.X, ALU.add))
                    step(dve.tensor_tensor(pairs[:, :, :], k.expert_before[0:Q, :, :], between(blocks[:, :], E), ALU.mult))
                    step(dve.tensor_reduce(start[:, :], pairs[:, :, :], AX.X, ALU.add))
                    step(dve.tensor_tensor(count[:, :], start[:, :], blocks[:, :], ALU.add))
                    step(dve.tensor_tensor(owner[:, :, :], along(k.ramp[0:Q, 0:BLOCKS0], E),
                                           between(count[:, :], BLOCKS0), ALU.is_ge))
                    step(dve.tensor_reduce(owner_of[:, :], owner[:, :, :], AX.X, ALU.add))
                    step(dve.tensor_scalar(owner_of[:, :], owner_of[:, :], float(E - 1), None, ALU.min))
                    step(dve.tensor_copy(r.block_expert[:, :], owner_of[0:1, :]))
                    step(dve.tensor_scalar(start[:, :], start[:, :], float(BLK), None, ALU.mult))
                else:
                    step(dve.tensor_scalar(start[:, :], k.ramp[0:Q, 0:E], float(BLK), None, ALU.mult))
                for i in range(top):
                    if top == 2:
                        step(dve.tensor_tensor(t[:, :, :], ranks, between(start[:, :], BATCH), ALU.add))
                        step(dve.tensor_tensor(t[:, :, :], t[:, :, :], r.hot[i][:, :, :], ALU.mult))
                        step(dve.tensor_reduce(a[:, :], t[:, :, :], AX.X, ALU.add))
                        step(dve.tensor_copy(r.slot[i][:, :], a[:, :]))
                        step(dve.tensor_copy(r.send[i][:, :], a[:, :]))
                    else:
                        step(dve.tensor_tensor(t[:, :, :], ranks, r.hot[i][:, :, :], ALU.mult))
                        step(dve.tensor_reduce(a[:, :], t[:, :, :], AX.X, ALU.add))
                        step(dve.tensor_scalar(b_[:, :], a[:, :], float(CAP1), None, ALU.is_lt))
                        step(dve.tensor_tensor(t[:, :, :], between(start[:, :], BATCH), r.hot[i][:, :, :], ALU.mult))
                        step(dve.tensor_reduce(c_[:, :], t[:, :, :], AX.X, ALU.add))
                        step(dve.tensor_tensor(a[:, :], a[:, :], c_[:, :], ALU.add))
                        step(dve.tensor_tensor(a[:, :], a[:, :], b_[:, :], ALU.mult))
                        step(dve.tensor_copy(r.slot[i][:, :], a[:, :]))
                        step(dve.tensor_scalar(token[:, :], token[:, :], float(SLOTS1), None, ALU.add))
                        step(dve.tensor_scalar(c_[:, :], b_[:, :], -1.0, 1.0, ALU.mult, ALU.add))
                        step(dve.tensor_tensor(token[:, :], token[:, :], c_[:, :], ALU.mult))
                        step(dve.tensor_tensor(a[:, :], a[:, :], token[:, :], ALU.add))
                        step(dve.tensor_copy(r.send[i][:, :], a[:, :]))
                        step(dve.tensor_tensor(r.weight[i][:, :], r.weight[i][:, :], b_[:, :], ALU.mult))
                step(dve.tensor_tensor(r.share[:, :, :], r.hot[0][:, :, :], along(r.weight[0][:, :], E), ALU.mult))
                for i in range(1, top):
                    step(dve.tensor_tensor(t[:, :, :], r.hot[i][:, :, :], along(r.weight[i][:, :], E), ALU.mult))
                    step(dve.tensor_tensor(r.share[:, :, :], r.share[:, :, :], t[:, :, :], ALU.add))


def send_rows(nc, r, h_all, slots, name, top):
    with Scope(nc, name) as s:
        sent = s.sem("sent")
        with nc.Block() as block:
            @block.gpsimd
            def _(pool):
                for b in range(BATCH):
                    for i in range(top):
                        pool.indirect_dma_start(slots, bass.IndirectOffsetOnAxis(ap=r.send[i][:, b:b + 1], axis=0),
                                                h_all[:, b, :], None).then_inc(sent, 16)
                pool.wait_ge(sent, 16 * BATCH * top)


def gather_outputs(nc, io, k, r, name, top, outputs, out_bias, out):
    with Scope(nc, name) as s:
        bias = s.sb("bias", [E, D])
        got = s.sb("got", [Q, 2, top, D])
        share_t = s.sb("share_t", [E, 2, Q])
        turned = s.ps("turned", [P, 2, D])
        biased = s.ps("biased", [P, 2, D])
        loaded, fetched = s.sem("loaded"), s.sems("fetched", 2)
        turn_done, share_ready, bias_done = s.sem("turn_done"), s.sem("share_ready"), s.sem("bias_done")
        added, own, stored = s.sem("added"), s.sem("own"), s.sem("stored")
        with nc.Block() as block:
            @block.sync
            def _(sp):
                sp.dma_start(bias[:, :], io[out_bias]).then_inc(loaded, 16)
                if out is not None:
                    for b in range(BATCH):
                        sp.wait_ge(added, 2 + b + 1)
                        sp.dma_start(out[b], k.x[:, b, :]).then_inc(stored, 16)
                    sp.wait_ge(stored, 16 * BATCH)

            @block.gpsimd
            def _(pool):
                for b in range(BATCH):
                    pool.wait_ge(added, b + 1)
                    for i in range(top):
                        pool.indirect_dma_start(got[:, b % 2, i, :], None, outputs,
                                                bass.IndirectOffsetOnAxis(ap=r.slot[i][:, b:b + 1], axis=0))\
                            .then_inc(fetched[b % 2], 16)

            @block.tensor
            def _(pe):
                pe.wait_ge(loaded, 16)
                for b in range(BATCH):
                    pe.wait_ge(share_ready, b + 1)
                    pe.transpose(turned[0:E, b % 2, 0:Q], r.share[:, b, :], k.ident[0:Q, 0:Q]).then_inc(turn_done, 1)
                    pe.wait_ge(share_ready, b + 3)
                    pe.wait_ge(added, b + 1)
                    pe.matmul(biased[0:Q, b % 2, :], share_t[:, b % 2, :], bias[:, :],
                              start=True, stop=True).then_inc(bias_done, 1)

            @block.scalar
            def _(act):
                act.sem_inc(share_ready, 2)
                for b in range(BATCH):
                    act.wait_ge(turn_done, b + 1)
                    if b >= 2:
                        act.wait_ge(bias_done, b - 1)
                    act.activation(share_t[:, b % 2, :], turned[0:E, b % 2, 0:Q], ACT.Copy).then_inc(share_ready, 1)

            @block.vector
            def _(dve):
                step = Chain(dve, own)
                dve.sem_inc(added, 2)
                for b in range(BATCH):
                    dve.wait_ge(bias_done, b + 1)
                    step(dve.tensor_tensor(k.x[:, b, :], k.x[:, b, :], biased[0:Q, b % 2, :], ALU.add))
                    dve.wait_ge(fetched[b % 2], 16 * top * (b // 2 + 1))
                    for i in range(top):
                        ins = dve.scalar_tensor_tensor(k.x[:, b, :], got[:, b % 2, i, :], r.weight[i][:, b:b + 1],
                                                       k.x[:, b, :], ALU.mult, ALU.add)
                        if i < top - 1:
                            step(ins)
                        else:
                            ins.then_inc(added, 1)
                dve.wait_ge(added, 2 + BATCH)


def second_attention(nc, io, k, up_t):
    CHUNKS = 2 * DC
    OWN = 4
    with Scope(nc, "xattn1") as s:
        wu = s.sb("wu", [P, DC, D])
        masks = s.sb("masks", [Q, BATCH, KEYS], U8)
        hide = s.sb("hide", [Q, 2, KEYS])
        ctx_t = s.sb("ctx_t", [P, 2, DC, KEYS])
        ctx = s.sb("ctx", [P, 2, KTILES, D])
        up_now = s.sb("up_now", [P, 2, DC, Q])
        uq_t = s.sb("uq_t", [P, 2, DC, KEYS])
        masked = s.sb("masked", [Q, KEYS])
        peak = s.sb("peak", [Q, 2])
        neg_peak = s.sb("neg_peak", [Q, 2])
        total = s.sb("total", [Q, 2])
        inv_total = s.sb("inv_total", [Q, 2])
        probs = s.sb("probs", [Q, 2, KEYS])
        probs_t = s.sb("probs_t", [P, 2, KTILES, Q])
        hid = s.ps("hid", [P, 2, D])
        scores = s.ps("scores", [P, 2, D])
        turned = s.ps("turned", [P, 2, D])
        mixed = s.ps("mixed", [P, 2, D])
        w_loaded, ctx_t_loaded, ctx_loaded = s.sem("w_loaded"), s.sems("ctx_t_loaded", 2), s.sems("ctx_loaded", 2)
        uq_done, uq_out, scores_done, peak_ready = s.sem("uq_done"), s.sem("uq_out"), s.sem("scores_done"), s.sem("peak_ready")
        own, exp_done, turn_done, probs_t_ready = s.sem("own"), s.sem("exp_done"), s.sem("turn_done"), s.sem("probs_t_ready")
        up_ready = s.sem("up_ready")
        mixed_done, x_added, prepared = s.sem("mixed_done"), s.sem("x_added"), s.sem("prepared")
        with nc.Block() as block:
            @block.sync
            def _(sp):
                def load_t(b, half):
                    sp.dma_start(ctx_t[:, half, :, :], io["ctx_t"][bass.ds(b, 1)].rearrange("a p c n -> p (a c) n"))\
                      .then_inc(ctx_t_loaded[half], 16)

                def load(b, half):
                    rows = io["ctx"][bass.ds(b, 1)].rearrange("a n d -> (a n) d")
                    sp.dma_start(ctx[:, half, 0:KTILES - 1, :],
                                 rows[0:KEYS - KLAST, :].rearrange("(t p) d -> p t d", p=P)).then_inc(ctx_loaded[half], 16)
                    sp.dma_start(ctx[0:KLAST, half, KTILES - 1, :], rows[KEYS - KLAST:KEYS, :])\
                      .then_inc(ctx_loaded[half], 16)

                sp.dma_start(wu[:, :, :], io["u"]).then_inc(w_loaded, 16)
                load_t(0, 0)
                sp.dma_start(masks[:, :, :].rearrange("p b n -> p (b n)"), io["mask"].partition_broadcast(Q))\
                  .then_inc(w_loaded, 16)
                load_t(1, 1)
                load(0, 0)
                load(1, 1)
                with sp.Fori(0, BATCH // 2 - 1) as i:
                    for half in range(2):
                        b = 2 * i + half
                        sp.wait_ge(uq_done, CHUNKS * b + CHUNKS)
                        load_t(b + 2, half)
                        sp.wait_ge(mixed_done, b + 3)
                        load(b + 2, half)

            @block.tensor
            def _(pe):
                def make_uq(c, b, half):
                    m, side = divmod(c, 2)
                    pe.wait_ge(uq_out, CHUNKS * b + (c + 1))
                    for d in range(DC):
                        mm = pe.matmul(hid[:, c % 2, 0:KH], wu[:, d, m * P:(m + 1) * P],
                                       ctx_t[:, half, d, side * KH:(side + 1) * KH], start=(d == 0), stop=(d == DC - 1))
                    mm.then_inc(uq_done, 1)

                def make_scores(b, half):
                    pe.wait_ge(uq_out, CHUNKS * b + (CHUNKS + 2))
                    pe.wait_ge(peak_ready, b + 1)
                    for side in range(2):
                        for d in range(DC):
                            mm = pe.matmul(scores[0:Q, side, 0:KH], up_now[:, half, d, :],
                                           uq_t[:, half, d, side * KH:(side + 1) * KH], start=(d == 0), stop=(d == DC - 1))
                    mm.then_inc(scores_done, 1)

                def turn(b, half):
                    pe.wait_ge(exp_done, b + 2)
                    pe.wait_ge(probs_t_ready, b + 1)
                    for t in range(KTILES):
                        n = P if t < KTILES - 1 else KLAST
                        mm = pe.transpose(turned[0:n, t // 3, t % 3 * Q:(t % 3 + 1) * Q],
                                          probs[:, half, t * P:t * P + n], k.ident[0:Q, 0:Q])
                    mm.then_inc(turn_done, 1)

                def mix(b, half):
                    pe.wait_ge(probs_t_ready, b + 2)
                    pe.wait_ge(ctx_loaded[half], (b - half) * 16 + 32)
                    pe.wait_ge(x_added, b + 1)
                    for t in range(KTILES):
                        n = P if t < KTILES - 1 else KLAST
                        mm = pe.matmul(mixed[0:Q, half, :], probs_t[0:n, half, t, :], ctx[0:n, half, t, :],
                                       start=(t == 0), stop=(t == KTILES - 1))
                    mm.then_inc(mixed_done, 1)

                def batch(b, half, more):
                    if more:
                        pe.wait_ge(ctx_t_loaded[1 - half], (b + 1 - (1 - half)) * 8 + 16)
                        for c in range(5):
                            make_uq(c, b + 1, 1 - half)
                    turn(b, half)
                    if more:
                        for c in range(5, CHUNKS):
                            make_uq(c, b + 1, 1 - half)
                    mix(b, half)
                    if more:
                        pe.wait_ge(up_ready, b + 2)
                        make_scores(b + 1, 1 - half)

                pe.sem_inc(mixed_done, 2)
                pe.sem_inc(turn_done, 2)
                pe.wait_ge(w_loaded, 32)
                pe.wait_ge(prepared, 1)
                pe.wait_ge(ctx_t_loaded[0], 16)
                for c in range(CHUNKS):
                    make_uq(c, 0, 0)
                pe.wait_ge(up_ready, 1)
                make_scores(0, 0)
                with pe.Fori(0, BATCH // 2 - 1) as i:
                    for half in range(2):
                        batch(2 * i + half, half, True)
                batch(BATCH - 2, 0, True)
                batch(BATCH - 1, 1, False)

            @block.gpsimd
            def _(pool):
                def bring(b, half):
                    pool.tensor_copy(up_now[:, half, :, :], up_t[:, :, bass.ds(b * Q, Q)]).then_inc(up_ready, 1)

                bring(0, 0)
                bring(1, 1)
                with pool.Fori(0, BATCH // 2 - 1) as i:
                    for half in range(2):
                        b = 2 * i + half
                        pool.wait_ge(scores_done, b + 1)
                        bring(b + 2, half)

            @block.scalar
            def _(act):
                def take_uq(c, b, half):
                    m, side = divmod(c, 2)
                    act.wait_ge(uq_done, CHUNKS * b + (c + 1))
                    act.activation(uq_t[:, half, m, side * KH:(side + 1) * KH], hid[:, c % 2, 0:KH],
                                   ACT.Relu).then_inc(uq_out, 1)

                def exponentials(b, half):
                    act.wait_ge(own, OWN * b + 3)
                    act.wait_ge(turn_done, b + 1)
                    act.activation(probs[:, half, :], masked[:, :], ACT.Exp, bias=neg_peak[:, half:half + 1],
                                   accum_out=total[:, half:half + 1]).then_inc(exp_done, 1)

                act.sem_inc(uq_out, 2)
                for c in range(CHUNKS):
                    take_uq(c, 0, 0)
                exponentials(0, 0)

                def batch(b, half, more):
                    if more:
                        for c in range(CHUNKS):
                            take_uq(c, b + 1, 1 - half)
                        exponentials(b + 1, 1 - half)

                with act.Fori(0, BATCH // 2 - 1) as i:
                    for half in range(2):
                        batch(2 * i + half, half, True)
                batch(BATCH - 2, 0, True)

            @block.vector
            def _(dve):
                def softmax_start(b, half):
                    one = slice(half, half + 1)
                    dve.tensor_scalar(hide[:, half, :], row(masks, b), LOWEST, None, ALU.mult).then_inc(own, 1)
                    dve.wait_ge(scores_done, b + 1)
                    dve.wait_ge(own, OWN * b + 1)
                    dve.wait_ge(exp_done, b + 1)
                    dve.tensor_tensor(masked[:, :].rearrange("p (s n) -> p s n", s=2), scores[0:Q, :, 0:KH],
                                      hide[:, half, :].rearrange("p (s n) -> p s n", s=2), ALU.add).then_inc(own, 1)
                    dve.wait_ge(own, OWN * b + 2)
                    dve.tensor_reduce(peak[:, one], masked[:, :], AX.X, ALU.max).then_inc(peak_ready, 1)
                    dve.wait_ge(peak_ready, b + 2)
                    dve.tensor_scalar(neg_peak[:, one], peak[:, one], FLOOR, -1.0, ALU.max, ALU.mult).then_inc(own, 1)

                def batch(b, half, more):
                    dve.wait_ge(turn_done, b + 3)
                    dve.wait_ge(mixed_done, b + 1)
                    dve.tensor_copy(probs_t[:, half, :, :].rearrange("p (s t) q -> p s (t q)", s=2),
                                    turned[:, :, 0:3 * Q]).then_inc(probs_t_ready, 1)
                    dve.reciprocal(inv_total[:, half:half + 1], total[:, half:half + 1]).then_inc(own, 1)
                    dve.wait_ge(own, OWN * b + OWN)
                    dve.wait_ge(mixed_done, b + 3)
                    dve.scalar_tensor_tensor(row(k.x, b), mixed[0:Q, half, :], inv_total[:, half:half + 1], row(k.x, b),
                                             ALU.mult, ALU.add).then_inc(x_added, 1)
                    if more:
                        softmax_start(b + 1, 1 - half)

                dve.sem_inc(peak_ready, 1)
                dve.sem_inc(exp_done, 1)
                dve.sem_inc(probs_t_ready, 1)
                dve.sem_inc(x_added, 2)
                dve.memset(turned[:, :, :], 0.0).then_inc(prepared, 1)
                dve.wait_ge(prepared, 1)
                dve.wait_ge(w_loaded, 32)
                softmax_start(0, 0)
                with dve.Fori(0, BATCH // 2 - 1) as i:
                    for half in range(2):
                        batch(2 * i + half, half, True)
                batch(BATCH - 2, 0, True)
                batch(BATCH - 1, 1, False)
                dve.wait_ge(x_added, 2 + BATCH)


def experts(nc, io, k, name, blocks, chunks, block_expert, hidden_step):
    gated = block_expert is not None
    PAIRS = NW if gated else F1 // P // 2
    TILES = PAIRS if gated else 2 * PAIRS
    W2_SLOTS = 2 if gated else 1
    with Scope(nc, name) as s:
        w1 = s.sb("w1", [P, 2, DC, 2 * PAIRS * P])
        w2 = s.sb("w2", [P, W2_SLOTS, TILES, D])
        b1 = s.sb("b1", [P, 2, 2 * PAIRS])
        rows = s.sb("rows", [P, 2, 2, D])
        rows_t = s.sb("rows_t", [P, 2, DC, BLK])
        hidden_act = s.sb("hidden_act", [P, 2, TILES, BLK])
        y = s.sb("y", [P, 2, 2, D])
        if gated:
            glu, lin, sig = (s.sb(n, [P, 2, BLK]) for n in ("glu", "lin", "sig"))
        hidden = s.ps("hidden", [P, 4, 2, BLK])
        turned = s.ps("turned", [P, DC, BLK])
        out = s.ps("out", [P, 2, D])
        rows_loaded, w1_loaded, w2_loaded = s.sems("rows_loaded", 2), s.sems("w1_loaded", 2), s.sems("w2_loaded", 2)
        turn_done, rows_t_ready, hidden_done = s.sem("turn_done"), s.sem("rows_t_ready"), s.sem("hidden_done")
        hidden_free, act_ready, out_done = s.sem("hidden_free"), s.sem("act_ready"), s.sem("out_done")
        y_ready, stored = s.sem("y_ready"), s.sems("stored", 2)
        glu_ready, sig_ready, own = s.sem("glu_ready"), s.sem("sig_ready"), s.sem("own")
        slots, results, W1, W2, B1 = (io[n + name[-1]] for n in ("slots", "results", "w1_", "w2_", "b1_"))
        with nc.Block() as block:
            @block.sync
            def _(sp):
                def load(j, half, first):
                    if not first:
                        sp.wait_ge(turn_done, j - 1)
                    sp.dma_start(rows[:, half, :, :], slots[bass.ds(j * BLK, BLK), :].rearrange("(t p) d -> p t d", p=P))\
                      .then_inc(rows_loaded[half], 16)
                    e = j
                    if gated:
                        e = sp.value_load(block_expert[0:1, bass.ds(j, 1)], min_val=0, max_val=E - 1)
                    if not first:
                        sp.wait_ge(hidden_done, (j - 1) * PAIRS)
                    sp.dma_start(w1[:, half, :, :], W1[bass.ds(e, 1)].rearrange("a p c f -> p (a c) f"))\
                      .then_inc(w1_loaded[half], 16)
                    if not first:
                        sp.wait_ge(hidden_free, (j - 1) * PAIRS + 4)
                    sp.dma_start(b1[:, half, :], B1[bass.ds(e, 1)].rearrange("a p f -> p (a f)"))\
                      .then_inc(w1_loaded[half], 16)
                    if gated:
                        load_w2(e, j, half, first)
                    elif not (first and half == 0):
                        load_w2(j - 1, j - 1, 1 - half, first)

                def load_w2(e, j, half, first):
                    if not first:
                        sp.wait_ge(out_done, 2 * (j - 1) if gated else 2 * j)
                    sp.dma_start(w2[:, half % W2_SLOTS, :, :], W2[bass.ds(e, 1)].rearrange("a p c d -> p (a c) d"))\
                      .then_inc(w2_loaded[half], 16)

                load(0, 0, True)
                load(1, 1, True)
                with sp.Fori(1, blocks // 2) as i:
                    for half in range(2):
                        load(2 * i + half, half, False)
                if not gated:
                    load_w2(blocks - 1, blocks - 1, 1, False)

            @block.tensor
            def _(pe):
                def uses(j, half):
                    return (j - half) * 8 + 16

                def make_hidden(j, half):
                    pe.wait_ge(rows_t_ready, j + 2)
                    pe.wait_ge(w1_loaded[half], 2 * uses(j, half))
                    for c in range(PAIRS):
                        pe.wait_ge(hidden_free, j * PAIRS + (c + 1))
                        for side in range(2):
                            f = (side * PAIRS + c if gated else 2 * c + side) * P
                            for d in range(DC):
                                mm = pe.matmul(hidden[:, c % 4, side, :], w1[:, half, d, f:f + P], rows_t[:, half, d, :],
                                               start=(d == 0), stop=(d == DC - 1))
                        mm.then_inc(hidden_done, 1)

                def turn(j, half):
                    pe.wait_ge(rows_loaded[half], uses(j, half))
                    pe.wait_ge(rows_t_ready, j + 1)
                    for t in range(2):
                        for d in range(DC):
                            mm = pe.transpose(turned[:, d, t * P:(t + 1) * P], rows[:, half, t, d * P:(d + 1) * P],
                                              k.ident[:, :])
                    mm.then_inc(turn_done, 1)

                def make_out(j, half):
                    pe.wait_ge(act_ready, j * TILES + TILES)
                    pe.wait_ge(w2_loaded[half], uses(j, half))
                    for t in range(2):
                        pe.wait_ge(y_ready, 2 * j + (t + 1))
                        for c in range(TILES):
                            mm = pe.matmul(out[:, t, :], hidden_act[:, half, c, t * P:(t + 1) * P],
                                           w2[:, half % W2_SLOTS, c, :], start=(c == 0), stop=(c == TILES - 1))
                        mm.then_inc(out_done, 1)

                turn(0, 0)
                make_hidden(0, 0)
                turn(1, 1)
                with pe.Fori(0, blocks // 2 - 1) as i:
                    for half in (1, 0):
                        j = 2 * i + (2 - half)
                        make_hidden(j, half)
                        turn(j + 1, 1 - half)
                        make_out(j - 1, 1 - half)
                make_hidden(blocks - 1, 1)
                make_out(blocks - 2, 0)
                make_out(blocks - 1, 1)

            @block.scalar
            def _(act):
                def copy_turned(j, half):
                    act.wait_ge(turn_done, j + 1)
                    act.activation(rows_t[:, half, :, :], turned[:, :, :], ACT.Copy).then_inc(rows_t_ready, 1)

                def hidden_part(j, half):
                    for c in range(PAIRS):
                        n = j * PAIRS + c
                        if gated:
                            act.wait_ge(glu_ready, j * PAIRS + (c + 1))
                            act.activation(sig[:, c % 2, :], glu[:, c % 2, :], ACT.Sigmoid, scale=ALPHA).then_inc(sig_ready, 1)
                        else:
                            if c == 0:
                                act.wait_ge(w1_loaded[half], 2 * ((j - half) * 8 + 16))
                            act.wait_ge(hidden_done, j * PAIRS + (c + 1))
                            for side in range(2):
                                f = 2 * c + side
                                ins = act.activation(hidden_act[:, half, f, :], hidden[:, c % 4, side, :], ACT.Gelu,
                                                     bias=b1[:, half, f:f + 1]).then_inc(act_ready, 1)
                            act.wait_ge(act_ready, j * TILES + (2 * c + 2))
                            act.sem_inc(hidden_free, 1)

                def take_out(j, half, first):
                    if not first:
                        act.wait_ge(stored[half], (j - half) * 8)
                    for t in range(2):
                        act.wait_ge(out_done, 2 * j + (t + 1))
                        act.activation(y[:, half, t, :], out[:, t, :], ACT.Copy).then_inc(y_ready, 1)
                    act.wait_ge(y_ready, 2 * j + 4)
                    act.dma_start(results[bass.ds(j * BLK, BLK), :].rearrange("(t p) d -> p t d", p=P), y[:, half, :, :])\
                       .then_inc(stored[half], 16)

                act.sem_inc(rows_t_ready, 1)
                act.sem_inc(y_ready, 2)
                if not gated:
                    act.sem_inc(hidden_free, 4)
                copy_turned(0, 0)
                hidden_part(0, 0)
                copy_turned(1, 1)
                hidden_part(1, 1)
                copy_turned(2, 0)
                take_out(0, 0, True)
                hidden_part(2, 0)
                copy_turned(3, 1)
                take_out(1, 1, True)
                with act.Fori(1, blocks // 2 - 1) as i:
                    for half in (1, 0):
                        j = 2 * i + (2 - half)
                        hidden_part(j, half)
                        copy_turned(j + 1, 1 - half)
                        take_out(j - 1, 1 - half, False)
                hidden_part(blocks - 1, 1)
                take_out(blocks - 2, 0, False)
                take_out(blocks - 1, 1, False)
                for half in range(2):
                    act.wait_ge(stored[half], 16 * (blocks // 2))

            @block.vector
            def _(dve):
                if not gated:
                    return

                def hidden_part(j, half):
                    dve.wait_ge(w1_loaded[half], 2 * ((j - half) * 8 + 16))
                    for c in range(PAIRS):
                        at = j * PAIRS + c
                        one = c % 2
                        dve.wait_ge(hidden_done, j * PAIRS + (c + 1))
                        dve.tensor_scalar(glu[:, one, :], hidden[:, c % 4, 0, :], b1[:, half, c:c + 1], LIMIT,
                                          ALU.add, ALU.min).then_inc(glu_ready, 1)
                        dve.tensor_scalar(lin[:, one, :], hidden[:, c % 4, 1, :], b1[:, half, PAIRS + c:PAIRS + c + 1], LIMIT,
                                          ALU.add, ALU.min).then_inc(hidden_free, 1)
                        dve.wait_ge(hidden_free, j * PAIRS + (c + 5))
                        dve.tensor_scalar(lin[:, one, :], lin[:, one, :], -LIMIT, 1.0, ALU.max, ALU.add).then_inc(own, 1)
                        dve.wait_ge(sig_ready, j * PAIRS + (c + 1))
                        dve.tensor_tensor(glu[:, one, :], glu[:, one, :], sig[:, one, :], ALU.mult).then_inc(own, 1)
                        dve.wait_ge(own, 2 * PAIRS * j + (2 * c + 2))
                        dve.tensor_tensor(hidden_act[:, half, c, :], glu[:, one, :], lin[:, one, :], ALU.mult)\
                           .then_inc(act_ready, 1)

                dve.sem_inc(hidden_free, 4)
                with dve.Fori(0, blocks // 2) as i:
                    for half in range(2):
                        hidden_part(2 * i + half, half)


class Keep:
    pass


def build(nc, io, stop=99):
    with ExitStack() as whole:
        def sb(name, shape, dt=F32):
            return whole.enter_context(nc.sbuf_tensor(name, shape, dt))

        k = Keep()
        k.x = sb("x", [Q, BATCH, D])
        k.ident = sb("ident", [P, P])
        k.ones = sb("ones", [P, P])
        k.before = sb("before", [P, P])
        k.ramp_i = sb("ramp_i", [P, P], I32)
        k.ramp = sb("ramp", [P, P])
        k.expert_before = sb("expert_before", [P, E, E])
        k.scale_row = sb("scale_row", [P, DC])
        load_constants(nc, io, k)

        with nc.sbuf_tensor("q_t", [P, DC, TOKENS], F32) as q_t:
            norm_and_project(nc, io, k, "queries", "wq", q_t,
                             lambda dve, out, acc, m: dve.tensor_scalar(out, acc, SCALE, None, ALU.mult))
            first_attention(nc, io, k, q_t)
        if stop > 1:
            with Scope(nc, "ffn0") as s:
                r = Routing(s, TOP0)
                with Scope(nc, "ffn0h") as sh:
                    h_all = sh.sb("h_all", [Q, BATCH, D])
                    norm_and_route(nc, io, k, "route_norm0", h_all, r.logits, "gate0", True)
                    route(nc, io, k, r, "route0", TOP0, "gate_b")
                    send_rows(nc, r, h_all, io["slots0"], "send0", TOP0)
                experts(nc, io, k, "experts0", BLOCKS0, NW, r.block_expert, None)
                gather_outputs(nc, io, k, r, "gather0", TOP0, io["results0"], "b2_0", None)
        if stop > 2:
            with nc.sbuf_tensor("up_t", [P, DC, TOKENS], F32) as up_t:
                norm_and_project(nc, io, k, "up", "u", up_t,
                                 lambda dve, out, acc, m: dve.tensor_scalar(out, acc, 0.0, k.scale_row[:, m:m + 1],
                                                                            ALU.max, ALU.mult))
                second_attention(nc, io, k, up_t)
        if stop > 3:
            with Scope(nc, "ffn1") as s:
                r = Routing(s, 1)
                with Scope(nc, "ffn1h") as sh:
                    h_all = sh.sb("h_all", [Q, BATCH, D])
                    norm_and_route(nc, io, k, "route_norm1", h_all, r.logits, "gate1", False)
                    route(nc, io, k, r, "route1", 1, None)
                    send_rows(nc, r, h_all, io["slots1"], "send1", 1)
                experts(nc, io, k, "experts1", E, None, None, None)
                gather_outputs(nc, io, k, r, "gather1", 1, io["results1"], "b2_1", io["out"])
        else:
            with Scope(nc, "dump") as s:
                d = s.sem("d")
                with nc.Block() as block:
                    @block.sync
                    def _(sp):
                        for b in range(BATCH):
                            sp.dma_start(io["out"][b], k.x[:, b, :]).then_inc(d, 16)
                        sp.wait_ge(d, 16 * BATCH)


def lay_out(a):
    def turn(w):
        return w.T.reshape(-1, P, w.shape[0]).transpose(1, 0, 2)

    w1 = a["L0_ffn_mlp1_w"]
    return {
        "x": a["x"].transpose(1, 0, 2),
        "ctx": a["ctx_1024"],
        "ctx_t": a["ctx_1024"].transpose(0, 2, 1).reshape(BATCH, DC, P, KEYS).transpose(0, 2, 1, 3),
        "mask": a["mask_BxS2_bk1"].reshape(BATCH * KEYS),
        "wq": turn(a["L0_xattn_wq"]), "wk": turn(a["L0_xattn_wk"]), "wv": turn(a["L0_xattn_wv"]),
        "wo": turn(a["L0_xattn_wo"]), "bo": a["L0_xattn_bo"],
        "norm_w": a["L0_ffn_norm_w"], "gate0": turn(a["L0_ffn_gate_w"]), "gate_b": a["L0_ffn_gate_b"],
        "w1_0": w1.reshape(E, INNER0, 2, DC, P).transpose(0, 4, 3, 2, 1).reshape(E, P, DC, 2 * INNER0),
        "b1_0": a["L0_ffn_mlp1_b"].reshape(E, NW, P, 2).transpose(0, 2, 3, 1).reshape(E, P, 2 * NW),
        "w2_0": a["L0_ffn_mlp2_w"].reshape(E, D, NW, P).transpose(0, 3, 2, 1),
        "b2_0": a["L0_ffn_mlp2_b"],
        "u": turn(a["L1_xattn_U_w"]), "d_param": a["L1_xattn_D_param"].reshape(DC, P).T,
        "gate1": a["L1_ffn_wg"].reshape(DC, P, E).transpose(1, 0, 2),
        "w1_1": a["L1_ffn_W1"].reshape(E, DC, P, F1).transpose(0, 2, 1, 3),
        "b1_1": a["L1_ffn_b1"].reshape(E, F1 // P, P).transpose(0, 2, 1),
        "w2_1": a["L1_ffn_W2"].reshape(E, F1 // P, P, D).transpose(0, 2, 1, 3),
        "b2_1": a["L1_ffn_b2"],
    }


def kernel(**inputs):
    import concourse.bacc as bacc
    from concourse.bass_utils import run_bass_kernel_spmd as run

    arrays = {f"in_{n}": np.ascontiguousarray(v) for n, v in lay_out({n: np.asarray(v) for n, v in inputs.items()}).items()}
    nc = bacc.Bacc("TRN2", target_bir_lowering=False, num_devices=1)
    io = {n[3:]: nc.dram_tensor(n, v.shape, mybir.dt.from_np(v.dtype), kind="ExternalInput").ap() for n, v in arrays.items()}
    io["slots0"] = nc.dram_tensor("slots0", [SLOTS0, D], F32, kind="Internal").ap()
    io["results0"] = nc.dram_tensor("results0", [SLOTS0, D], F32, kind="Internal").ap()
    io["slots1"] = nc.dram_tensor("slots1", [SLOTS1 + TOKENS, D], F32, kind="Internal").ap()
    io["results1"] = nc.dram_tensor("results1", [SLOTS1, D], F32, kind="Internal").ap()
    io["out"] = nc.dram_tensor("out", [BATCH, Q, D], F32, kind="ExternalOutput").ap()
    build(nc, io)
    got = run(nc, [arrays], core_ids=[0])
    return got.results[0]["out"]
```

```python
from contextlib import ExitStack

import numpy as np

import concourse.bass as bass
from concourse import mybir

F32 = mybir.dt.float32
F32R = mybir.dt.float32r
I32 = mybir.dt.int32
U8 = mybir.dt.uint8
ALU = mybir.AluOpType
ACT = mybir.ActivationFunctionType
AX = mybir.AxisListType

P = 128
BATCH, Q, D = 16, 100, 512
KEYS = 722
KH = KEYS // 2
KTILES = -(-KEYS // P)
KLAST = KEYS - (KTILES - 1) * P
DC = D // P
HEADS, HD = 16, 32
HPC = P // HD
TOKENS = BATCH * Q
GROUPS = 4
GT = TOKENS // GROUPS
BPG = BATCH // GROUPS
E = 8
INNER0 = 512
F1 = 2048
BLK = 256
TOP0 = 2
BLOCKS0 = E + (TOP0 * TOKENS - E) // BLK
SLOTS0 = BLOCKS0 * BLK
COUNTS0 = -(-TOKENS // BLK)
CAP1 = int(TOKENS / E * 1.25) + 1
SLOTS1 = E * BLK
LN_EPS = 1e-5
RMS_EPS = float(np.finfo(np.float32).eps)
SCALE = HD ** -0.5
LIMIT, ALPHA = 7.0, 1.702
LOWEST = -3.0e38
FLOOR = -1.0e38
NW = -(-INNER0 // P)


class Chain:

    def __init__(self, eng, sem):
        self.eng, self.sem, self.value = eng, sem, 0

    def __call__(self, ins):
        self.value += 1
        ins.then_inc(self.sem, 1)
        self.eng.wait_ge(self.sem, self.value)


class Scope(ExitStack):

    def __init__(self, nc, name):
        super().__init__()
        self.nc, self.stage, self.signals = nc, name, []
        self.callback(self.clear)

    def clear(self):
        if self.signals:
            self.nc.clear_and_free_semaphores(self.signals)
            self.nc.all_engine_barrier(sem_only=True)

    def sb(self, name, shape, dt=F32):
        return self.enter_context(self.nc.sbuf_tensor(f"{self.stage}_{name}", shape, dt))

    def ps(self, name, shape, dt=F32):
        return self.enter_context(self.nc.psum_tensor(f"{self.stage}_{name}", shape, dt))

    def sem(self, name):
        self.signals.append(self.nc.alloc_semaphore(f"{self.stage}_{name}"))
        return self.signals[-1]

    def sems(self, name, n):
        return [self.sem(f"{name}{i}") for i in range(n)]


def load_constants(nc, io, k):
    with Scope(nc, "const") as s:
        loaded = s.sem("loaded")
        zeroed = s.sem("zeroed")
        pool_made = s.sem("pool_made")
        with nc.Block() as block:
            @block.sync
            def _(sp):
                sp.dma_start(k.scale_row[:, :], io["d_param"]).then_inc(loaded, 16)
                sp.wait_ge(loaded, 16)

            @block.gpsimd
            def _(pool):
                step = Chain(pool, pool_made)
                step(pool.memset(k.ident[:, :], 1.0))
                step(pool.affine_select(out=k.ident[:, :], in_=k.ident[:, :], compare_op=ALU.is_equal, fill=0.0,
                                        base=0, pattern=[[-1, P]], channel_multiplier=1))
                step(pool.memset(k.ones[:, :], 1.0))
                step(pool.affine_select(out=k.before[:, :], in_=k.ones[:, :], compare_op=ALU.is_gt, fill=0.0,
                                        base=0, pattern=[[1, P]], channel_multiplier=-1))
                step(pool.iota(k.ramp_i[:, :], [[1, P]], base=0, channel_multiplier=0))
                step(pool.affine_select(out=k.expert_before[:, :, :],
                                        in_=k.ones[:, 0:E * E].rearrange("p (e f) -> p e f", e=E),
                                        compare_op=ALU.is_gt, fill=0.0, base=0,
                                        pattern=[[1, E], [-1, E]], channel_multiplier=0))

            @block.vector
            def _(dve):
                dve.wait_ge(pool_made, 6)
                dve.tensor_copy(k.ramp[:, :], k.ramp_i[:, :]).then_inc(zeroed, 1)
                dve.wait_ge(zeroed, 1)


def layer_norm_stats(dve, step, x, tmp, stats_done, x_loaded=None):
    for g in range(GROUPS):
        if x_loaded is not None:
            dve.wait_ge(x_loaded[g], 16)
        with dve.Fori(g * BPG, (g + 1) * BPG) as b:
            dve.bn_stats(tmp.stats[:, bass.ds(b, 1), :].rearrange("p a s -> p (a s)"),
                         x[:, bass.ds(b, 1), :].rearrange("p a d -> p (a d)")).then_inc(stats_done, 1)
    dve.wait_ge(stats_done, BATCH)
    even_mean, even_m2 = tmp.stats[:, :, 1], tmp.stats[:, :, 2]
    odd_mean, odd_m2 = tmp.stats[:, :, 4], tmp.stats[:, :, 5]
    step(dve.tensor_tensor(tmp.mean[:, :], even_mean, odd_mean, ALU.add))
    step(dve.tensor_scalar(tmp.mean[:, :], tmp.mean[:, :], 0.5, None, ALU.mult))
    step(dve.tensor_tensor(tmp.a[:, :], even_mean, odd_mean, ALU.subtract))
    step(dve.tensor_tensor(tmp.a[:, :], tmp.a[:, :], tmp.a[:, :], ALU.mult))
    step(dve.tensor_tensor(tmp.var[:, :], even_m2, odd_m2, ALU.add))
    step(dve.tensor_scalar(tmp.var[:, :], tmp.var[:, :], 1.0 / D, None, ALU.mult))
    step(dve.scalar_tensor_tensor(tmp.var[:, :], tmp.a[:, :], 0.25, tmp.var[:, :], ALU.mult, ALU.add))


def inverse_root(dve, step, act_ready, act_done, act_count, root, value, inv, tmp):
    dve.nop().then_inc(act_ready, 1)
    dve.wait_ge(act_done, act_count)
    step(dve.reciprocal(inv[:, :], root[:, :]))
    step(dve.tensor_tensor(tmp[:, :], inv[:, :], inv[:, :], ALU.mult))
    step(dve.tensor_tensor(tmp[:, :], tmp[:, :], value[:, :], ALU.mult))
    step(dve.tensor_scalar(tmp[:, :], tmp[:, :], -0.5, 1.5, ALU.mult, ALU.add))
    step(dve.tensor_tensor(inv[:, :], inv[:, :], tmp[:, :], ALU.mult))


class NormBuffers:
    def __init__(self, s):
        self.stats = s.sb("stats", [Q, BATCH, 6])
        self.mean = s.sb("mean", [Q, BATCH])
        self.var = s.sb("var", [Q, BATCH])
        self.a = s.sb("a", [Q, BATCH])
        self.root = s.sb("root", [Q, BATCH])
        self.inv = s.sb("inv", [Q, BATCH])
        self.value = s.sb("value", [Q, BATCH])
        self.inv2 = s.sb("inv2", [Q, BATCH])
        self.mul2 = s.sb("mul2", [Q, BATCH])


def times(pe, out, left, right, first, last):
    (lh, ll), (rh, rl) = left, right
    pe.matmul(out, lh, rh, start=first, stop=False)
    pe.matmul(out, lh, rl, start=False, stop=False)
    return pe.matmul(out, ll, rh, start=False, stop=last)


def high(act, dst, src, func=ACT.Copy):
    return act.activation(dst, src, func)


def low(eng, dst, src, upper):
    return eng.tensor_tensor(dst, src, upper.bitcast(F32), ALU.subtract)


def wait(eng, sem, value):
    if not (isinstance(value, int) and value <= 0):
        eng.wait_ge(sem, value)


def norm_and_project(nc, io, k, name, weight, w_parts, out, steps, source=None):
    with Scope(nc, name) as s:
        n = NormBuffers(s)
        w = s.sb("w", [P, DC, D])
        rows = s.sb("rows", [Q, 2, D])
        rows_h, rows_l = (s.sb(name_, [P, DC, TOKENS], F32R) for name_ in ("rows_h", "rows_l"))
        whole = s.sb("whole", [P, 2, GT])
        parts = [s.sb(name_, [P, 2, DC, GT], F32R) for name_ in ("part_h", "part_l")]
        turned = s.ps("turned", [P, 2, D])
        acc = s.ps("acc", [P, DC, D])
        w_loaded, w_h_ready, w_l_ready = s.sem("w_loaded"), s.sem("w_h_ready"), s.sem("w_l_ready")
        x_loaded = s.sems("x_loaded", GROUPS)
        stats_done, own = s.sem("stats_done"), s.sem("own")
        root_ask, root_done = s.sem("root_ask"), s.sem("root_done")
        norm_done, turn_done = s.sem("norm_done"), s.sem("turn_done")
        rows_h_ready, turned_free = s.sem("rows_h_ready"), s.sem("turned_free")
        proj_done, acc_free = s.sem("proj_done"), s.sem("acc_free")
        part_h_ready, part_l_ready = s.sem("part_h_ready"), s.sem("part_l_ready")
        out_stored = s.sems("out_stored", 2)
        with nc.Block() as block:
            @block.sync
            def _(sp):
                if source is not None:
                    for g in range(GROUPS):
                        at = slice(g * BPG, (g + 1) * BPG)
                        sp.dma_start(k.x[:, at, :], source[:, at, :]).then_inc(x_loaded[g], 16)
                sp.dma_start(w[:, :, :], io[weight]).then_inc(w_loaded, 16)
                with sp.Fori(0, GROUPS // 2) as i:
                    for half in range(2):
                        g = 2 * i + half
                        sp.wait_ge(part_l_ready, g * DC + DC)
                        for part in range(2):
                            sp.dma_start(out[part, :, :, bass.ds(g * GT, GT)],
                                         parts[part][:, half, :, :].bitcast(F32)).then_inc(out_stored[half], 16)
                for half in range(2):
                    sp.wait_ge(out_stored[half], 32 * (GROUPS // 2) + 32)

            @block.vector
            def _(dve):
                step = Chain(dve, own)
                dve.sem_inc(turned_free, 2)
                layer_norm_stats(dve, step, k.x, n, stats_done, x_loaded if source is not None else None)
                step(dve.tensor_scalar(n.value[:, :], n.var[:, :], LN_EPS, None, ALU.add))
                inverse_root(dve, step, root_ask, root_done, 1, n.root, n.value, n.inv, n.a)

                def normalise(b, half):
                    dve.wait_ge(turn_done, b + 1)
                    dve.tensor_scalar(rows[:, half, :], row(k.x, b), n.mean[:, bass.ds(b, 1)],
                                      n.inv[:, bass.ds(b, 1)], ALU.subtract, ALU.mult).then_inc(norm_done, 1)

                def lower_rows(b, half):
                    dve.wait_ge(rows_h_ready, b + 1)
                    at = bass.ds(b * Q, Q)
                    low(dve, rows_l[:, :, at], turned[:, half, 0:DC * Q].rearrange("p (c q) -> p c q", c=DC),
                        rows_h[:, :, at]).then_inc(turned_free, 1)

                normalise(0, 0)
                normalise(1, 1)
                with dve.Fori(0, BATCH // 2 - 1) as i:
                    for half in range(2):
                        lower_rows(2 * i + half, half)
                        normalise(2 * i + (half + 2), half)
                for half in range(2):
                    lower_rows(BATCH - 2 + half, half)
                dve.wait_ge(w_h_ready, 1)
                low(dve, w_parts[1][:, :, :], w[:, :, :], w_parts[0][:, :, :]).then_inc(w_l_ready, 1)
                dve.sem_inc(acc_free, DC)

                def take(g, m):
                    dve.wait_ge(proj_done, g * DC + (m + 1))
                    steps(dve, whole[:, m % 2, :], acc[:, m, 0:GT], m).then_inc(acc_free, 1)

                def lower_out(g, m, half):
                    dve.wait_ge(part_h_ready, g * DC + (m + 1))
                    low(dve, parts[1][:, half, m, :], whole[:, m % 2, :], parts[0][:, half, m, :])\
                        .then_inc(part_l_ready, 1)

                with dve.Fori(0, GROUPS // 2) as i:
                    for half in range(2):
                        g = 2 * i + half
                        take(g, 0)
                        for m in range(1, DC):
                            if m > 1:
                                dve.wait_ge(part_l_ready, g * DC + (m - 1))
                            take(g, m)
                            lower_out(g, m - 1, half)
                        lower_out(g, DC - 1, half)
                        dve.wait_ge(part_l_ready, g * DC + DC)
                dve.wait_ge(acc_free, DC + GROUPS * DC)

            @block.scalar
            def _(act):
                act.wait_ge(root_ask, 1)
                act.activation(n.root[:, :], n.value[:, :], ACT.Sqrt).then_inc(root_done, 1)
                act.wait_ge(w_loaded, 16)
                high(act, w_parts[0][:, :, :], w[:, :, :]).then_inc(w_h_ready, 1)
                with act.Fori(0, BATCH // 2) as i:
                    for half in range(2):
                        b = 2 * i + half
                        act.wait_ge(turn_done, b + 3)
                        high(act, rows_h[:, :, bass.ds(b * Q, Q)],
                             turned[:, half, 0:DC * Q].rearrange("p (c q) -> p c q", c=DC)).then_inc(rows_h_ready, 1)
                for half in range(2):
                    act.sem_inc(out_stored[half], 32)
                with act.Fori(0, GROUPS // 2) as i:
                    for half in range(2):
                        g = 2 * i + half
                        act.wait_ge(out_stored[half], 32 * i + 32)
                        for m in range(DC):
                            act.wait_ge(acc_free, DC + g * DC + (m + 1))
                            high(act, parts[0][:, half, m, :], whole[:, m % 2, :]).then_inc(part_h_ready, 1)

            @block.tensor
            def _(pe):
                pe.sem_inc(turn_done, 2)
                with pe.Fori(0, BATCH // 2) as i:
                    for half in range(2):
                        b = 2 * i + half
                        pe.wait_ge(norm_done, b + 1)
                        pe.wait_ge(turned_free, b + 1)
                        for c in range(DC):
                            mm = pe.transpose(turned[:, half, c * Q:(c + 1) * Q],
                                              rows[:, half, c * P:(c + 1) * P], k.ident[0:Q, 0:Q])
                        mm.then_inc(turn_done, 1)
                pe.wait_ge(w_l_ready, 1)
                with pe.Fori(0, GROUPS) as g:
                    pe.wait_ge(turned_free, 2 + BPG + g * BPG)
                    for m in range(DC):
                        pe.wait_ge(acc_free, g * DC + (m + 1))
                        for c in range(DC):
                            cols, at = slice(m * P, (m + 1) * P), bass.ds(g * GT, GT)
                            mm = times(pe, acc[:, m, 0:GT], [part[:, c, cols] for part in w_parts],
                                       (rows_h[:, c, at], rows_l[:, c, at]), c == 0, c == DC - 1)
                        mm.then_inc(proj_done, 1)


def row(t, b):
    return t[:, bass.ds(b, 1), :].rearrange("p a d -> p (a d)")


def first_attention(nc, io, k):
    SIDES = ((0, KEYS // 2 + 1), (KEYS // 2 + 1, KEYS // 2 - 1))
    N = SIDES[0][1]
    TRIPLE = 3 * HD
    K_CHUNKS = 2 * DC
    CHUNKS = K_CHUNKS + KTILES
    FIRST = 2
    assert CHUNKS + FIRST <= HEADS
    PER = CHUNKS + 1
    PAIR = 2 * HPC
    order = [("k", 0, 0), ("k", 1, 0), ("k", 0, 1), ("k", 1, 1)] + [("v", t, 0) for t in range(KTILES)] + \
            [("k", 2, 0), ("k", 3, 0), ("k", 2, 1), ("k", 3, 1)]
    side_free = [12, 14]
    pair_made = [4, 14]
    pair_packed = [max(made, (i + 1) * PAIR - FIRST - 1) for i, made in enumerate(pair_made)]
    PARTS = (0, 1, 0), (0, 0, 1)
    with Scope(nc, "xattn0") as s:
        wk, wv = ([s.sb(f"{n}{i}", [P, DC, D], F32R) for i in range(2)] for n in ("wk", "wv"))
        wo = s.sb("wo", [P, DC, D])
        bo = s.sb("bo", [Q, D])
        zeros = s.sb("zeros", [P, 2 * D])
        ctx_t = s.sb("ctx_t", [P, DC, KEYS])
        ctx_h, ctx_l = (s.sb(n, [P, DC, KEYS], F32R) for n in ("ctx_h", "ctx_l"))
        keys = [s.sb(n, [P, 2, KEYS], F32R) for n in ("keys_h", "keys_l")]
        k_pack = s.sb("k_pack", [TRIPLE, HEADS, KEYS], F32R)
        q_pack = s.sb("q_pack", [TRIPLE, 2, HEADS, Q], F32R)
        vals = s.sb("vals", [P, 2, KTILES, D])
        neg_max = s.sb("neg_max", [Q, 2])
        total = s.sb("total", [Q, 2])
        inv_total = s.sb("inv_total", [Q, 2])
        probs = s.sb("probs", [Q, 2, KEYS])
        probs_t = s.sb("probs_t", [P, 2, KTILES, Q])
        out_t = s.sb("out_t", [P, DC, Q])
        x = s.sb("x", [Q, 2, D])
        scores = s.ps("scores", [P, 2, 2, D])
        turned = s.ps("turned", [P, 2, D])
        heads_out = s.ps("heads_out", [P, D])
        proj = s.ps("proj", [P, D])
        wk_loaded, wv_loaded, wo_loaded, w_h_ready, w_l_ready = (
            s.sem("wk_loaded"), s.sem("wv_loaded"), s.sem("wo_loaded"), s.sem("w_h_ready"), s.sem("w_l_ready"))
        ctx_loaded, ctx_h_ready, ctx_l_ready = s.sem("ctx_loaded"), s.sem("ctx_h_ready"), s.sem("ctx_l_ready")
        proj_done, bank_free, k_h_ready = s.sem("proj_done"), s.sem("bank_free"), s.sem("k_h_ready")
        packed, q_loaded = s.sems("packed", 2), s.sems("q_loaded", 2)
        scores_done, max_ready = s.sem("scores_done"), s.sem("max_ready")
        exp_done, inv_done, probs_ready = s.sem("exp_done"), s.sem("inv_done"), s.sem("probs_ready")
        turn_done, probs_t_ready, values_done = s.sem("turn_done"), s.sem("probs_t_ready"), s.sem("values_done")
        out_t_ready, prepared_psum = s.sem("out_t_ready"), s.sem("prepared_psum")
        x_loaded, x_stored = s.sems("x_loaded", 2), s.sems("x_stored", 2)
        bo_added, x_added = s.sem("bo_added"), s.sem("x_added")
        slots_zeroed = s.sem("slots_zeroed")

        PACKED = 16 * 3 * HPC

        def index(b, c):
            return CHUNKS + PER * b + c

        def k_index(c):
            return c if c < K_CHUNKS // 2 else c - KTILES

        def bank(n, c):
            return heads_out if n is None and c % 2 else proj

        def side_keys(side):
            return slice(SIDES[side][0], sum(SIDES[side]))

        def scores_of(h):
            return scores[0:Q, h % 2, :, :].rearrange("p s n -> p (s n)")[:, 2:2 * D]\
                .rearrange("p (s n) -> p s n", s=2)[:, :, 0:N - 1]

        with nc.Block() as block:
            @block.sync
            def _(sp):
                def load_ctx(b):
                    sp.dma_start(ctx_t[:, :, :], io["ctx_t"][bass.ds(b, 1)].rearrange("a p c n -> p (a c) n"))\
                      .then_inc(ctx_loaded, 16)

                def load_q(b, half):
                    for group, part in enumerate(PARTS[0]):
                        for j in range(HPC):
                            dst = q_pack[group * HD:(group + 1) * HD, half, :, :].bitcast(F32)\
                                .rearrange("p (m j) q -> p j m q", j=HPC)[:, j, :, :]
                            sp.dma_start(dst, io["q_parts"][part, j * HD:(j + 1) * HD, :, bass.ds(b * Q, Q)])\
                              .then_inc(q_loaded[half], 16)

                def pack(pair):
                    for j in range(HPC):
                        for group, part in enumerate(PARTS[1]):
                            dst = k_pack[group * HD:(group + 1) * HD, pair * PAIR:(pair + 1) * PAIR, :].bitcast(F32)\
                                .rearrange("p (m j) n -> p j m n", j=HPC)[:, j, :, :]
                            sp.dma_start(dst, keys[part][j * HD:(j + 1) * HD, :, :].bitcast(F32))\
                              .then_inc(packed[pair], 16)

                def load_x(b, half):
                    sp.dma_start(x[:, half, :], row(io["x"], b)).then_inc(x_loaded[half], 16)

                sp.dma_start(vals[:, 0, 0:DC, :], io["wk"]).then_inc(wk_loaded, 16)
                load_ctx(0)
                sp.dma_start(vals[:, 1, 0:DC, :], io["wv"]).then_inc(wv_loaded, 16)
                load_q(0, 0)
                load_q(1, 1)
                sp.dma_start(wo[:, :, :], io["wo"]).then_inc(wo_loaded, 16)
                sp.dma_start(bo[:, :], io["bo"].partition_broadcast(Q)).then_inc(wo_loaded, 16)
                load_x(0, 0)
                load_x(1, 1)
                sp.wait_ge(ctx_l_ready, 2)
                load_ctx(1)
                for pair in range(2):
                    if pair:
                        sp.wait_ge(packed[0], PACKED)
                    sp.wait_ge(bank_free, pair_made[pair] + 1)
                    pack(pair)
                sp.wait_ge(prepared_psum, 2)
                for dst, n in ((io["slots0"], SLOTS0), (io["slots1"][0:SLOTS1, :], SLOTS1)):
                    flat = dst.rearrange("(p r) d -> p (r d)", p=P)
                    for c in range(n * D // P // zeros.shape[1]):
                        w = zeros.shape[1]
                        sp.dma_start(flat[:, c * w:(c + 1) * w], zeros[:, :]).then_inc(slots_zeroed, 16)

                def batch(b, i, half, more, after):
                    if after:
                        sp.wait_ge(ctx_l_ready, 2 * b + 4)
                        load_ctx(b + 2)
                    if more:
                        for pair in range(2):
                            sp.wait_ge(bank_free, index(b, pair_packed[pair]) + 1)
                            pack(pair)
                            if pair and after:
                                load_q(b + 2, half)
                    sp.wait_ge(x_added, b + 1)
                    sp.dma_start(row(io["x1"], b), x[:, half, :]).then_inc(x_stored[half], 16)
                    if after:
                        sp.wait_ge(x_stored[half], 16 * i + 16)
                        load_x(b + 2, half)

                with sp.Fori(0, BATCH // 2 - 1) as i:
                    for half in range(2):
                        batch(2 * i + half, i, half, True, True)
                batch(BATCH - 2, BATCH // 2 - 1, 0, True, False)
                batch(BATCH - 1, BATCH // 2 - 1, 1, False, False)
                for half in range(2):
                    sp.wait_ge(x_stored[half], 16 * (BATCH // 2))
                sp.wait_ge(slots_zeroed, 16 * ((SLOTS0 + SLOTS1) * D // P // zeros.shape[1]))

            @block.gpsimd
            def _(pool):
                def split_side(b, side):
                    pool.wait_ge(ctx_h_ready, 2 * b + (side + 1))
                    at = side_keys(side)
                    low(pool, ctx_l[:, :, at], ctx_t[:, :, at], ctx_h[:, :, at]).then_inc(ctx_l_ready, 1)

                def add_bo(i, half):
                    pool.wait_ge(x_loaded[half], 16 * i + 16)
                    pool.tensor_tensor(x[:, half, :], x[:, half, :], bo[:, :], ALU.add).then_inc(bo_added, 1)

                for side in range(2):
                    split_side(0, side)
                pool.wait_ge(wo_loaded, 32)
                add_bo(0, 0)
                for side in range(2):
                    split_side(1, side)
                add_bo(0, 1)
                with pool.Fori(0, BATCH // 2 - 1) as i:
                    for half in range(2):
                        for side in range(2):
                            split_side(2 * i + (half + 2), side)
                        add_bo(i + 1, half)
                pool.wait_ge(bo_added, BATCH)

            @block.tensor
            def _(pe):
                def make_chunk(n, c, half):
                    kind, m, side = order[c]
                    out = bank(n, c)
                    if n is not None:
                        pe.wait_ge(bank_free, index(n, c) + 1)
                    elif c:
                        pe.wait_ge(bank_free, c)
                    if kind == "k":
                        w = SIDES[side][1]
                        for d in range(DC):
                            mm = times(pe, out[:, 0:w], [part[:, d, m * P:(m + 1) * P] for part in wk],
                                       [part[:, d, side_keys(side)] for part in (ctx_h, ctx_l)], d == 0, d == DC - 1)
                    else:
                        w = P if m < KTILES - 1 else KLAST
                        for d in range(DC):
                            mm = times(pe, out[0:w, :], [part[:, d, m * P:m * P + w] for part in (ctx_h, ctx_l)],
                                       [part[:, d, :] for part in wv], d == 0, d == DC - 1)
                    mm.then_inc(proj_done, 1)

                def make_scores(g, h, half):
                    pe.matmul(scores[0:Q, h % 2, 0, 2:2 + N], q_pack[:, half, h, :], k_pack[:, h, 0:N],
                              start=True, stop=True)
                    pe.matmul(scores[0:Q, h % 2, 1, 0:N], q_pack[:, half, h, :], k_pack[:, h, KEYS - N:KEYS],
                              start=True, stop=True).then_inc(scores_done, 1)

                def turn(g, h):
                    pe.wait_ge(probs_ready, g + 1)
                    pe.wait_ge(probs_t_ready, g + 1)
                    for t in range(KTILES):
                        n = P if t < KTILES - 1 else KLAST
                        mm = pe.transpose(turned[0:n, t // 3, t % 3 * Q:(t % 3 + 1) * Q],
                                          probs[:, h % 2, t * P:t * P + n], k.ident[0:Q, 0:Q])
                    mm.then_inc(turn_done, 1)

                def times_values(g, h, half):
                    pe.wait_ge(probs_t_ready, g + 2)
                    m, j = divmod(h, HPC)
                    for t in range(KTILES):
                        n = P if t < KTILES - 1 else KLAST
                        mm = pe.matmul(heads_out[HD * j:HD * (j + 1), m * Q:(m + 1) * Q],
                                       vals[0:n, half, t, h * HD:(h + 1) * HD], probs_t[0:n, h % 2, t, :],
                                       start=(t == 0), stop=(t == KTILES - 1), tile_position=(0, HD * j))
                    mm.then_inc(values_done, 1)

                def project_out(b, n):
                    pe.wait_ge(out_t_ready, b + 2)
                    pe.wait_ge(bank_free, n + 1)
                    for c in range(DC):
                        mm = pe.matmul(proj[0:Q, :], out_t[:, c, :], wo[:, c, :], start=(c == 0), stop=(c == DC - 1))
                    mm.then_inc(proj_done, 1)

                def step(b, i, h, half, more):
                    g = b * HEADS + h
                    if h <= HEADS - 2:
                        if h + 1 == PAIR:
                            pe.wait_ge(packed[1], PACKED * b + PACKED)
                        pe.wait_ge(exp_done, g)
                        make_scores(g + 1, h + 1, half)
                    elif more:
                        if h == HEADS - 1:
                            pe.wait_ge(packed[0], PACKED * b + 2 * PACKED)
                            pe.wait_ge(q_loaded[1 - half], (16 * 3 * HPC) * (i + half) + 16 * 3 * HPC)
                        pe.wait_ge(exp_done, g)
                        make_scores(g + 1, h + 1 - HEADS, 1 - half)
                    if more and FIRST <= h < FIRST + CHUNKS:
                        c = h - FIRST
                        if order[c][0] == "k" and c in (0, 2):
                            pe.wait_ge(ctx_l_ready, 2 * b + (2 + c // 2 + 1))
                        make_chunk(b, c, 1 - half)

                def finish_step(b, h, half, more):
                    g = b * HEADS + h
                    if h < HEADS or more:
                        turn(g, h % HEADS)
                    if h == 1:
                        pe.wait_ge(out_t_ready, b + 1)
                    times_values(g - 1, h - 1, half)

                def batch(b, i, half, more):
                    for h in range(FIRST, HEADS + 1):
                        step(b, i, h, half, more)
                        finish_step(b, h, half, more)
                    if more:
                        step(b + 1, None, 1, 1 - half, more)
                        project_out(b, index(b, CHUNKS))
                        finish_step(b + 1, 1, 1 - half, True)
                    else:
                        project_out(b, index(b, 0))

                pe.sem_inc(turn_done, 2)
                pe.sem_inc(values_done, 2)
                pe.wait_ge(prepared_psum, 2)
                pe.wait_ge(w_l_ready, 1)
                pe.wait_ge(ctx_l_ready, 1)
                for c in range(CHUNKS):
                    if c == 2:
                        pe.wait_ge(ctx_l_ready, 2)
                    if c == K_CHUNKS // 2:
                        pe.wait_ge(w_l_ready, 2)
                    make_chunk(None, c, 0)
                pe.wait_ge(packed[0], PACKED)
                pe.wait_ge(q_loaded[0], 16 * 3 * HPC)
                pe.wait_ge(wo_loaded, 32)
                make_scores(0, 0, 0)
                make_scores(1, 1, 0)
                turn(0, 0)
                pe.wait_ge(bank_free, 1 + CHUNKS)
                step(0, None, 1, 0, True)
                finish_step(0, 1, 0, True)
                with pe.Fori(0, BATCH // 2 - 1) as i:
                    for half in range(2):
                        batch(2 * i + half, i, half, True)
                batch(BATCH - 2, BATCH // 2 - 1, 0, True)
                batch(BATCH - 1, BATCH // 2 - 1, 1, False)

            @block.scalar
            def _(act):
                def take_chunk(n, c, b_k, half):
                    kind, m, side = order[c]
                    if kind == "v" and n is None:
                        return
                    act.wait_ge(proj_done, (index(n, c) if n is not None else c) + 1)
                    if kind == "k":
                        pair = m // 2
                        if n is not None and m % 2 == 0 and side == 0:
                            act.wait_ge(packed[1 - pair], PACKED * n + (PACKED if pair == 0 else 2 * PACKED))
                        elif m == 2 and side == 0:
                            act.wait_ge(packed[0], PACKED)
                        high(act, keys[0][:, m % 2, side_keys(side)], bank(n, c)[:, 0:SIDES[side][1]])\
                            .then_inc(k_h_ready, 1)
                    else:
                        w = P if m < KTILES - 1 else KLAST
                        act.activation(vals[0:w, half, m, :], proj[0:w, :], ACT.Copy).then_inc(bank_free, 1)

                def exponentials(g, h):
                    act.wait_ge(max_ready, g + 1)
                    act.wait_ge(turn_done, g + 1)
                    act.activation(probs[:, h % 2, :].rearrange("p (s n) -> p s n", s=2), scores_of(h),
                                   ACT.Exp, bias=neg_max[:, h % 2:h % 2 + 1],
                                   accum_out=total[:, h % 2:h % 2 + 1]).then_inc(exp_done, 1)

                def split_side(b, side):
                    act.wait_ge(ctx_loaded, 16 * b + 16)
                    at = side_keys(side)
                    high(act, ctx_h[:, :, at], ctx_t[:, :, at]).then_inc(ctx_h_ready, 1)

                def step(b, h, half, more, after):
                    if h <= HEADS - 2 or more:
                        exponentials(b * HEADS + (h + 1), (h + 1) % HEADS)
                    if more and FIRST <= h < FIRST + CHUNKS:
                        take_chunk(b, h - FIRST, b * K_CHUNKS + K_CHUNKS, 1 - half)
                    if after and h - FIRST in side_free:
                        side = side_free.index(h - FIRST)
                        act.wait_ge(proj_done, index(b, side_free[side]))
                        split_side(b + 2, side)

                def batch(b, half, more, after):
                    for h in range(FIRST, HEADS + 1):
                        step(b, h, half, more, after)
                    if more:
                        step(b + 1, 1, 1 - half, True, False)

                act.wait_ge(wk_loaded, 16)
                high(act, wk[0][:, :, :], vals[:, 0, 0:DC, :]).then_inc(w_h_ready, 1)
                for side in range(2):
                    split_side(0, side)
                act.wait_ge(wv_loaded, 16)
                high(act, wv[0][:, :, :], vals[:, 1, 0:DC, :]).then_inc(w_h_ready, 1)
                for c in range(CHUNKS):
                    take_chunk(None, c, 0, 0)
                for side in range(2):
                    act.wait_ge(proj_done, side_free[side])
                    split_side(1, side)
                exponentials(0, 0)
                exponentials(1, 1)
                step(0, 1, 0, True, False)
                with act.Fori(0, BATCH // 2 - 1) as i:
                    for half in range(2):
                        batch(2 * i + half, half, True, True)
                batch(BATCH - 2, 0, True, False)
                batch(BATCH - 1, 1, False, False)

            @block.vector
            def _(dve):
                def maximum(g, h):
                    dve.wait_ge(scores_done, g + 1)
                    dve.tensor_reduce(neg_max[:, h % 2:h % 2 + 1], scores_of(h), AX.XY, ALU.max,
                                      negate=True).then_inc(max_ready, 1)

                def divide(g, h):
                    one = slice(h % 2, h % 2 + 1)
                    dve.wait_ge(exp_done, g + 1)
                    dve.reciprocal(inv_total[:, one], total[:, one]).then_inc(inv_done, 1)
                    dve.wait_ge(inv_done, g + 1)
                    dve.tensor_scalar(probs[:, h % 2, :], probs[:, h % 2, :], inv_total[:, one], None,
                                      ALU.mult).then_inc(probs_ready, 1)

                def copy_turned(g, h):
                    dve.wait_ge(turn_done, g + 3)
                    dve.wait_ge(values_done, g + 1)
                    dve.tensor_copy(probs_t[:, h % 2, :, :].rearrange("p (s t) q -> p s (t q)", s=2),
                                    turned[:, :, 0:3 * Q]).then_inc(probs_t_ready, 1)

                def take_chunk(n, c, half):
                    kind, m, side = order[c]
                    if kind == "k":
                        before = n * K_CHUNKS + K_CHUNKS if n is not None else 0
                        dve.wait_ge(k_h_ready, before + (k_index(c) + 1))
                        at = side_keys(side)
                        low(dve, keys[1][:, m % 2, at], bank(n, c)[:, 0:SIDES[side][1]], keys[0][:, m % 2, at])\
                            .then_inc(bank_free, 1)
                    elif n is None:
                        w = P if m < KTILES - 1 else KLAST
                        dve.wait_ge(proj_done, c + 1)
                        dve.tensor_copy(vals[0:w, half, m, :], bank(n, c)[0:w, :]).then_inc(bank_free, 1)

                def step(b, h, half, more):
                    g = b * HEADS + h
                    if h <= HEADS - 2 or more:
                        maximum(g + 1, (h + 1) % HEADS)
                        divide(g + 1, (h + 1) % HEADS)
                    if more and FIRST <= h < FIRST + CHUNKS:
                        take_chunk(b, h - FIRST, 1 - half)
                    if h < HEADS or more:
                        copy_turned(g, h % HEADS)

                def add_output(b, n, half):
                    dve.wait_ge(proj_done, n + 1)
                    dve.wait_ge(bo_added, b + 1)
                    dve.tensor_tensor(x[:, half, :], proj[0:Q, :], x[:, half, :], ALU.add).then_inc(x_added, 1)
                    dve.wait_ge(x_added, b + 1)
                    dve.sem_inc(bank_free, 1)

                def batch(b, half, more):
                    for h in range(FIRST, HEADS + 1):
                        step(b, h, half, more)
                    dve.wait_ge(values_done, b * HEADS + HEADS + 2)
                    dve.tensor_copy(out_t[:, :, :], heads_out[:, 0:DC * Q].rearrange("p (c q) -> p c q", c=DC))\
                       .then_inc(out_t_ready, 1)
                    if more:
                        step(b + 1, 1, 1 - half, True)
                    add_output(b, index(b, CHUNKS if more else 0), half)

                dve.sem_inc(bank_free, 1)
                dve.sem_inc(probs_t_ready, 1)
                dve.sem_inc(out_t_ready, 1)
                dve.memset(turned[:, :, :], 0.0).then_inc(prepared_psum, 1)
                dve.memset(zeros[:, :], 0.0).then_inc(prepared_psum, 1)
                dve.wait_ge(prepared_psum, 2)
                for i, w in enumerate((wk, wv)):
                    dve.wait_ge(w_h_ready, i + 1)
                    low(dve, w[1][:, :, :], vals[:, i, 0:DC, :], w[0][:, :, :]).then_inc(w_l_ready, 1)
                for c in range(CHUNKS):
                    if c == K_CHUNKS // 2:
                        dve.wait_ge(w_l_ready, 2)
                    take_chunk(None, c, 0)
                maximum(0, 0)
                divide(0, 0)
                maximum(1, 1)
                divide(1, 1)
                copy_turned(0, 0)
                step(0, 1, 0, True)
                with dve.Fori(0, BATCH // 2 - 1) as i:
                    for half in range(2):
                        batch(2 * i + half, half, True)
                batch(BATCH - 2, 0, True)
                batch(BATCH - 1, 1, False)


def norm_and_route(nc, io, k, name, h_all, logits, gate, rms, source=None):
    with Scope(nc, name) as s:
        n = NormBuffers(s)
        w = s.sb("w", [P, DC, E])
        rows = s.sb("rows", [Q, 2, D])
        h = s.sb("h", [Q, 2, D]) if rms else rows
        weight = s.sb("weight", [Q, D])
        rows_t = s.sb("rows_t", [P, 2, DC, Q])
        turned = s.ps("turned", [P, 2, D])
        acc = s.ps("acc", [P, 2, D])
        w_loaded, stats_done, own = s.sem("w_loaded"), s.sem("stats_done"), s.sem("own")
        root_ask, root_done = s.sem("root_ask"), s.sem("root_done")
        norm_done, h_done, turn_done = s.sem("norm_done"), s.sem("h_done"), s.sem("turn_done")
        turned_out, logits_done, logits_out, kept = (
            s.sem("turned_out"), s.sem("logits_done"), s.sem("logits_out"), s.sem("kept"))
        x_added = s.sem("x_added")
        x_loaded = s.sems("x_loaded", GROUPS)
        with nc.Block() as block:
            @block.sync
            def _(sp):
                if source is not None:
                    for g in range(GROUPS):
                        at = slice(g * BPG, (g + 1) * BPG)
                        sp.dma_start(k.x[:, at, :], source[:, at, :]).then_inc(x_loaded[g], 16)
                sp.dma_start(w[:, :, :], io[gate]).then_inc(w_loaded, 16)
                sp.dma_start(weight[:, :], io["norm_w"].partition_broadcast(Q)).then_inc(w_loaded, 16)

            @block.vector
            def _(dve):
                step = Chain(dve, own)
                layer_norm_stats(dve, step, k.x, n, stats_done, x_loaded if source is not None else None)
                step(dve.tensor_scalar(n.value[:, :], n.var[:, :], LN_EPS, None, ALU.add))
                inverse_root(dve, step, root_ask, root_done, 1, n.root, n.value, n.inv, n.a)
                if rms:
                    step(dve.tensor_tensor(n.a[:, :], n.inv[:, :], n.inv[:, :], ALU.mult))
                    step(dve.tensor_tensor(n.value[:, :], n.a[:, :], n.var[:, :], ALU.mult))
                    step(dve.tensor_scalar(n.value[:, :], n.value[:, :], RMS_EPS, None, ALU.add))
                    inverse_root(dve, step, root_ask, root_done, 2, n.root, n.value, n.inv2, n.a)
                dve.wait_ge(w_loaded, 32)
                dve.sem_inc(logits_out, 2)

                def take_logits(b, half):
                    dve.wait_ge(logits_done, b + 3)
                    dve.tensor_copy(logits[:, bass.ds(b, 1), :].rearrange("p a e -> p (a e)"),
                                    acc[0:Q, half, 0:E]).then_inc(logits_out, 1)

                with dve.Fori(0, BATCH // 2) as i:
                    for half in range(2):
                        b = 2 * i + half
                        dve.wait_ge(turn_done, b + 1)
                        dve.wait_ge(kept, b + 1)
                        dve.tensor_scalar(rows[:, half, :], row(k.x, b), n.mean[:, bass.ds(b, 1)],
                                          n.inv[:, bass.ds(b, 1)], ALU.subtract, ALU.mult).then_inc(norm_done, 1)
                        if rms:
                            dve.wait_ge(norm_done, b + 1)
                            dve.scalar_tensor_tensor(h[:, half, :], rows[:, half, :], n.inv2[:, bass.ds(b, 1)],
                                                     weight[:, :], ALU.mult, ALU.mult).then_inc(h_done, 1)
                    for half in range(2):
                        take_logits(2 * i + half, half)
                dve.wait_ge(logits_out, 2 + BATCH)

            @block.gpsimd
            def _(pool):
                pool.sem_inc(kept, 2)
                with pool.Fori(0, BATCH // 2) as i:
                    for half in range(2):
                        b = 2 * i + half
                        if rms:
                            pool.wait_ge(norm_done, b + 1)
                            pool.tensor_tensor(row(k.x, b), row(k.x, b), rows[:, half, :], ALU.add).then_inc(x_added, 1)
                            pool.wait_ge(x_added, b + 1)
                            pool.wait_ge(h_done, b + 1)
                        else:
                            pool.wait_ge(norm_done, b + 1)
                        pool.tensor_copy(row(h_all, b), h[:, half, :]).then_inc(kept, 1)
                pool.wait_ge(kept, 2 + BATCH)

            @block.scalar
            def _(act):
                act.wait_ge(root_ask, 1)
                act.activation(n.root[:, :], n.value[:, :], ACT.Sqrt).then_inc(root_done, 1)
                if rms:
                    act.wait_ge(root_ask, 2)
                    act.activation(n.root[:, :], n.value[:, :], ACT.Sqrt).then_inc(root_done, 1)
                act.sem_inc(turned_out, 2)
                with act.Fori(0, BATCH // 2) as i:
                    for half in range(2):
                        b = 2 * i + half
                        act.wait_ge(turn_done, b + 3)
                        act.wait_ge(logits_done, b + 1)
                        act.activation(rows_t[:, half, :, :],
                                       turned[:, half, 0:DC * Q].rearrange("p (c q) -> p c q", c=DC),
                                       ACT.Copy).then_inc(turned_out, 1)

            @block.tensor
            def _(pe):
                pe.sem_inc(turn_done, 2)
                pe.sem_inc(logits_done, 2)
                pe.wait_ge(w_loaded, 32)

                def turn(b, half):
                    pe.wait_ge(h_done if rms else norm_done, b + 1)
                    pe.wait_ge(turned_out, b + 1)
                    for c in range(DC):
                        mm = pe.transpose(turned[:, half, c * Q:(c + 1) * Q], h[:, half, c * P:(c + 1) * P],
                                          k.ident[0:Q, 0:Q])
                    mm.then_inc(turn_done, 1)

                def dot_gate(b, half):
                    pe.wait_ge(turned_out, b + 3)
                    pe.wait_ge(logits_out, b + 1)
                    for c in range(DC):
                        mm = pe.matmul(acc[0:Q, half, 0:E], rows_t[:, half, c, :], w[:, c, :],
                                       start=(c == 0), stop=(c == DC - 1))
                    mm.then_inc(logits_done, 1)

                with pe.Fori(0, BATCH // 2) as i:
                    for half in range(2):
                        turn(2 * i + half, half)
                    for half in range(2):
                        dot_gate(2 * i + half, half)


class Routing:

    def __init__(self, s, top):
        self.logits = s.sb("logits", [Q, BATCH, E])
        self.hot = [s.sb(f"hot{i}", [Q, BATCH, E]) for i in range(top)]
        self.weight = [s.sb(f"weight{i}", [Q, BATCH]) for i in range(top)]
        self.slot = [s.sb(f"slot{i}", [Q, BATCH], I32) for i in range(top)]
        self.send = [s.sb(f"send{i}", [Q, BATCH], I32) for i in range(top)]
        self.share = s.sb("share", [Q, BATCH, E])
        self.block_expert = s.sb("block_expert", [1, BLOCKS0], I32)


def along(v, n):
    return v.unsqueeze(2).to_broadcast([v.shape[0], v.shape[1], n])


def between(v, n):
    return v.unsqueeze(1).to_broadcast([v.shape[0], n, v.shape[1]])


def route(nc, io, k, r, name, top, bias):
    with Scope(nc, name) as s:
        gate_bias = s.sb("gate_bias", [Q, E])
        left = s.sb("left", [Q, BATCH, E])
        same = s.sb("same", [Q, BATCH, E])
        peak = [s.sb(f"peak{i}", [Q, BATCH]) for i in range(2)]
        first = s.sb("first", [Q, BATCH])
        t = s.sb("t", [Q, BATCH, E])
        both = s.sb("both", [Q, BATCH, E])
        earlier = s.sb("earlier", [Q, BATCH + 1, E])
        count = s.sb("count", [Q, E])
        blocks = s.sb("blocks", [Q, E])
        start = s.sb("start", [Q, E])
        cover = s.sb("cover", [Q, E, COUNTS0])
        pairs = s.sb("pairs", [Q, E, E])
        owner = s.sb("owner", [Q, BLOCKS0, E])
        owner_of = s.sb("owner_of", [Q, BLOCKS0])
        a, b_, c_ = (s.sb(f"v{i}", [Q, BATCH]) for i in range(3))
        token_i = s.sb("token_i", [Q, BATCH], I32)
        token = s.sb("token", [Q, BATCH])
        rank = s.ps("rank", [P, D])
        totals = s.ps("totals", [P, D])
        loaded, own, ask_exp, exp_done = s.sem("loaded"), s.sem("own"), s.sem("ask_exp"), s.sem("exp_done")
        hot_ready, ranked, token_made = s.sem("hot_ready"), s.sem("ranked"), s.sem("token_made")
        with nc.Block() as block:
            @block.sync
            def _(sp):
                if bias is not None:
                    sp.dma_start(gate_bias[:, :], io[bias].partition_broadcast(Q)).then_inc(loaded, 16)

            @block.gpsimd
            def _(pool):
                pool.iota(token_i[:, :], [[Q, BATCH]], base=0, channel_multiplier=1).then_inc(token_made, 1)

            @block.tensor
            def _(pe):
                pe.wait_ge(hot_ready, 1)
                flat = both[:, :, :].rearrange("p b e -> p (b e)")
                before = earlier[:, 0:BATCH, :].rearrange("p b e -> p (b e)")
                pe.matmul(rank[0:Q, 0:BATCH * E], k.before[0:Q, 0:Q], flat, start=True, stop=False)
                pe.matmul(rank[0:Q, 0:BATCH * E], k.ones[0:Q, 0:Q], before, start=False, stop=True)
                pe.matmul(totals[0:Q, 0:E], k.ones[0:Q, 0:Q], earlier[:, BATCH, :],
                          start=True, stop=True).then_inc(ranked, 1)

            @block.scalar
            def _(act):
                act.wait_ge(ask_exp, 1)
                if top == 2:
                    act.activation(a[:, :], b_[:, :], ACT.Exp).then_inc(exp_done, 1)
                else:
                    act.activation(t[:, :, :], left[:, :, :], ACT.Exp).then_inc(exp_done, 1)

            @block.vector
            def _(dve):
                step = Chain(dve, own)
                if bias is not None:
                    dve.wait_ge(loaded, 16)
                    step(dve.tensor_tensor(r.logits[:, :, :], r.logits[:, :, :], between(gate_bias[:, :], BATCH), ALU.add))
                dve.wait_ge(token_made, 1)
                step(dve.tensor_copy(token[:, :], token_i[:, :]))
                step(dve.tensor_copy(left[:, :, :], r.logits[:, :, :]))
                experts = between(k.ramp[0:Q, 0:E], BATCH)
                for i in range(top):
                    step(dve.tensor_reduce(peak[i][:, :], left[:, :, :], AX.X, ALU.max))
                    step(dve.tensor_tensor(same[:, :, :], left[:, :, :], along(peak[i][:, :], E), ALU.is_equal))
                    step(dve.tensor_scalar(t[:, :, :], same[:, :, :], -float(E), float(E), ALU.mult, ALU.add))
                    step(dve.tensor_tensor(same[:, :, :], same[:, :, :], experts, ALU.mult))
                    step(dve.tensor_tensor(t[:, :, :], t[:, :, :], same[:, :, :], ALU.add))
                    step(dve.tensor_reduce(first[:, :], t[:, :, :], AX.X, ALU.min))
                    step(dve.scalar_tensor_tensor(first[:, :], first[:, :], float(E), first[:, :], ALU.is_lt, ALU.mult))
                    step(dve.tensor_tensor(r.hot[i][:, :, :], experts, along(first[:, :], E), ALU.is_equal))
                    if i + 1 < top:
                        step(dve.scalar_tensor_tensor(left[:, :, :], r.hot[i][:, :, :], LOWEST, left[:, :, :],
                                                      ALU.mult, ALU.add))
                if top == 2:
                    step(dve.tensor_tensor(both[:, :, :], r.hot[0][:, :, :], r.hot[1][:, :, :], ALU.add))
                else:
                    step(dve.tensor_copy(both[:, :, :], r.hot[0][:, :, :]))
                step(dve.memset(earlier[:, 0, :], 0.0))
                for i in range(BATCH):
                    step(dve.tensor_tensor(earlier[:, i + 1, :], earlier[:, i, :], both[:, i, :], ALU.add))
                dve.nop().then_inc(hot_ready, 1)
                if top == 2:
                    step(dve.tensor_tensor(b_[:, :], peak[1][:, :], peak[0][:, :], ALU.subtract))
                    dve.nop().then_inc(ask_exp, 1)
                    dve.wait_ge(exp_done, 1)
                    step(dve.tensor_scalar(c_[:, :], a[:, :], 1.0, None, ALU.add))
                    step(dve.reciprocal(r.weight[0][:, :], c_[:, :]))
                    step(dve.tensor_tensor(r.weight[1][:, :], r.weight[0][:, :], a[:, :], ALU.mult))
                else:
                    step(dve.tensor_tensor(left[:, :, :], r.logits[:, :, :], along(peak[0][:, :], E), ALU.subtract))
                    dve.nop().then_inc(ask_exp, 1)
                    dve.wait_ge(exp_done, 1)
                    step(dve.tensor_reduce(a[:, :], t[:, :, :], AX.X, ALU.add))
                    step(dve.reciprocal(r.weight[0][:, :], a[:, :]))
                dve.wait_ge(ranked, 1)
                ranks = rank[0:Q, 0:BATCH * E].rearrange("p (b e) -> p b e", e=E)
                if top == 2:
                    step(dve.tensor_copy(count[:, :], totals[0:Q, 0:E]))
                    step(dve.tensor_scalar(blocks[:, :], k.ramp[0:Q, 0:E], float(BLK), None, ALU.mult))
                    step(dve.tensor_tensor(cover[:, :, :], along(count[:, :], COUNTS0),
                                           between(blocks[:, 0:COUNTS0], E), ALU.is_gt))
                    step(dve.tensor_reduce(blocks[:, :], cover[:, :, :], AX.X, ALU.add))
                    step(dve.tensor_tensor(pairs[:, :, :], k.expert_before[0:Q, :, :], between(blocks[:, :], E), ALU.mult))
                    step(dve.tensor_reduce(start[:, :], pairs[:, :, :], AX.X, ALU.add))
                    step(dve.tensor_tensor(count[:, :], start[:, :], blocks[:, :], ALU.add))
                    step(dve.tensor_tensor(owner[:, :, :], along(k.ramp[0:Q, 0:BLOCKS0], E),
                                           between(count[:, :], BLOCKS0), ALU.is_ge))
                    step(dve.tensor_reduce(owner_of[:, :], owner[:, :, :], AX.X, ALU.add))
                    step(dve.tensor_scalar(owner_of[:, :], owner_of[:, :], float(E - 1), None, ALU.min))
                    step(dve.tensor_copy(r.block_expert[:, :], owner_of[0:1, :]))
                    step(dve.tensor_scalar(start[:, :], start[:, :], float(BLK), None, ALU.mult))
                else:
                    step(dve.tensor_scalar(start[:, :], k.ramp[0:Q, 0:E], float(BLK), None, ALU.mult))
                for i in range(top):
                    if top == 2:
                        step(dve.tensor_tensor(t[:, :, :], ranks, between(start[:, :], BATCH), ALU.add))
                        step(dve.tensor_tensor(t[:, :, :], t[:, :, :], r.hot[i][:, :, :], ALU.mult))
                        step(dve.tensor_reduce(a[:, :], t[:, :, :], AX.X, ALU.add))
                        step(dve.tensor_copy(r.slot[i][:, :], a[:, :]))
                        step(dve.tensor_copy(r.send[i][:, :], a[:, :]))
                    else:
                        step(dve.tensor_tensor(t[:, :, :], ranks, r.hot[i][:, :, :], ALU.mult))
                        step(dve.tensor_reduce(a[:, :], t[:, :, :], AX.X, ALU.add))
                        step(dve.tensor_scalar(b_[:, :], a[:, :], float(CAP1), None, ALU.is_lt))
                        step(dve.tensor_tensor(t[:, :, :], between(start[:, :], BATCH), r.hot[i][:, :, :], ALU.mult))
                        step(dve.tensor_reduce(c_[:, :], t[:, :, :], AX.X, ALU.add))
                        step(dve.tensor_tensor(a[:, :], a[:, :], c_[:, :], ALU.add))
                        step(dve.tensor_tensor(a[:, :], a[:, :], b_[:, :], ALU.mult))
                        step(dve.tensor_copy(r.slot[i][:, :], a[:, :]))
                        step(dve.tensor_scalar(token[:, :], token[:, :], float(SLOTS1), None, ALU.add))
                        step(dve.tensor_scalar(c_[:, :], b_[:, :], -1.0, 1.0, ALU.mult, ALU.add))
                        step(dve.tensor_tensor(token[:, :], token[:, :], c_[:, :], ALU.mult))
                        step(dve.tensor_tensor(a[:, :], a[:, :], token[:, :], ALU.add))
                        step(dve.tensor_copy(r.send[i][:, :], a[:, :]))
                        step(dve.tensor_tensor(r.weight[i][:, :], r.weight[i][:, :], b_[:, :], ALU.mult))
                step(dve.tensor_tensor(r.share[:, :, :], r.hot[0][:, :, :], along(r.weight[0][:, :], E), ALU.mult))
                for i in range(1, top):
                    step(dve.tensor_tensor(t[:, :, :], r.hot[i][:, :, :], along(r.weight[i][:, :], E), ALU.mult))
                    step(dve.tensor_tensor(r.share[:, :, :], r.share[:, :, :], t[:, :, :], ALU.add))


def send_rows(nc, r, h_all, slots, name, top):
    with Scope(nc, name) as s:
        sent = s.sem("sent")
        with nc.Block() as block:
            @block.gpsimd
            def _(pool):
                for b in range(BATCH):
                    for i in range(top):
                        pool.indirect_dma_start(slots, bass.IndirectOffsetOnAxis(ap=r.send[i][:, b:b + 1], axis=0),
                                                h_all[:, b, :], None).then_inc(sent, 16)
                pool.wait_ge(sent, 16 * BATCH * top)


def gather_outputs(nc, io, k, r, name, top, outputs, out_bias, out):
    with Scope(nc, name) as s:
        bias = s.sb("bias", [E, D])
        got = s.sb("got", [Q, 2, top, D])
        share_t = s.sb("share_t", [E, 2, Q])
        turned = s.ps("turned", [P, 2, D])
        biased = s.ps("biased", [P, 2, D])
        loaded, fetched = s.sem("loaded"), s.sems("fetched", 2)
        turn_done, share_ready, bias_done = s.sem("turn_done"), s.sem("share_ready"), s.sem("bias_done")
        added, own, stored = s.sem("added"), s.sem("own"), s.sem("stored")
        with nc.Block() as block:
            @block.sync
            def _(sp):
                sp.dma_start(bias[:, :], io[out_bias]).then_inc(loaded, 16)
                if out is not None:
                    for b in range(BATCH):
                        sp.wait_ge(added, 2 + b + 1)
                        sp.dma_start(out[b], k.x[:, b, :]).then_inc(stored, 16)
                    sp.wait_ge(stored, 16 * BATCH)

            @block.gpsimd
            def _(pool):
                for b in range(BATCH):
                    pool.wait_ge(added, b + 1)
                    for i in range(top):
                        pool.indirect_dma_start(got[:, b % 2, i, :], None, outputs,
                                                bass.IndirectOffsetOnAxis(ap=r.slot[i][:, b:b + 1], axis=0))\
                            .then_inc(fetched[b % 2], 16)

            @block.tensor
            def _(pe):
                pe.wait_ge(loaded, 16)
                for b in range(BATCH):
                    pe.wait_ge(share_ready, b + 1)
                    pe.transpose(turned[0:E, b % 2, 0:Q], r.share[:, b, :], k.ident[0:Q, 0:Q]).then_inc(turn_done, 1)
                    pe.wait_ge(share_ready, b + 3)
                    pe.wait_ge(added, b + 1)
                    pe.matmul(biased[0:Q, b % 2, :], share_t[:, b % 2, :], bias[:, :],
                              start=True, stop=True).then_inc(bias_done, 1)

            @block.scalar
            def _(act):
                act.sem_inc(share_ready, 2)
                for b in range(BATCH):
                    act.wait_ge(turn_done, b + 1)
                    if b >= 2:
                        act.wait_ge(bias_done, b - 1)
                    act.activation(share_t[:, b % 2, :], turned[0:E, b % 2, 0:Q], ACT.Copy).then_inc(share_ready, 1)

            @block.vector
            def _(dve):
                step = Chain(dve, own)
                dve.sem_inc(added, 2)
                for b in range(BATCH):
                    dve.wait_ge(bias_done, b + 1)
                    step(dve.tensor_tensor(k.x[:, b, :], k.x[:, b, :], biased[0:Q, b % 2, :], ALU.add))
                    dve.wait_ge(fetched[b % 2], 16 * top * (b // 2 + 1))
                    for i in range(top):
                        ins = dve.scalar_tensor_tensor(k.x[:, b, :], got[:, b % 2, i, :], r.weight[i][:, b:b + 1],
                                                       k.x[:, b, :], ALU.mult, ALU.add)
                        if i < top - 1:
                            step(ins)
                        else:
                            ins.then_inc(added, 1)
                dve.wait_ge(added, 2 + BATCH)


def second_attention(nc, io, k, wu):
    SIDES = ((0, KEYS // 2 + 1), (KEYS // 2 + 1, KEYS // 2 - 1))
    assert all(n % 2 == 0 for _, n in SIDES)
    CHUNKS = 2 * DC
    OWN = 4
    TURN_AFTER = DC
    with Scope(nc, "xattn1") as s:
        masks = s.sb("masks", [Q, BATCH, KEYS], U8)
        hide = s.sb("hide", [Q, KEYS])
        ctx_t = s.sb("ctx_t", [P, 2, DC, KEYS])
        ctx_t_h, ctx_t_l = (s.sb(n, [P, DC, KEYS], F32R) for n in ("ctx_t_h", "ctx_t_l"))
        ctx = s.sb("ctx", [P, KTILES, D])
        ctx_h, ctx_l = (s.sb(n, [P, KTILES, D], F32R) for n in ("ctx_h", "ctx_l"))
        up = [s.sb(n, [P, 2, DC, Q], F32R) for n in ("up_h", "up_l")]
        uq_h, uq_l = (s.sb(n, [P, DC, KEYS], F32R) for n in ("uq_h", "uq_l"))
        masked = s.sb("masked", [Q, KEYS])
        peak, neg_peak, total, inv_total = (s.sb(n, [Q, 1]) for n in ("peak", "neg_peak", "total", "inv_total"))
        probs = s.sb("probs", [Q, KEYS])
        probs_h, probs_l = (s.sb(n, [P, KTILES, Q], F32R) for n in ("probs_h", "probs_l"))
        hid = s.ps("hid", [P, 2, D])
        scores = s.ps("scores", [P, 2, D])
        turned = s.ps("turned", [P, 2, D])
        mixed = s.ps("mixed", [P, D])
        masks_loaded, ctx_t_loaded, ctx_loaded = s.sem("masks_loaded"), s.sems("ctx_t_loaded", 2), s.sem("ctx_loaded")
        ctx_t_h_ready, ctx_t_l_ready = s.sem("ctx_t_h_ready"), s.sem("ctx_t_l_ready")
        ctx_h_ready, ctx_l_ready = s.sem("ctx_h_ready"), s.sem("ctx_l_ready")
        uq_done, uq_h_ready, uq_l_ready = s.sem("uq_done"), s.sem("uq_h_ready"), s.sem("uq_l_ready")
        up_loaded = s.sems("up_loaded", 2)
        scores_done, own, exp_done = s.sem("scores_done"), s.sem("own"), s.sem("exp_done")
        turn_done, probs_h_ready, probs_l_ready = s.sem("turn_done"), s.sem("probs_h_ready"), s.sem("probs_l_ready")
        peak_done = s.sem("peak_done")
        mixed_done, x_added, prepared = s.sem("mixed_done"), s.sem("x_added"), s.sem("prepared")

        def steps(step, eng):
            step(-1, 1, False, True, True)
            with eng.Fori(0, BATCH // 2 - 1) as i:
                for half in range(2):
                    step(2 * i + half, half, True, True, True)
            step(BATCH - 2, 0, True, True, False)
            step(BATCH - 1, 1, True, False, False)

        def up_count(b, half):
            return 16 * (b + (2 if half == 0 else 3))

        def chunk(c):
            side, m = divmod(c, DC)
            return side, m, slice(SIDES[side][0], sum(SIDES[side]))

        with nc.Block() as block:
            @block.sync
            def _(sp):
                def load_t(b, half):
                    wait(sp, ctx_t_l_ready, 2 * b - 2)
                    sp.dma_start(ctx_t[:, half, :, :], io["ctx_t"][bass.ds(b, 1)].rearrange("a p c n -> p (a c) n"))\
                      .then_inc(ctx_t_loaded[half], 16)

                def load(b):
                    wait(sp, ctx_l_ready, b)
                    rows = io["ctx"][bass.ds(b, 1)].rearrange("a n d -> (a n) d")
                    sp.dma_start(ctx[:, 0:KTILES - 1, :],
                                 rows[0:KEYS - KLAST, :].rearrange("(t p) d -> p t d", p=P)).then_inc(ctx_loaded, 16)
                    sp.dma_start(ctx[0:KLAST, KTILES - 1, :], rows[KEYS - KLAST:KEYS, :]).then_inc(ctx_loaded, 16)

                def load_up(b, half):
                    for part in range(2):
                        sp.dma_start(up[part][:, half, :, :].bitcast(F32), io["up_parts"][part, :, :, bass.ds(b * Q, Q)])\
                          .then_inc(up_loaded[half], 16)

                load_t(0, 0)
                load_t(1, 1)
                load_up(0, 0)
                load_up(1, 1)
                sp.dma_start(masks[:, :, :].rearrange("p b n -> p (b n)"), io["mask"].partition_broadcast(Q))\
                  .then_inc(masks_loaded, 16)
                sp.wait_ge(prepared, 2)
                load(0)
                with sp.Fori(0, BATCH // 2 - 1) as i:
                    for half in range(2):
                        b = 2 * i + half
                        load_t(b + 2, half)
                        sp.wait_ge(scores_done, b + 1)
                        load_up(b + 2, half)
                        load(b + 1)
                load(BATCH - 1)

            @block.tensor
            def _(pe):
                def step(b, half, now, next_, after):
                    for c in range(CHUNKS if next_ else 0):
                        side, m, keys = chunk(c)
                        if m == 0:
                            pe.wait_ge(ctx_t_l_ready, 2 * b + (2 + side + 1))
                        pe.wait_ge(uq_l_ready, CHUNKS * b + (CHUNKS + c + 1))
                        for d in range(DC):
                            mm = times(pe, hid[:, c % 2, 0:SIDES[side][1]], [w[:, d, m * P:(m + 1) * P] for w in wu],
                                       (ctx_t_h[:, d, keys], ctx_t_l[:, d, keys]), d == 0, d == DC - 1)
                        mm.then_inc(uq_done, 1)
                        if c == TURN_AFTER and now:
                            turn(b)
                    if now:
                        if not next_:
                            turn(b)
                        pe.wait_ge(probs_l_ready, b + 1)
                        pe.wait_ge(ctx_l_ready, b + 1)
                        wait(pe, x_added, b)
                        for t in range(KTILES):
                            n = P if t < KTILES - 1 else KLAST
                            mm = times(pe, mixed[0:Q, :], (probs_h[0:n, t, :], probs_l[0:n, t, :]),
                                       (ctx_h[0:n, t, :], ctx_l[0:n, t, :]), t == 0, t == KTILES - 1)
                        mm.then_inc(mixed_done, 1)
                    if next_:
                        pe.wait_ge(uq_l_ready, CHUNKS * b + (2 * CHUNKS + 2))
                        pe.wait_ge(up_loaded[1 - half], up_count(b, half))
                        wait(pe, own, OWN * b + 2)
                        for side, (at, n) in enumerate(SIDES):
                            for d in range(DC):
                                mm = times(pe, scores[0:Q, side, 0:n], [part[:, 1 - half, d, :] for part in up],
                                           (uq_h[:, d, at:at + n], uq_l[:, d, at:at + n]), d == 0, d == DC - 1)
                        mm.then_inc(scores_done, 1)

                def turn(b):
                    pe.wait_ge(exp_done, b + 1)
                    wait(pe, probs_l_ready, b)
                    for t in range(KTILES):
                        n = P if t < KTILES - 1 else KLAST
                        mm = pe.transpose(turned[0:n, t // 3, t % 3 * Q:(t % 3 + 1) * Q],
                                          probs[:, t * P:t * P + n], k.ident[0:Q, 0:Q])
                    mm.then_inc(turn_done, 1)

                pe.wait_ge(prepared, 2)
                steps(step, pe)

            @block.gpsimd
            def _(pool):
                def step(b, half, now, next_, after):
                    if not next_:
                        return
                    pool.wait_ge(ctx_h_ready, b + 2)
                    low(pool, ctx_l[:, :, :], ctx[:, :, :], ctx_h[:, :, :]).then_inc(ctx_l_ready, 1)

                steps(step, pool)

            def raw_count(b, half):
                return 8 * (b - half) + 16

            def split_side(b, side, eng, make, loaded, ready):
                keys = slice(SIDES[side][0], sum(SIDES[side]))
                eng.wait_ge(*loaded)
                wait(eng, uq_done, CHUNKS * b + ((side + 1) * DC - CHUNKS))
                make(keys).then_inc(ready, 1)

            @block.scalar
            def _(act):
                def upper_side(b, half, side):
                    split_side(b, side, act, lambda keys: high(act, ctx_t_h[:, :, keys], ctx_t[:, half, :, keys]),
                               (ctx_t_loaded[half], raw_count(b, half)), ctx_t_h_ready)

                def step(b, half, now, next_, after):
                    for c in range(CHUNKS if next_ else 0):
                        side, m, keys = chunk(c)
                        act.wait_ge(uq_done, CHUNKS * b + (CHUNKS + c + 1))
                        high(act, uq_h[:, m, keys], hid[:, c % 2, 0:SIDES[side][1]], ACT.Relu).then_inc(uq_h_ready, 1)
                        if c == 0 and now:
                            exponentials(b)
                        if c == TURN_AFTER and now:
                            upper_probs(b)
                        if c % DC == DC - 1 and after:
                            upper_side(b + 2, half, side)
                    if now and not next_:
                        exponentials(b)
                        upper_probs(b)
                    if next_:
                        wait(act, mixed_done, b + 1)
                        act.wait_ge(ctx_loaded, 32 * b + 64)
                        high(act, ctx_h[:, :, :], ctx[:, :, :]).then_inc(ctx_h_ready, 1)

                def exponentials(b):
                    act.wait_ge(own, OWN * b + 3)
                    act.activation(probs[:, :], masked[:, :], ACT.Exp, bias=neg_peak[:, :],
                                   accum_out=total[:, :]).then_inc(exp_done, 1)

                def upper_probs(b):
                    act.wait_ge(turn_done, b + 1)
                    high(act, probs_h[:, :, :].rearrange("p (s t) q -> p s (t q)", s=2), turned[:, :, 0:3 * Q])\
                        .then_inc(probs_h_ready, 1)

                for side in range(2):
                    upper_side(0, 0, side)
                act.wait_ge(prepared, 2)
                steps(step, act)

            @block.vector
            def _(dve):
                def lower_side(b, half, side):
                    split_side(b, side, dve, lambda keys: low(dve, ctx_t_l[:, :, keys], ctx_t[:, half, :, keys], ctx_t_h[:, :, keys]),
                               (ctx_t_h_ready, 2 * b + (side + 1)), ctx_t_l_ready)

                def lower_probs(b):
                    dve.wait_ge(probs_h_ready, b + 1)
                    low(dve, probs_l[:, :, :].rearrange("p (s t) q -> p s (t q)", s=2), turned[:, :, 0:3 * Q],
                        probs_h[:, :, :].rearrange("p (s t) q -> p s (t q)", s=2)).then_inc(probs_l_ready, 1)
                    dve.reciprocal(inv_total[:, :], total[:, :]).then_inc(own, 1)

                def step(b, half, now, next_, after):
                    for c in range(CHUNKS if next_ else 0):
                        side, m, keys = chunk(c)
                        dve.wait_ge(uq_h_ready, CHUNKS * b + (CHUNKS + c + 1))
                        dve.scalar_tensor_tensor(uq_l[:, m, keys], hid[:, c % 2, 0:SIDES[side][1]], 0.0,
                                                 uq_h[:, m, keys].bitcast(F32), ALU.max, ALU.subtract)\
                           .then_inc(uq_l_ready, 1)
                        if c == TURN_AFTER and now:
                            lower_probs(b)
                        if c % DC == DC - 1 and after:
                            lower_side(b + 2, half, side)
                    if now:
                        if not next_:
                            lower_probs(b)
                        dve.wait_ge(own, OWN * b + OWN)
                        dve.wait_ge(mixed_done, b + 1)
                        dve.scalar_tensor_tensor(row(k.x, b), mixed[0:Q, :], inv_total[:, :], row(k.x, b),
                                                 ALU.mult, ALU.add).then_inc(x_added, 1)
                    if next_:
                        dve.tensor_scalar(hide[:, :], row(masks, b + 1), LOWEST, None, ALU.mult).then_inc(own, 1)
                        dve.wait_ge(own, OWN * b + (OWN + 1))
                        dve.wait_ge(scores_done, b + 2)
                        wait(dve, exp_done, b + 1)
                        for side, (at, n) in enumerate(SIDES):
                            ins = dve.tensor_tensor(masked[:, at:at + n], scores[0:Q, side, 0:n], hide[:, at:at + n], ALU.add)
                        ins.then_inc(own, 1)
                        dve.wait_ge(own, OWN * b + (OWN + 2))
                        dve.tensor_reduce(peak[:, :], masked[:, :], AX.X, ALU.max).then_inc(peak_done, 1)
                        dve.wait_ge(peak_done, b + 2)
                        dve.tensor_scalar(neg_peak[:, :], peak[:, :], FLOOR, -1.0, ALU.max, ALU.mult).then_inc(own, 1)

                dve.sem_inc(uq_l_ready, 2)
                dve.memset(turned[:, :, :], 0.0).then_inc(prepared, 1)
                dve.memset(ctx[:, KTILES - 1, :], 0.0).then_inc(prepared, 1)
                dve.wait_ge(prepared, 2)
                dve.wait_ge(masks_loaded, 16)
                for side in range(2):
                    lower_side(0, 0, side)
                steps(step, dve)
                dve.wait_ge(x_added, BATCH)


def experts(nc, io, ident, name, blocks, gated, block_expert):
    PAIRS = NW if gated else F1 // P // 2
    TILES = PAIRS if gated else 2 * PAIRS
    OUTS = TILES // 2
    CH = PAIRS + OUTS
    RING = CH if CH <= 8 else 8
    assert CH % RING == 0
    LAPS = CH // RING
    POOLS = (1, 3, 5) if gated else (0, 3, 6)
    W = 2 * D
    with Scope(nc, name) as s:
        raw = s.sb("raw", [P, RING, W])
        upper = s.sb("upper", [P, RING, W], F32R)
        lower = s.sb("lower", [P, RING, W], F32R)
        b1 = s.sb("b1", [P, blocks, 2 * PAIRS])
        rows = s.sb("rows", [P, 2, D])
        rows_h, rows_l = (s.sb(n, [P, DC, BLK], F32R) for n in ("rows_h", "rows_l"))
        act_h, act_l = (s.sb(n, [P, TILES, BLK], F32R) for n in ("act_h", "act_l"))
        act_f = s.sb("act_f", [P, 2, 2 * BLK])
        y = s.sb("y", [P, 2, D])
        if gated:
            glu, lin, sig = (s.sb(n, [P, 2, BLK]) for n in ("glu", "lin", "sig"))
        hidden = s.ps("hidden", [P, 4, 2, BLK])
        turned = s.ps("turned", [P, DC, BLK])
        out = s.ps("out", [P, 2, D])
        rows_loaded, raw_loaded = s.sem("rows_loaded"), s.sems("raw_loaded", RING)
        upper_ready, lower_ready = s.sems("upper_ready", RING), s.sems("lower_ready", RING)
        chunk_done, turn_done = s.sem("chunk_done"), s.sem("turn_done")
        rows_h_ready, rows_l_ready = s.sem("rows_h_ready"), s.sem("rows_l_ready")
        hidden_free, act_made, act_h_ready, act_ready = (
            s.sem("hidden_free"), s.sem("act_made"), s.sem("act_h_ready"), s.sem("act_ready"))
        y_ready, stored, glu_ready, sig_ready, own = (
            s.sem("y_ready"), s.sem("stored"), s.sem("glu_ready"), s.sem("sig_ready"), s.sem("own"))
        slots, results, weights, biases = (io[n + name[-1]] for n in ("slots", "results", "chunks", "b1_"))

        def used(j, c):
            return j * LAPS + (c // RING + 1)

        def ahead(j, c):
            return (j, c + RING) if c + RING < CH else (j + 1, c + RING - CH)

        def each_ahead(j, last, do):
            for c in range(CH):
                nj, nc_ = ahead(j, c)
                if not (last and nj is not j):
                    do(nj, nc_)

        with nc.Block() as block:
            @block.sync
            def _(sp):
                def load(j):
                    sp.wait_ge(turn_done, j + 1)
                    sp.dma_start(rows[:, :, :], slots[bass.ds(j * BLK, BLK), :].rearrange("(t p) d -> p t d", p=P))\
                      .then_inc(rows_loaded, 16)
                    e = j
                    if gated:
                        e = sp.value_load(block_expert[0:1, bass.ds(j, 1)], min_val=0, max_val=E - 1)
                    sp.dma_start(b1[:, bass.ds(j, 1), :].rearrange("p a f -> p (a f)"),
                                 biases[bass.ds(e, 1)].rearrange("a p f -> p (a f)")).then_inc(rows_loaded, 16)
                    for c in range(CH):
                        sp.wait_ge(lower_ready[c % RING], used(j, c))
                        sp.dma_start(raw[:, c % RING, :], weights[bass.ds(e, 1), c].rearrange("a p w -> p (a w)"))\
                          .then_inc(raw_loaded[c % RING], 16)

                with sp.Fori(0, blocks) as j:
                    load(j)

            @block.tensor
            def _(pe):
                def turn(j):
                    pe.wait_ge(rows_loaded, 32 * j + 32)
                    pe.wait_ge(rows_l_ready, j + 1)
                    for t in range(2):
                        for d in range(DC):
                            mm = pe.transpose(turned[:, d, t * P:(t + 1) * P], rows[:, t, d * P:(d + 1) * P],
                                              ident[:, :])
                    mm.then_inc(turn_done, 1)

                def block_of(j, last):
                    pe.wait_ge(rows_l_ready, j + 2)
                    for c in range(PAIRS):
                        w_h, w_l = (w[:, c % RING, :].rearrange("p (s d f) -> p s d f", s=2, d=DC) for w in (upper, lower))
                        pe.wait_ge(lower_ready[c % RING], used(j, c) + 1)
                        pe.wait_ge(hidden_free, j * PAIRS + (c + 1))
                        for side in range(2):
                            for d in range(DC):
                                mm = times(pe, hidden[:, c % 4, side, :], (w_h[:, side, d, :], w_l[:, side, d, :]),
                                           (rows_h[:, d, :], rows_l[:, d, :]), d == 0, d == DC - 1)
                        mm.then_inc(chunk_done, 1)
                    if not last:
                        turn(j + 1)
                    pe.wait_ge(y_ready, 2 * j + 2)
                    for o in range(OUTS):
                        c = PAIRS + o
                        w_h, w_l = (w[:, c % RING, :].rearrange("p (s d) -> p s d", s=2) for w in (upper, lower))
                        pe.wait_ge(lower_ready[c % RING], used(j, c) + 1)
                        pe.wait_ge(act_ready, j * PAIRS + (2 * o + 2 if gated else o + 3))
                        for t in range(2):
                            for side in range(2):
                                f, cols = 2 * o + side, slice(t * P, (t + 1) * P)
                                mm = times(pe, out[:, t, :], (act_h[:, f, cols], act_l[:, f, cols]),
                                           (w_h[:, side, :], w_l[:, side, :]), f == 0, f == TILES - 1)
                        mm.then_inc(chunk_done, 1)

                pe.sem_inc(chunk_done, RING)
                pe.sem_inc(turn_done, 1)
                turn(0)
                with pe.Fori(0, blocks - 1) as j:
                    block_of(j, False)
                block_of(blocks - 1, True)

            def make_lower(eng, j, c):
                eng.wait_ge(upper_ready[c % RING], used(j, c))
                low(eng, lower[:, c % RING, :], raw[:, c % RING, :], upper[:, c % RING, :])\
                    .then_inc(lower_ready[c % RING], 1)

            @block.gpsimd
            def _(pool):
                def mine(j, c):
                    if c % RING in POOLS:
                        make_lower(pool, j, c)

                for c in POOLS:
                    pool.sem_inc(lower_ready[c], 1)
                for c in range(RING):
                    mine(0, c)
                with pool.Fori(0, blocks - 1) as j:
                    each_ahead(j, False, mine)
                each_ahead(blocks - 1, True, mine)

            @block.scalar
            def _(act):
                def make_upper(j, c):
                    act.wait_ge(raw_loaded[c % RING], 16 * used(j, c))
                    act.wait_ge(chunk_done, j * CH + (c + 1))
                    high(act, upper[:, c % RING, :], raw[:, c % RING, :]).then_inc(upper_ready[c % RING], 1)

                def copy_turned(j):
                    act.wait_ge(turn_done, j + 2)
                    high(act, rows_h[:, :, :], turned[:, :, :]).then_inc(rows_h_ready, 1)

                def block_of(j, last):
                    for c in range(CH):
                        if c < PAIRS and gated:
                            act.wait_ge(glu_ready, j * PAIRS + (c + 1))
                            act.activation(sig[:, c % 2, :], glu[:, c % 2, :], ACT.Sigmoid, scale=ALPHA).then_inc(sig_ready, 1)
                        elif c < PAIRS:
                            act.wait_ge(chunk_done, j * CH + (c + 1 + RING))
                            act.wait_ge(act_ready, j * PAIRS + (c + 1))
                            for side in range(2):
                                f = 2 * c + side
                                act.activation(act_f[:, c % 2, side * BLK:(side + 1) * BLK], hidden[:, c % 4, side, :],
                                               ACT.Gelu, bias=b1[:, bass.ds(j, 1), f]).then_inc(act_made, 1)
                        nj, nc_ = ahead(j, c)
                        if not (last and nj is not j):
                            make_upper(nj, nc_)
                        if c < PAIRS and gated:
                            act.wait_ge(act_made, j * PAIRS + (c + 1))
                            high(act, act_h[:, c, :], act_f[:, c % 2, 0:BLK]).then_inc(act_h_ready, 1)
                        if c == PAIRS - 1 and not last:
                            copy_turned(j + 1)
                    act.wait_ge(stored, 16 * j + 16)
                    act.wait_ge(chunk_done, j * CH + (CH + RING))
                    for t in range(2):
                        act.activation(y[:, t, :], out[:, t, :], ACT.Copy).then_inc(y_ready, 1)
                    act.wait_ge(y_ready, 2 * j + 4)
                    act.dma_start(results[bass.ds(j * BLK, BLK), :].rearrange("(t p) d -> p t d", p=P), y[:, :, :])\
                       .then_inc(stored, 16)

                act.sem_inc(y_ready, 2)
                act.sem_inc(stored, 16)
                for c in range(RING):
                    make_upper(0, c)
                copy_turned(0)
                with act.Fori(0, blocks - 1) as j:
                    block_of(j, False)
                block_of(blocks - 1, True)
                act.wait_ge(stored, 16 * blocks + 16)

            @block.vector
            def _(dve):
                def mine(j, c):
                    if c % RING not in POOLS:
                        make_lower(dve, j, c)

                def split_turned(j):
                    dve.wait_ge(rows_h_ready, j + 1)
                    low(dve, rows_l[:, :, :], turned[:, :, :], rows_h[:, :, :]).then_inc(rows_l_ready, 1)

                def lower_act(j, c):
                    if gated:
                        whole, upper_part, part = act_f[:, c % 2, 0:BLK], act_h[:, c, :], act_l[:, c, :]
                    else:
                        whole = act_f[:, c % 2, :]
                        upper_part, part = (a[:, 2 * c:2 * c + 2, :].rearrange("p s n -> p (s n)") for a in (act_h, act_l))
                    dve.wait_ge(act_h_ready, j * PAIRS + (c + 1))
                    low(dve, part, whole, upper_part).then_inc(act_ready, 1)

                def block_of(j, last):
                    for c in range(CH):
                        one = c % 2
                        if c < PAIRS and gated:
                            dve.wait_ge(chunk_done, j * CH + (c + 1 + RING))
                            dve.tensor_scalar(glu[:, one, :], hidden[:, c % 4, 0, :], b1[:, bass.ds(j, 1), c], LIMIT,
                                              ALU.add, ALU.min).then_inc(glu_ready, 1)
                            dve.tensor_scalar(lin[:, one, :], hidden[:, c % 4, 1, :], b1[:, bass.ds(j, 1), PAIRS + c],
                                              LIMIT, ALU.add, ALU.min).then_inc(hidden_free, 1)
                            dve.wait_ge(hidden_free, j * PAIRS + (c + 5))
                            dve.tensor_scalar(lin[:, one, :], lin[:, one, :], -LIMIT, 1.0, ALU.max, ALU.add).then_inc(own, 1)
                            if c > 0:
                                lower_act(j, c - 1)
                            dve.wait_ge(sig_ready, j * PAIRS + (c + 1))
                            dve.tensor_tensor(glu[:, one, :], glu[:, one, :], sig[:, one, :], ALU.mult).then_inc(own, 1)
                            dve.wait_ge(own, 2 * PAIRS * j + (2 * c + 2))
                            dve.tensor_tensor(act_f[:, one, 0:BLK], glu[:, one, :], lin[:, one, :], ALU.mult)\
                               .then_inc(act_made, 1)
                        elif c < PAIRS:
                            dve.wait_ge(act_made, j * TILES + (2 * c + 2))
                            dve.sem_inc(hidden_free, 1)
                            dve.tensor_copy(act_h[:, 2 * c:2 * c + 2, :].rearrange("p s n -> p (s n)"), act_f[:, one, :])\
                               .then_inc(act_h_ready, 1)
                            lower_act(j, c)
                        nj, nc_ = ahead(j, c)
                        if not (last and nj is not j):
                            mine(nj, nc_)
                        if c == PAIRS - 1:
                            if gated:
                                lower_act(j, c)
                            if not last:
                                split_turned(j + 1)

                for c in range(RING):
                    if c not in POOLS:
                        dve.sem_inc(lower_ready[c], 1)
                dve.sem_inc(rows_l_ready, 1)
                dve.sem_inc(hidden_free, 4)
                if not gated:
                    dve.sem_inc(act_ready, 2)
                for c in range(RING):
                    mine(0, c)
                split_turned(0)
                with dve.Fori(0, blocks - 1) as j:
                    block_of(j, False)
                block_of(blocks - 1, True)


class Keep:
    pass


def build(nc, io):
    with ExitStack() as whole:
        def sb(name, shape, dt=F32):
            return whole.enter_context(nc.sbuf_tensor(name, shape, dt))

        k = Keep()
        k.ident = sb("ident", [P, P])
        k.ones = sb("ones", [P, P])
        k.before = sb("before", [P, P])
        k.ramp_i = sb("ramp_i", [P, P], I32)
        k.ramp = sb("ramp", [P, P])
        k.expert_before = sb("expert_before", [P, E, E])
        k.scale_row = sb("scale_row", [P, DC])
        load_constants(nc, io, k)

        with Scope(nc, "before0") as s:
            k.x = s.sb("x", [Q, BATCH, D])
            wq = [s.sb(f"wq{i}", [P, DC, D], F32R) for i in range(2)]
            norm_and_project(nc, io, k, "queries", "wq", wq, io["q_parts"],
                             lambda dve, out, acc, m: dve.tensor_scalar(out, acc, SCALE, None, ALU.mult), io["x"])
        first_attention(nc, io, k)
        k.x = sb("x", [Q, BATCH, D])
        with Scope(nc, "ffn0") as s:
            r = Routing(s, TOP0)
            with Scope(nc, "ffn0h") as sh:
                h_all = sh.sb("h_all", [Q, BATCH, D])
                norm_and_route(nc, io, k, "route_norm0", h_all, r.logits, "gate0", True, io["x1"])
                route(nc, io, k, r, "route0", TOP0, "gate_b")
                send_rows(nc, r, h_all, io["slots0"], "send0", TOP0)
            experts(nc, io, k.ident, "experts0", BLOCKS0, True, r.block_expert)
            gather_outputs(nc, io, k, r, "gather0", TOP0, io["results0"], "b2_0", None)
        with Scope(nc, "attention1") as s:
            wu = [s.sb(f"wu{i}", [P, DC, D], F32R) for i in range(2)]
            norm_and_project(nc, io, k, "up", "u", wu, io["up_parts"],
                             lambda dve, out, acc, m: dve.tensor_scalar(out, acc, 0.0, k.scale_row[:, m:m + 1],
                                                                        ALU.max, ALU.mult))
            second_attention(nc, io, k, wu)
        with Scope(nc, "ffn1") as s:
            r = Routing(s, 1)
            with Scope(nc, "ffn1h") as sh:
                h_all = sh.sb("h_all", [Q, BATCH, D])
                norm_and_route(nc, io, k, "route_norm1", h_all, r.logits, "gate1", False)
                route(nc, io, k, r, "route1", 1, None)
                send_rows(nc, r, h_all, io["slots1"], "send1", 1)
            experts(nc, io, k.ident, "experts1", E, False, None)
            gather_outputs(nc, io, k, r, "gather1", 1, io["results1"], "b2_1", io["out"])


def lay_out(a):
    def turn(w):
        return w.T.reshape(-1, P, w.shape[0]).transpose(1, 0, 2)

    def chunks(w1, w2):
        return np.concatenate([w1.reshape(E, -1, P, 2 * D), w2.reshape(E, -1, P, 2 * D)], axis=1)

    w1 = a["L0_ffn_mlp1_w"]
    return {
        "x": a["x"].transpose(1, 0, 2),
        "ctx": a["ctx_1024"],
        "ctx_t": a["ctx_1024"].transpose(0, 2, 1).reshape(BATCH, DC, P, KEYS).transpose(0, 2, 1, 3),
        "mask": a["mask_BxS2_bk1"].reshape(BATCH * KEYS),
        "wq": turn(a["L0_xattn_wq"]), "wk": turn(a["L0_xattn_wk"]), "wv": turn(a["L0_xattn_wv"]),
        "wo": turn(a["L0_xattn_wo"]), "bo": a["L0_xattn_bo"],
        "norm_w": a["L0_ffn_norm_w"], "gate0": turn(a["L0_ffn_gate_w"]), "gate_b": a["L0_ffn_gate_b"],
        "chunks0": chunks(w1.reshape(E, NW, P, 2, DC, P).transpose(0, 1, 5, 3, 4, 2),
                          a["L0_ffn_mlp2_w"].reshape(E, D, NW // 2, 2, P).transpose(0, 2, 4, 3, 1)),
        "b1_0": a["L0_ffn_mlp1_b"].reshape(E, NW, P, 2).transpose(0, 2, 3, 1).reshape(E, P, 2 * NW),
        "b2_0": a["L0_ffn_mlp2_b"],
        "u": turn(a["L1_xattn_U_w"]), "d_param": a["L1_xattn_D_param"].reshape(DC, P).T,
        "gate1": a["L1_ffn_wg"].reshape(DC, P, E).transpose(1, 0, 2),
        "chunks1": chunks(a["L1_ffn_W1"].reshape(E, DC, P, F1 // P // 2, 2, P).transpose(0, 3, 2, 4, 1, 5),
                          a["L1_ffn_W2"].reshape(E, F1 // P // 2, 2, P, D).transpose(0, 1, 3, 2, 4)),
        "b1_1": a["L1_ffn_b1"].reshape(E, F1 // P, P).transpose(0, 2, 1),
        "b2_1": a["L1_ffn_b2"],
    }


def scratch(nc):
    shapes = {"x1": [Q, BATCH, D], "q_parts": [2, P, DC, TOKENS], "up_parts": [2, P, DC, TOKENS],
              "slots0": [SLOTS0, D], "results0": [SLOTS0, D], "slots1": [SLOTS1 + TOKENS, D], "results1": [SLOTS1, D]}
    return {n: nc.dram_tensor(n, shape, F32, kind="Internal").ap() for n, shape in shapes.items()}


def kernel(**inputs):
    import concourse.bacc as bacc
    from concourse.bass_utils import run_bass_kernel_spmd as run

    arrays = {f"in_{n}": np.ascontiguousarray(v) for n, v in lay_out({n: np.asarray(v) for n, v in inputs.items()}).items()}
    nc = bacc.Bacc("TRN2", target_bir_lowering=False, num_devices=1)
    io = {n[3:]: nc.dram_tensor(n, v.shape, mybir.dt.from_np(v.dtype), kind="ExternalInput").ap() for n, v in arrays.items()}
    io.update(scratch(nc))
    io["out"] = nc.dram_tensor("out", [BATCH, Q, D], F32, kind="ExternalOutput").ap()
    build(nc, io)
    got = run(nc, [arrays], core_ids=[0])
    return got.results[0]["out"]
```

```python
from contextlib import ExitStack

import numpy as np

import concourse.bass as bass
from concourse import mybir

F32 = mybir.dt.float32
F32R = mybir.dt.float32r
I32 = mybir.dt.int32
U8 = mybir.dt.uint8
ALU = mybir.AluOpType
ACT = mybir.ActivationFunctionType
AX = mybir.AxisListType

P = 128
BATCH, Q, D = 16, 100, 512
KEYS = 722
KH = KEYS // 2
KTILES = -(-KEYS // P)
KLAST = KEYS - (KTILES - 1) * P
DC = D // P
HEADS, HD = 16, 32
HPC = P // HD
TOKENS = BATCH * Q
GROUPS = 4
GT = TOKENS // GROUPS
BPG = BATCH // GROUPS
E = 8
INNER0 = 512
F1 = 2048
BLK = 256
TOP0 = 2
BLOCKS0 = E + (TOP0 * TOKENS - E) // BLK
SLOTS0 = BLOCKS0 * BLK
COUNTS0 = -(-TOKENS // BLK)
CAP1 = int(TOKENS / E * 1.25) + 1
SLOTS1 = E * BLK
LN_EPS = 1e-5
RMS_EPS = float(np.finfo(np.float32).eps)
SCALE = HD ** -0.5
LIMIT, ALPHA = 7.0, 1.702
LOWEST = -3.0e38
FLOOR = -1.0e38
NW = -(-INNER0 // P)


class Chain:

    def __init__(self, eng, sem):
        self.eng, self.sem, self.value = eng, sem, 0

    def __call__(self, ins):
        self.value += 1
        ins.then_inc(self.sem, 1)
        self.eng.wait_ge(self.sem, self.value)


class Scope(ExitStack):

    def __init__(self, nc, name):
        super().__init__()
        self.nc, self.stage, self.signals = nc, name, []
        self.callback(self.clear)

    def clear(self):
        if self.signals:
            self.nc.clear_and_free_semaphores(self.signals)
            self.nc.all_engine_barrier(sem_only=True)

    def sb(self, name, shape, dt=F32):
        return self.enter_context(self.nc.sbuf_tensor(f"{self.stage}_{name}", shape, dt))

    def ps(self, name, shape, dt=F32):
        return self.enter_context(self.nc.psum_tensor(f"{self.stage}_{name}", shape, dt))

    def sem(self, name):
        self.signals.append(self.nc.alloc_semaphore(f"{self.stage}_{name}"))
        return self.signals[-1]

    def sems(self, name, n):
        return [self.sem(f"{name}{i}") for i in range(n)]


def load_constants(nc, io, k):
    with Scope(nc, "const") as s:
        loaded = s.sem("loaded")
        ramp_made = s.sem("ramp_made")
        pool_made = s.sem("pool_made")
        with nc.Block() as block:
            @block.sync
            def _(sp):
                sp.dma_start(k.scale_row[:, :], io["d_param"]).then_inc(loaded, 16)
                sp.wait_ge(loaded, 16)

            @block.gpsimd
            def _(pool):
                step = Chain(pool, pool_made)
                step(pool.memset(k.ident[:, :], 1.0))
                step(pool.affine_select(out=k.ident[:, :], in_=k.ident[:, :], compare_op=ALU.is_equal, fill=0.0,
                                        base=0, pattern=[[-1, P]], channel_multiplier=1))
                step(pool.memset(k.ones[:, :], 1.0))
                step(pool.affine_select(out=k.before[:, :], in_=k.ones[:, :], compare_op=ALU.is_gt, fill=0.0,
                                        base=0, pattern=[[1, P]], channel_multiplier=-1))
                step(pool.iota(k.ramp_i[:, :], [[1, P]], base=0, channel_multiplier=0))
                step(pool.affine_select(out=k.expert_before[:, :, :],
                                        in_=k.ones[:, 0:E * E].rearrange("p (e f) -> p e f", e=E),
                                        compare_op=ALU.is_gt, fill=0.0, base=0,
                                        pattern=[[1, E], [-1, E]], channel_multiplier=0))

            @block.vector
            def _(dve):
                dve.wait_ge(pool_made, 6)
                dve.tensor_copy(k.ramp[:, :], k.ramp_i[:, :]).then_inc(ramp_made, 1)
                dve.wait_ge(ramp_made, 1)


def row_stats(dve, k, b, x_row):
    return dve.bn_stats(k.stats[:, bass.ds(b, 1), :].rearrange("p a s -> p (a s)"), x_row)


def mean_and_variance(dve, step, k, tmp):
    even_mean, even_m2 = k.stats[:, :, 1], k.stats[:, :, 2]
    odd_mean, odd_m2 = k.stats[:, :, 4], k.stats[:, :, 5]
    step(dve.tensor_tensor(tmp.mean[:, :], even_mean, odd_mean, ALU.add))
    step(dve.tensor_scalar(tmp.mean[:, :], tmp.mean[:, :], 0.5, None, ALU.mult))
    step(dve.tensor_tensor(tmp.a[:, :], even_mean, odd_mean, ALU.subtract))
    step(dve.tensor_tensor(tmp.a[:, :], tmp.a[:, :], tmp.a[:, :], ALU.mult))
    step(dve.tensor_tensor(tmp.var[:, :], even_m2, odd_m2, ALU.add))
    step(dve.tensor_scalar(tmp.var[:, :], tmp.var[:, :], 1.0 / D, None, ALU.mult))
    step(dve.scalar_tensor_tensor(tmp.var[:, :], tmp.a[:, :], 0.25, tmp.var[:, :], ALU.mult, ALU.add))


def inverse_root(dve, step, act_ready, act_done, act_count, root, value, inv, tmp):
    dve.nop().then_inc(act_ready, 1)
    dve.wait_ge(act_done, act_count)
    step(dve.reciprocal(inv[:, :], root[:, :]))
    step(dve.tensor_tensor(tmp[:, :], inv[:, :], inv[:, :], ALU.mult))
    step(dve.tensor_tensor(tmp[:, :], tmp[:, :], value[:, :], ALU.mult))
    step(dve.tensor_scalar(tmp[:, :], tmp[:, :], -0.5, 1.5, ALU.mult, ALU.add))
    step(dve.tensor_tensor(inv[:, :], inv[:, :], tmp[:, :], ALU.mult))


class NormBuffers:
    def __init__(self, s):
        self.mean = s.sb("mean", [Q, BATCH])
        self.var = s.sb("var", [Q, BATCH])
        self.a = s.sb("a", [Q, BATCH])
        self.root = s.sb("root", [Q, BATCH])
        self.inv = s.sb("inv", [Q, BATCH])
        self.value = s.sb("value", [Q, BATCH])
        self.inv2 = s.sb("inv2", [Q, BATCH])
        self.mul2 = s.sb("mul2", [Q, BATCH])


def times(pe, out, left, right, first, last):
    (lh, ll), (rh, rl) = left, right
    pe.matmul(out, lh, rh, start=first, stop=False)
    pe.matmul(out, lh, rl, start=False, stop=False)
    return pe.matmul(out, ll, rh, start=False, stop=last)


def high(act, dst, src, func=ACT.Copy):
    return act.activation(dst, src, func)


def low(eng, dst, src, upper):
    return eng.tensor_tensor(dst, src, upper.bitcast(F32), ALU.subtract)


def wait(eng, sem, value):
    if not (isinstance(value, int) and value <= 0):
        eng.wait_ge(sem, value)


def norm_and_project(nc, io, k, name, weight, w_parts, out, steps, source=None, cleared=()):
    with Scope(nc, name) as s:
        n = NormBuffers(s)
        w = s.sb("w", [P, DC, D])
        rows = s.sb("rows", [Q, 2, D])
        rows_h, rows_l = (s.sb(name_, [P, DC, TOKENS], F32R) for name_ in ("rows_h", "rows_l"))
        zeros = s.sb("zeros", [P, 2 * D])
        zero_made, zeros_stored = s.sem("zero_made"), s.sem("zeros_stored")
        whole = s.sb("whole", [P, 2, GT])
        parts = [s.sb(name_, [P, DC, TOKENS], F32R) for name_ in ("part_h", "part_l")]
        turned = s.ps("turned", [P, 2, D])
        acc = s.ps("acc", [P, DC, D])
        w_loaded, w_h_ready, w_l_ready = s.sem("w_loaded"), s.sem("w_h_ready"), s.sem("w_l_ready")
        x_loaded = s.sems("x_loaded", GROUPS)
        stats_done, own = s.sem("stats_done"), s.sem("own")
        root_ask, root_done = s.sem("root_ask"), s.sem("root_done")
        norm_done, turn_done = s.sem("norm_done"), s.sem("turn_done")
        rows_h_ready, turned_free = s.sem("rows_h_ready"), s.sem("turned_free")
        proj_done, acc_free = s.sem("proj_done"), s.sem("acc_free")
        part_h_ready, part_l_ready = s.sem("part_h_ready"), s.sem("part_l_ready")
        out_stored = s.sem("out_stored")
        with nc.Block() as block:
            @block.sync
            def _(sp):
                for g in range(GROUPS):
                    at = slice(g * BPG, (g + 1) * BPG)
                    if source is not None:
                        sp.dma_start(k.x[:, at, :], source[:, at, :]).then_inc(x_loaded[g], 16)
                    if g == 0:
                        sp.dma_start(w[:, :, :], io[weight]).then_inc(w_loaded, 16)
                width, count = zeros.shape[1], 0
                if cleared:
                    sp.wait_ge(zero_made, 1)
                for dst in cleared:
                    flat = dst.rearrange("(p r) d -> p (r d)", p=P)
                    for at in range(0, flat.shape[1], width):
                        sp.dma_start(flat[:, at:at + width], zeros[:, :]).then_inc(zeros_stored, 16)
                        count += 1
                with sp.Fori(0, GROUPS) as g:
                    sp.wait_ge(part_l_ready, g * DC + (DC + 2))
                    for part in range(2):
                        sp.dma_start(out[part, :, :, bass.ds(g * GT, GT)],
                                     parts[part][:, :, bass.ds(g * GT, GT)].bitcast(F32)).then_inc(out_stored, 16)
                sp.wait_ge(out_stored, 32 * GROUPS)
                if cleared:
                    sp.wait_ge(zeros_stored, 16 * count)

            @block.gpsimd
            def _(pool):
                if cleared:
                    pool.memset(zeros[:, :], 0.0).then_inc(zero_made, 1)
                pool.wait_ge(w_h_ready, 1)
                low(pool, w_parts[1][:, :, :], w[:, :, :], w_parts[0][:, :, :]).then_inc(w_l_ready, 1)

            @block.vector
            def _(dve):
                step = Chain(dve, own)
                dve.sem_inc(turned_free, 2)
                if source is not None:
                    for g in range(GROUPS):
                        dve.wait_ge(x_loaded[g], 16)
                        with dve.Fori(g * BPG, (g + 1) * BPG) as b:
                            row_stats(dve, k, b, row(k.x, b)).then_inc(stats_done, 1)
                    dve.wait_ge(stats_done, BATCH)
                mean_and_variance(dve, step, k, n)
                step(dve.tensor_scalar(n.value[:, :], n.var[:, :], LN_EPS, None, ALU.add))
                inverse_root(dve, step, root_ask, root_done, 1, n.root, n.value, n.inv, n.a)

                def normalise(b, half):
                    dve.wait_ge(turn_done, b + 1)
                    dve.tensor_scalar(rows[:, half, :], row(k.x, b), n.mean[:, bass.ds(b, 1)],
                                      n.inv[:, bass.ds(b, 1)], ALU.subtract, ALU.mult).then_inc(norm_done, 1)

                def lower_rows(b, half):
                    dve.wait_ge(rows_h_ready, b + 1)
                    at = bass.ds(b * Q, Q)
                    low(dve, rows_l[:, :, at], turned[:, half, 0:DC * Q].rearrange("p (c q) -> p c q", c=DC),
                        rows_h[:, :, at]).then_inc(turned_free, 1)

                normalise(0, 0)
                for b in range(BPG):
                    normalise(b + 1, (b + 1) % 2)
                    lower_rows(b, b % 2)
                dve.sem_inc(acc_free, DC)
                dve.sem_inc(part_l_ready, 2)

                def take(g, m):
                    dve.wait_ge(proj_done, g * DC + (m + 1))
                    dve.wait_ge(part_l_ready, g * DC + (m + 1))
                    steps(dve, whole[:, m % 2, :], acc[:, m, 0:GT], m).then_inc(acc_free, 1)

                def lower_out(g, m):
                    dve.wait_ge(part_h_ready, g * DC + (m + 1))
                    at = bass.ds(g * GT, GT)
                    low(dve, parts[1][:, m, at], whole[:, m % 2, :], parts[0][:, m, at]).then_inc(part_l_ready, 1)

                def group(g, more, after):
                    for m in range(DC):
                        b = (g + 1) * BPG + m
                        if more and m < DC - 1 or after:
                            normalise(b + 1, (m + 1) % 2)
                        if more:
                            lower_rows(b, m % 2)
                        take(g, m)
                        if m:
                            lower_out(g, m - 1)
                    lower_out(g, DC - 1)

                with dve.Fori(0, GROUPS - 2) as g:
                    group(g, True, True)
                group(GROUPS - 2, True, False)
                group(GROUPS - 1, False, False)
                dve.wait_ge(acc_free, DC + GROUPS * DC)

            @block.scalar
            def _(act):
                def upper_rows(b, half):
                    act.wait_ge(turn_done, b + 3)
                    high(act, rows_h[:, :, bass.ds(b * Q, Q)],
                         turned[:, half, 0:DC * Q].rearrange("p (c q) -> p c q", c=DC)).then_inc(rows_h_ready, 1)

                def group(g, more):
                    for m in range(DC):
                        if more:
                            upper_rows((g + 1) * BPG + m, m % 2)
                        act.wait_ge(acc_free, DC + g * DC + (m + 1))
                        high(act, parts[0][:, m, bass.ds(g * GT, GT)], whole[:, m % 2, :]).then_inc(part_h_ready, 1)

                def upper_weights():
                    act.wait_ge(w_loaded, 16)
                    high(act, w_parts[0][:, :, :], w[:, :, :]).then_inc(w_h_ready, 1)

                if source is not None:
                    upper_weights()
                act.wait_ge(root_ask, 1)
                act.activation(n.root[:, :], n.value[:, :], ACT.Sqrt).then_inc(root_done, 1)
                if source is None:
                    upper_weights()
                for b in range(BPG):
                    upper_rows(b, b % 2)
                with act.Fori(0, GROUPS - 1) as g:
                    group(g, True)
                group(GROUPS - 1, False)

            @block.tensor
            def _(pe):
                def turn(b, half):
                    pe.wait_ge(norm_done, b + 1)
                    pe.wait_ge(turned_free, b + 1)
                    for c in range(DC):
                        mm = pe.transpose(turned[:, half, c * Q:(c + 1) * Q],
                                          rows[:, half, c * P:(c + 1) * P], k.ident[0:Q, 0:Q])
                    mm.then_inc(turn_done, 1)

                def group(g, more):
                    pe.wait_ge(turned_free, 2 + BPG + g * BPG)
                    for m in range(DC):
                        if more:
                            turn((g + 1) * BPG + m, m % 2)
                        pe.wait_ge(acc_free, g * DC + (m + 1))
                        for c in range(DC):
                            cols, at = slice(m * P, (m + 1) * P), bass.ds(g * GT, GT)
                            mm = times(pe, acc[:, m, 0:GT], [part[:, c, cols] for part in w_parts],
                                       (rows_h[:, c, at], rows_l[:, c, at]), c == 0, c == DC - 1)
                        mm.then_inc(proj_done, 1)

                pe.sem_inc(turn_done, 2)
                for b in range(BPG):
                    turn(b, b % 2)
                pe.wait_ge(w_l_ready, 1)
                with pe.Fori(0, GROUPS - 1) as g:
                    group(g, True)
                group(GROUPS - 1, False)


def row(t, b):
    return t[:, bass.ds(b, 1), :].rearrange("p a d -> p (a d)")


def first_attention(nc, io, k):
    SIDES = ((0, KEYS // 2 + 1), (KEYS // 2 + 1, KEYS // 2 - 1))
    N = SIDES[0][1]
    TRIPLE = 3 * HD
    K_CHUNKS = 2 * DC
    CHUNKS = K_CHUNKS + KTILES
    FIRST = 2
    assert CHUNKS + FIRST <= HEADS
    PER = CHUNKS + 1
    PAIR = 2 * HPC
    order = [("k", 0, 0), ("k", 1, 0), ("k", 0, 1), ("k", 1, 1)] + [("v", t, 0) for t in range(KTILES)] + \
            [("k", 2, 0), ("k", 3, 0), ("k", 2, 1), ("k", 3, 1)]
    side_free = [12, 14]
    PARTS = (0, 1, 0), (0, 0, 1)
    with Scope(nc, "xattn0") as s:
        wk, wv = ([s.sb(f"{n}{i}", [P, DC, D], F32R) for i in range(2)] for n in ("wk", "wv"))
        wo = s.sb("wo", [P, DC, D])
        bo = s.sb("bo", [Q, D])
        ctx_t = s.sb("ctx_t", [P, DC, KEYS])
        ctx_h, ctx_l = (s.sb(n, [P, DC, KEYS], F32R) for n in ("ctx_h", "ctx_l"))
        keys = [s.sb(n, [P, 2, KEYS], F32R) for n in ("keys_h", "keys_l")]
        k_raw = s.sb("k_raw", [P, 2, N])
        k_pack = s.sb("k_pack", [TRIPLE, HEADS, KEYS], F32R)
        q_pack = s.sb("q_pack", [TRIPLE, 2, HEADS, Q], F32R)
        vals = s.sb("vals", [P, 2, KTILES, D])
        neg_max = s.sb("neg_max", [Q, 2])
        total = s.sb("total", [Q, 2])
        inv_total = s.sb("inv_total", [Q, 2])
        probs = s.sb("probs", [Q, 2, KEYS])
        probs_t = s.sb("probs_t", [P, 2, KTILES, Q])
        out_t = s.sb("out_t", [P, DC, Q])
        x = s.sb("x", [Q, 2, D])
        scores = s.ps("scores", [P, 2, 2, D])
        turned = s.ps("turned", [P, 2, D])
        heads_out = s.ps("heads_out", [P, D])
        proj = s.ps("proj", [P, D])
        wk_loaded, wv_loaded, wo_loaded, w_h_ready, w_l_ready = (
            s.sem("wk_loaded"), s.sem("wv_loaded"), s.sem("wo_loaded"), s.sem("w_h_ready"), s.sem("w_l_ready"))
        ctx_loaded, ctx_h_ready, ctx_l_ready = s.sem("ctx_loaded"), s.sem("ctx_h_ready"), s.sem("ctx_l_ready")
        proj_done, bank_free, k_h_ready = s.sem("proj_done"), s.sem("bank_free"), s.sem("k_h_ready")
        k_l_ready = s.sem("k_l_ready")
        packed, q_loaded = s.sems("packed", 2), s.sems("q_loaded", 2)
        scores_done, max_ready = s.sem("scores_done"), s.sem("max_ready")
        exp_done, inv_done, probs_ready = s.sem("exp_done"), s.sem("inv_done"), s.sem("probs_ready")
        turn_done, probs_t_ready, values_done = s.sem("turn_done"), s.sem("probs_t_ready"), s.sem("values_done")
        out_t_ready, turned_cleared = s.sem("out_t_ready"), s.sem("turned_cleared")
        x_loaded, x_stored = s.sems("x_loaded", 2), s.sems("x_stored", 2)
        bo_added, x_added = s.sem("bo_added"), s.sem("x_added")

        PACKED = 16 * 3 * HPC

        def index(b, c):
            return CHUNKS + PER * b + c

        def k_index(c):
            return c if c < K_CHUNKS // 2 else c - KTILES

        def bank(n, c):
            return heads_out if n is None and c % 2 else proj

        def side_keys(side):
            return slice(SIDES[side][0], sum(SIDES[side]))

        def scores_of(h):
            return scores[0:Q, h % 2, :, :].rearrange("p s n -> p (s n)")[:, 2:2 * D]\
                .rearrange("p (s n) -> p s n", s=2)[:, :, 0:N - 1]

        with nc.Block() as block:
            @block.sync
            def _(sp):
                def load_ctx(b):
                    sp.dma_start(ctx_t[:, :, :], io["ctx_t"][bass.ds(b, 1)].rearrange("a p c n -> p (a c) n"))\
                      .then_inc(ctx_loaded, 16)

                def load_q(b, half):
                    for group, part in enumerate(PARTS[0]):
                        for j in range(HPC):
                            dst = q_pack[group * HD:(group + 1) * HD, half, :, :].bitcast(F32)\
                                .rearrange("p (m j) q -> p j m q", j=HPC)[:, j, :, :]
                            sp.dma_start(dst, io["q_parts"][part, j * HD:(j + 1) * HD, :, bass.ds(b * Q, Q)])\
                              .then_inc(q_loaded[half], 16)

                def pack(pair):
                    for j in range(HPC):
                        for group, part in enumerate(PARTS[1]):
                            dst = k_pack[group * HD:(group + 1) * HD, pair * PAIR:(pair + 1) * PAIR, :].bitcast(F32)\
                                .rearrange("p (m j) n -> p j m n", j=HPC)[:, j, :, :]
                            sp.dma_start(dst, keys[part][j * HD:(j + 1) * HD, :, :].bitcast(F32))\
                              .then_inc(packed[pair], 16)

                def load_x(b, half):
                    sp.dma_start(x[:, half, :], row(io["x"], b)).then_inc(x_loaded[half], 16)

                sp.dma_start(vals[:, 0, 0:DC, :], io["wk"]).then_inc(wk_loaded, 16)
                load_ctx(0)
                sp.dma_start(vals[:, 1, 0:DC, :], io["wv"]).then_inc(wv_loaded, 16)
                load_q(0, 0)
                load_q(1, 1)
                sp.dma_start(wo[:, :, :], io["wo"]).then_inc(wo_loaded, 16)
                sp.dma_start(bo[:, :], io["bo"].partition_broadcast(Q)).then_inc(wo_loaded, 16)
                load_x(0, 0)
                load_x(1, 1)
                sp.wait_ge(ctx_l_ready, 2)
                load_ctx(1)
                for pair in range(2):
                    if pair:
                        sp.wait_ge(packed[0], PACKED)
                    sp.wait_ge(k_l_ready, 2 + (pair + 1) * K_CHUNKS // 2)
                    pack(pair)
                def batch(b, i, half, more, after):
                    if after:
                        sp.wait_ge(ctx_l_ready, 2 * b + 4)
                        load_ctx(b + 2)
                    if more:
                        for pair in range(2):
                            if pair == 0:
                                sp.wait_ge(max_ready, b * HEADS + (PAIR + 1))
                            else:
                                sp.wait_ge(k_l_ready, b * K_CHUNKS + (2 * K_CHUNKS + 2))
                            pack(pair)
                            if pair and after:
                                load_q(b + 2, half)
                    sp.wait_ge(x_added, b + 1)
                    sp.dma_start(row(io["x1"], b), x[:, half, :]).then_inc(x_stored[half], 16)
                    if after:
                        sp.wait_ge(x_stored[half], 16 * i + 16)
                        load_x(b + 2, half)

                with sp.Fori(0, BATCH // 2 - 1) as i:
                    for half in range(2):
                        batch(2 * i + half, i, half, True, True)
                batch(BATCH - 2, BATCH // 2 - 1, 0, True, False)
                batch(BATCH - 1, BATCH // 2 - 1, 1, False, False)
                for half in range(2):
                    sp.wait_ge(x_stored[half], 16 * (BATCH // 2))

            @block.gpsimd
            def _(pool):
                def split_side(b, side):
                    pool.wait_ge(ctx_h_ready, 2 * b + (side + 1))
                    at = side_keys(side)
                    low(pool, ctx_l[:, :, at], ctx_t[:, :, at], ctx_h[:, :, at]).then_inc(ctx_l_ready, 1)

                def add_bo(i, half):
                    pool.wait_ge(x_loaded[half], 16 * i + 16)
                    pool.tensor_tensor(x[:, half, :], x[:, half, :], bo[:, :], ALU.add).then_inc(bo_added, 1)

                for side in range(2):
                    split_side(0, side)
                pool.wait_ge(wo_loaded, 32)
                add_bo(0, 0)
                for side in range(2):
                    split_side(1, side)
                add_bo(0, 1)
                with pool.Fori(0, BATCH // 2 - 1) as i:
                    for half in range(2):
                        for side in range(2):
                            split_side(2 * i + (half + 2), side)
                        add_bo(i + 1, half)
                pool.wait_ge(bo_added, BATCH)

            @block.tensor
            def _(pe):
                def make_chunk(n, c, half):
                    kind, m, side = order[c]
                    out = bank(n, c)
                    if n is not None:
                        pe.wait_ge(bank_free, index(n, c) + 1)
                    elif c:
                        pe.wait_ge(bank_free, c)
                    if kind == "k":
                        w = SIDES[side][1]
                        for d in range(DC):
                            mm = times(pe, out[:, 0:w], [part[:, d, m * P:(m + 1) * P] for part in wk],
                                       [part[:, d, side_keys(side)] for part in (ctx_h, ctx_l)], d == 0, d == DC - 1)
                    else:
                        w = P if m < KTILES - 1 else KLAST
                        for d in range(DC):
                            mm = times(pe, out[0:w, :], [part[:, d, m * P:m * P + w] for part in (ctx_h, ctx_l)],
                                       [part[:, d, :] for part in wv], d == 0, d == DC - 1)
                    mm.then_inc(proj_done, 1)

                def make_scores(g, h, half):
                    pe.matmul(scores[0:Q, h % 2, 0, 2:2 + N], q_pack[:, half, h, :], k_pack[:, h, 0:N],
                              start=True, stop=True)
                    pe.matmul(scores[0:Q, h % 2, 1, 0:N], q_pack[:, half, h, :], k_pack[:, h, KEYS - N:KEYS],
                              start=True, stop=True).then_inc(scores_done, 1)

                def turn(g, h):
                    pe.wait_ge(probs_ready, g + 1)
                    pe.wait_ge(probs_t_ready, g + 1)
                    for t in range(KTILES):
                        n = P if t < KTILES - 1 else KLAST
                        mm = pe.transpose(turned[0:n, t // 3, t % 3 * Q:(t % 3 + 1) * Q],
                                          probs[:, h % 2, t * P:t * P + n], k.ident[0:Q, 0:Q])
                    mm.then_inc(turn_done, 1)

                def times_values(g, h, half):
                    pe.wait_ge(probs_t_ready, g + 2)
                    m, j = divmod(h, HPC)
                    for t in range(KTILES):
                        n = P if t < KTILES - 1 else KLAST
                        mm = pe.matmul(heads_out[HD * j:HD * (j + 1), m * Q:(m + 1) * Q],
                                       vals[0:n, half, t, h * HD:(h + 1) * HD], probs_t[0:n, h % 2, t, :],
                                       start=(t == 0), stop=(t == KTILES - 1), tile_position=(0, HD * j))
                    mm.then_inc(values_done, 1)

                def project_out(b, n):
                    pe.wait_ge(out_t_ready, b + 2)
                    pe.wait_ge(bank_free, n + 1)
                    for c in range(DC):
                        mm = pe.matmul(proj[0:Q, :], out_t[:, c, :], wo[:, c, :], start=(c == 0), stop=(c == DC - 1))
                    mm.then_inc(proj_done, 1)

                def step(b, i, h, half, more):
                    g = b * HEADS + h
                    if h <= HEADS - 2:
                        if h + 1 == PAIR:
                            pe.wait_ge(packed[1], PACKED * b + PACKED)
                        pe.wait_ge(exp_done, g)
                        make_scores(g + 1, h + 1, half)
                    elif more:
                        if h == HEADS - 1:
                            pe.wait_ge(packed[0], PACKED * b + 2 * PACKED)
                            pe.wait_ge(q_loaded[1 - half], (16 * 3 * HPC) * (i + half) + 16 * 3 * HPC)
                        pe.wait_ge(exp_done, g)
                        make_scores(g + 1, h + 1 - HEADS, 1 - half)
                    if more and FIRST <= h < FIRST + CHUNKS:
                        c = h - FIRST
                        if order[c][0] == "k" and c in (0, 2):
                            pe.wait_ge(ctx_l_ready, 2 * b + (2 + c // 2 + 1))
                        make_chunk(b, c, 1 - half)

                def finish_step(b, h, half, more):
                    g = b * HEADS + h
                    if h < HEADS or more:
                        turn(g, h % HEADS)
                    if h == 1:
                        pe.wait_ge(out_t_ready, b + 1)
                    times_values(g - 1, h - 1, half)

                def batch(b, i, half, more):
                    for h in range(FIRST, HEADS + 1):
                        step(b, i, h, half, more)
                        finish_step(b, h, half, more)
                    if more:
                        step(b + 1, None, 1, 1 - half, more)
                        project_out(b, index(b, CHUNKS))
                        finish_step(b + 1, 1, 1 - half, True)
                    else:
                        project_out(b, index(b, 0))

                pe.sem_inc(turn_done, 2)
                pe.sem_inc(values_done, 2)
                pe.wait_ge(turned_cleared, 1)
                pe.wait_ge(w_l_ready, 1)
                pe.wait_ge(ctx_l_ready, 1)
                for c in range(CHUNKS):
                    if c == 2:
                        pe.wait_ge(ctx_l_ready, 2)
                    if c == K_CHUNKS // 2:
                        pe.wait_ge(w_l_ready, 2)
                    make_chunk(None, c, 0)
                pe.wait_ge(packed[0], PACKED)
                pe.wait_ge(q_loaded[0], 16 * 3 * HPC)
                pe.wait_ge(wo_loaded, 32)
                make_scores(0, 0, 0)
                make_scores(1, 1, 0)
                turn(0, 0)
                pe.wait_ge(bank_free, 1 + CHUNKS)
                step(0, None, 1, 0, True)
                finish_step(0, 1, 0, True)
                with pe.Fori(0, BATCH // 2 - 1) as i:
                    for half in range(2):
                        batch(2 * i + half, i, half, True)
                batch(BATCH - 2, BATCH // 2 - 1, 0, True)
                batch(BATCH - 1, BATCH // 2 - 1, 1, False)

            @block.scalar
            def _(act):
                def take_chunk(n, c, b_k, half):
                    kind, m, side = order[c]
                    act.wait_ge(proj_done, (index(n, c) if n is not None else c) + 1)
                    if kind == "k":
                        w = SIDES[side][1]
                        act.wait_ge(k_l_ready, b_k + (k_index(c) + 1))
                        dst, src = k_raw[:, k_index(c) % 2, 0:w], bank(n, c)[:, 0:w]
                    else:
                        w = P if m < KTILES - 1 else KLAST
                        if n is None:
                            act.wait_ge(w_l_ready, 2)
                        dst, src = vals[0:w, half, m, :], bank(n, c)[0:w, :]
                    act.activation(dst, src, ACT.Copy).then_inc(bank_free, 1)

                def exponentials(g, h):
                    act.wait_ge(max_ready, g + 1)
                    act.wait_ge(turn_done, g + 1)
                    act.activation(probs[:, h % 2, :].rearrange("p (s n) -> p s n", s=2), scores_of(h),
                                   ACT.Exp, bias=neg_max[:, h % 2:h % 2 + 1],
                                   accum_out=total[:, h % 2:h % 2 + 1]).then_inc(exp_done, 1)

                def copy_turned(g, h):
                    act.wait_ge(turn_done, g + 3)
                    act.wait_ge(values_done, g + 1)
                    act.activation(probs_t[:, h % 2, :, :].rearrange("p (s t) q -> p s (t q)", s=2),
                                   turned[:, :, 0:3 * Q], ACT.Copy).then_inc(probs_t_ready, 1)

                def split_side(b, side):
                    act.wait_ge(ctx_loaded, 16 * b + 16)
                    at = side_keys(side)
                    high(act, ctx_h[:, :, at], ctx_t[:, :, at]).then_inc(ctx_h_ready, 1)

                def step(b, h, half, more, after):
                    if h <= HEADS - 2 or more:
                        exponentials(b * HEADS + (h + 1), (h + 1) % HEADS)
                    if more and FIRST <= h < FIRST + CHUNKS:
                        take_chunk(b, h - FIRST, b * K_CHUNKS + K_CHUNKS, 1 - half)
                    if h < HEADS or more:
                        copy_turned(b * HEADS + h, h % HEADS)
                    if after and h - FIRST == side_free[0]:
                        act.wait_ge(proj_done, index(b, side_free[0]))
                        split_side(b + 2, 0)

                def batch(b, half, more, after):
                    for h in range(FIRST, HEADS + 1):
                        step(b, h, half, more, after)
                    if more:
                        step(b + 1, 1, 1 - half, True, False)
                    if after:
                        act.wait_ge(proj_done, index(b, side_free[1]))
                        split_side(b + 2, 1)

                act.wait_ge(wk_loaded, 16)
                high(act, wk[0][:, :, :], vals[:, 0, 0:DC, :]).then_inc(w_h_ready, 1)
                for side in range(2):
                    split_side(0, side)
                act.wait_ge(wv_loaded, 16)
                high(act, wv[0][:, :, :], vals[:, 1, 0:DC, :]).then_inc(w_h_ready, 1)
                for c in range(CHUNKS):
                    take_chunk(None, c, 0, 0)
                exponentials(0, 0)
                exponentials(1, 1)
                for side in range(2):
                    act.wait_ge(proj_done, side_free[side])
                    split_side(1, side)
                copy_turned(0, 0)
                step(0, 1, 0, True, False)
                with act.Fori(0, BATCH // 2 - 1) as i:
                    for half in range(2):
                        batch(2 * i + half, half, True, True)
                batch(BATCH - 2, 0, True, False)
                batch(BATCH - 1, 1, False, False)

            @block.vector
            def _(dve):
                def maximum(g, h):
                    dve.wait_ge(scores_done, g + 1)
                    dve.tensor_reduce(neg_max[:, h % 2:h % 2 + 1], scores_of(h), AX.XY, ALU.max,
                                      negate=True).then_inc(max_ready, 1)

                def divide(g, h):
                    one = slice(h % 2, h % 2 + 1)
                    dve.wait_ge(exp_done, g + 1)
                    dve.reciprocal(inv_total[:, one], total[:, one]).then_inc(inv_done, 1)
                    dve.wait_ge(inv_done, g + 1)
                    dve.tensor_scalar(probs[:, h % 2, :], probs[:, h % 2, :], inv_total[:, one], None,
                                      ALU.mult).then_inc(probs_ready, 1)

                def split_chunk(n, c):
                    kind, m, side = order[c]
                    if kind == "k":
                        number = (n * K_CHUNKS + K_CHUNKS if n is not None else 0) + k_index(c)
                        pair = m // 2
                        if n is not None and m % 2 == 0 and side == 0:
                            dve.wait_ge(packed[1 - pair], PACKED * n + (PACKED if pair == 0 else 2 * PACKED))
                        elif m == 2 and side == 0:
                            dve.wait_ge(packed[0], PACKED)
                        dve.wait_ge(bank_free, (index(n, c) if n is not None else c) + 2)
                        at, whole = side_keys(side), k_raw[:, k_index(c) % 2, 0:SIDES[side][1]]
                        dve.tensor_copy(keys[0][:, m % 2, at], whole).then_inc(k_h_ready, 1)
                        dve.wait_ge(k_h_ready, number + 1)
                        low(dve, keys[1][:, m % 2, at], whole, keys[0][:, m % 2, at]).then_inc(k_l_ready, 1)

                def step(b, h, half, more):
                    g = b * HEADS + h
                    scored = h <= HEADS - 2 or more
                    if scored:
                        maximum(g + 1, (h + 1) % HEADS)
                    if h == HEADS:
                        dve.wait_ge(values_done, g + 2)
                        dve.tensor_copy(out_t[:, :, :], heads_out[:, 0:DC * Q].rearrange("p (c q) -> p c q", c=DC))\
                           .then_inc(out_t_ready, 1)
                    if more and FIRST < h <= FIRST + CHUNKS:
                        split_chunk(b, h - FIRST - 1)
                    if scored:
                        divide(g + 1, (h + 1) % HEADS)

                def add_output(b, n, half):
                    dve.wait_ge(proj_done, n + 1)
                    dve.wait_ge(bo_added, b + 1)
                    dve.tensor_tensor(x[:, half, :], proj[0:Q, :], x[:, half, :], ALU.add).then_inc(bank_free, 1)
                    dve.wait_ge(bank_free, n + 2)
                    row_stats(dve, k, b, x[:, half, :]).then_inc(x_added, 1)

                def batch(b, half, more):
                    for h in range(FIRST, HEADS + 1):
                        step(b, h, half, more)
                    if more:
                        step(b + 1, 1, 1 - half, True)
                    add_output(b, index(b, CHUNKS if more else 0), half)

                dve.sem_inc(bank_free, 1)
                dve.sem_inc(k_l_ready, 2)
                dve.sem_inc(probs_t_ready, 1)
                dve.sem_inc(out_t_ready, 1)
                dve.memset(turned[:, :, :], 0.0).then_inc(turned_cleared, 1)
                for i, w in enumerate((wk, wv)):
                    dve.wait_ge(w_h_ready, i + 1)
                    low(dve, w[1][:, :, :], vals[:, i, 0:DC, :], w[0][:, :, :]).then_inc(w_l_ready, 1)
                for c in range(CHUNKS):
                    split_chunk(None, c)
                maximum(0, 0)
                maximum(1, 1)
                divide(0, 0)
                divide(1, 1)
                step(0, 1, 0, True)
                with dve.Fori(0, BATCH // 2 - 1) as i:
                    for half in range(2):
                        batch(2 * i + half, half, True)
                batch(BATCH - 2, 0, True)
                batch(BATCH - 1, 1, False)
                dve.wait_ge(x_added, BATCH)


def norm_and_route(nc, io, k, name, h_all, logits, gate, rms, source=None):
    with Scope(nc, name) as s:
        n = NormBuffers(s)
        w = s.sb("w", [P, DC, E])
        rows = s.sb("rows", [Q, 2, D])
        h = s.sb("h", [Q, 2, D]) if rms else rows
        weight = s.sb("weight", [Q, D])
        rows_t = s.sb("rows_t", [P, 2, DC, Q])
        turned = s.ps("turned", [P, 2, D])
        acc = s.ps("acc", [P, 2, D])
        w_loaded, own = s.sem("w_loaded"), s.sem("own")
        root_ask, root_done = s.sem("root_ask"), s.sem("root_done")
        norm_done, h_done, turn_done = s.sem("norm_done"), s.sem("h_done"), s.sem("turn_done")
        turned_out, logits_done, logits_out, kept = (
            s.sem("turned_out"), s.sem("logits_done"), s.sem("logits_out"), s.sem("kept"))
        x_added = s.sem("x_added")
        x_loaded = s.sems("x_loaded", GROUPS)
        with nc.Block() as block:
            @block.sync
            def _(sp):
                if source is not None:
                    for g in range(GROUPS):
                        at = slice(g * BPG, (g + 1) * BPG)
                        sp.dma_start(k.x[:, at, :], source[:, at, :]).then_inc(x_loaded[g], 16)
                sp.dma_start(w[:, :, :], io[gate]).then_inc(w_loaded, 16)
                sp.dma_start(weight[:, :], io["norm_w"].partition_broadcast(Q)).then_inc(w_loaded, 16)

            @block.vector
            def _(dve):
                step = Chain(dve, own)
                mean_and_variance(dve, step, k, n)
                step(dve.tensor_scalar(n.value[:, :], n.var[:, :], LN_EPS, None, ALU.add))
                inverse_root(dve, step, root_ask, root_done, 1, n.root, n.value, n.inv, n.a)
                if rms:
                    step(dve.tensor_tensor(n.a[:, :], n.inv[:, :], n.inv[:, :], ALU.mult))
                    step(dve.tensor_tensor(n.value[:, :], n.a[:, :], n.var[:, :], ALU.mult))
                    step(dve.tensor_scalar(n.value[:, :], n.value[:, :], RMS_EPS, None, ALU.add))
                    inverse_root(dve, step, root_ask, root_done, 2, n.root, n.value, n.inv2, n.a)
                dve.wait_ge(w_loaded, 32)
                dve.sem_inc(logits_out, 2)

                def take_logits(b, half):
                    dve.wait_ge(logits_done, b + 3)
                    dve.tensor_copy(logits[:, bass.ds(b, 1), :].rearrange("p a e -> p (a e)"),
                                    acc[0:Q, half, 0:E]).then_inc(logits_out, 1)

                def normalise(b, half):
                    dve.wait_ge(turn_done, b + 1)
                    dve.wait_ge(x_added if rms else kept, b + 1)
                    dve.tensor_scalar(rows[:, half, :], row(k.x, b), n.mean[:, bass.ds(b, 1)],
                                      n.inv[:, bass.ds(b, 1)], ALU.subtract, ALU.mult).then_inc(norm_done, 1)
                    if rms:
                        dve.wait_ge(kept, b + 1)
                        dve.wait_ge(norm_done, b + 1)
                        dve.scalar_tensor_tensor(h[:, half, :], rows[:, half, :], n.inv2[:, bass.ds(b, 1)],
                                                 weight[:, :], ALU.mult, ALU.mult).then_inc(h_done, 1)

                for g in range(GROUPS):
                    if source is not None:
                        dve.wait_ge(x_loaded[g], 16)
                    if g == 0:
                        for half in range(2):
                            normalise(half, half)
                    with dve.Fori(max(0, g * BPG // 2 - 1), (g + 1) * BPG // 2 - 1) as i:
                        for half in range(2):
                            normalise(2 * i + (half + 2), half)
                            take_logits(2 * i + half, half)
                for half in range(2):
                    take_logits(BATCH - 2 + half, half)
                dve.wait_ge(logits_out, 2 + BATCH)

            @block.gpsimd
            def _(pool):
                if not rms:
                    return
                pool.sem_inc(x_added, 2)
                with pool.Fori(0, BATCH // 2) as i:
                    for half in range(2):
                        b = 2 * i + half
                        pool.wait_ge(norm_done, b + 1)
                        pool.tensor_tensor(row(k.x, b), row(k.x, b), rows[:, half, :], ALU.add).then_inc(x_added, 1)
                pool.wait_ge(x_added, 2 + BATCH)

            @block.scalar
            def _(act):
                act.wait_ge(root_ask, 1)
                act.activation(n.root[:, :], n.value[:, :], ACT.Sqrt).then_inc(root_done, 1)
                if rms:
                    act.wait_ge(root_ask, 2)
                    act.activation(n.root[:, :], n.value[:, :], ACT.Sqrt).then_inc(root_done, 1)
                act.sem_inc(turned_out, 2)
                act.sem_inc(kept, 2)
                with act.Fori(0, BATCH // 2) as i:
                    for half in range(2):
                        b = 2 * i + half
                        act.wait_ge(h_done if rms else norm_done, b + 1)
                        act.activation(row(h_all, b), h[:, half, :], ACT.Copy).then_inc(kept, 1)
                        act.wait_ge(turn_done, b + 3)
                        act.wait_ge(logits_done, b + 1)
                        act.activation(rows_t[:, half, :, :],
                                       turned[:, half, 0:DC * Q].rearrange("p (c q) -> p c q", c=DC),
                                       ACT.Copy).then_inc(turned_out, 1)
                act.wait_ge(kept, 2 + BATCH)

            @block.tensor
            def _(pe):
                pe.sem_inc(turn_done, 2)
                pe.sem_inc(logits_done, 2)
                pe.wait_ge(w_loaded, 32)

                def turn(b, half):
                    pe.wait_ge(h_done if rms else norm_done, b + 1)
                    pe.wait_ge(turned_out, b + 1)
                    for c in range(DC):
                        mm = pe.transpose(turned[:, half, c * Q:(c + 1) * Q], h[:, half, c * P:(c + 1) * P],
                                          k.ident[0:Q, 0:Q])
                    mm.then_inc(turn_done, 1)

                def dot_gate(b, half):
                    pe.wait_ge(turned_out, b + 3)
                    pe.wait_ge(logits_out, b + 1)
                    for c in range(DC):
                        mm = pe.matmul(acc[0:Q, half, 0:E], rows_t[:, half, c, :], w[:, c, :],
                                       start=(c == 0), stop=(c == DC - 1))
                    mm.then_inc(logits_done, 1)

                for half in range(2):
                    turn(half, half)
                with pe.Fori(0, BATCH // 2 - 1) as i:
                    for half in range(2):
                        dot_gate(2 * i + half, half)
                        turn(2 * i + (half + 2), half)
                for half in range(2):
                    dot_gate(BATCH - 2 + half, half)


class Routing:

    def __init__(self, s, top):
        self.logits = s.sb("logits", [Q, BATCH, E])
        self.hot = [s.sb(f"hot{i}", [Q, BATCH, E]) for i in range(top)]
        self.weight = [s.sb(f"weight{i}", [Q, BATCH]) for i in range(top)]
        self.slot = [s.sb(f"slot{i}", [Q, BATCH], I32) for i in range(top)]
        self.send = [s.sb(f"send{i}", [Q, BATCH], I32) for i in range(top)]
        self.block_expert = s.sb("block_expert", [1, BLOCKS0], I32)


def along(v, n):
    return v.unsqueeze(2).to_broadcast([v.shape[0], v.shape[1], n])


def between(v, n):
    return v.unsqueeze(1).to_broadcast([v.shape[0], n, v.shape[1]])


def route(nc, io, k, r, name, top, bias):
    with Scope(nc, name) as s:
        gate_bias = s.sb("gate_bias", [Q, E])
        left = s.sb("left", [Q, BATCH, E])
        same = s.sb("same", [Q, BATCH, E])
        peak = [s.sb(f"peak{i}", [Q, BATCH]) for i in range(2)]
        first = s.sb("first", [Q, BATCH])
        t = s.sb("t", [Q, BATCH, E])
        both = s.sb("both", [Q, BATCH, E])
        earlier = s.sb("earlier", [Q, BATCH + 1, E])
        count = s.sb("count", [Q, E])
        blocks = s.sb("blocks", [Q, E])
        start = s.sb("start", [Q, E])
        cover = s.sb("cover", [Q, E, COUNTS0])
        pairs = s.sb("pairs", [Q, E, E])
        owner = s.sb("owner", [Q, BLOCKS0, E])
        owner_of = s.sb("owner_of", [Q, BLOCKS0])
        a, b_, c_ = (s.sb(f"v{i}", [Q, BATCH]) for i in range(3))
        token_i = s.sb("token_i", [Q, BATCH], I32)
        token = s.sb("token", [Q, BATCH])
        rank = s.ps("rank", [P, D])
        totals = s.ps("totals", [P, D])
        loaded, own, ask_exp, exp_done = s.sem("loaded"), s.sem("own"), s.sem("ask_exp"), s.sem("exp_done")
        hot_ready, ranked, token_made = s.sem("hot_ready"), s.sem("ranked"), s.sem("token_made")
        with nc.Block() as block:
            @block.sync
            def _(sp):
                if bias is not None:
                    sp.dma_start(gate_bias[:, :], io[bias].partition_broadcast(Q)).then_inc(loaded, 16)

            @block.gpsimd
            def _(pool):
                pool.iota(token_i[:, :], [[Q, BATCH]], base=0, channel_multiplier=1).then_inc(token_made, 1)

            @block.tensor
            def _(pe):
                pe.wait_ge(hot_ready, 1)
                flat = both[:, :, :].rearrange("p b e -> p (b e)")
                before = earlier[:, 0:BATCH, :].rearrange("p b e -> p (b e)")
                pe.matmul(rank[0:Q, 0:BATCH * E], k.before[0:Q, 0:Q], flat, start=True, stop=False)
                pe.matmul(rank[0:Q, 0:BATCH * E], k.ones[0:Q, 0:Q], before, start=False, stop=True)
                pe.matmul(totals[0:Q, 0:E], k.ones[0:Q, 0:Q], earlier[:, BATCH, :],
                          start=True, stop=True).then_inc(ranked, 1)

            @block.scalar
            def _(act):
                act.wait_ge(ask_exp, 1)
                if top == 2:
                    act.activation(a[:, :], b_[:, :], ACT.Exp).then_inc(exp_done, 1)
                else:
                    act.activation(t[:, :, :], left[:, :, :], ACT.Exp).then_inc(exp_done, 1)

            @block.vector
            def _(dve):
                step = Chain(dve, own)
                if bias is not None:
                    dve.wait_ge(loaded, 16)
                    step(dve.tensor_tensor(r.logits[:, :, :], r.logits[:, :, :], between(gate_bias[:, :], BATCH), ALU.add))
                dve.wait_ge(token_made, 1)
                step(dve.tensor_copy(token[:, :], token_i[:, :]))
                step(dve.tensor_copy(left[:, :, :], r.logits[:, :, :]))
                experts = between(k.ramp[0:Q, 0:E], BATCH)
                for i in range(top):
                    step(dve.tensor_reduce(peak[i][:, :], left[:, :, :], AX.X, ALU.max))
                    step(dve.tensor_tensor(same[:, :, :], left[:, :, :], along(peak[i][:, :], E), ALU.is_equal))
                    step(dve.tensor_scalar(t[:, :, :], same[:, :, :], -float(E), float(E), ALU.mult, ALU.add))
                    step(dve.tensor_tensor(same[:, :, :], same[:, :, :], experts, ALU.mult))
                    step(dve.tensor_tensor(t[:, :, :], t[:, :, :], same[:, :, :], ALU.add))
                    step(dve.tensor_reduce(first[:, :], t[:, :, :], AX.X, ALU.min))
                    step(dve.scalar_tensor_tensor(first[:, :], first[:, :], float(E), first[:, :], ALU.is_lt, ALU.mult))
                    step(dve.tensor_tensor(r.hot[i][:, :, :], experts, along(first[:, :], E), ALU.is_equal))
                    if i + 1 < top:
                        step(dve.scalar_tensor_tensor(left[:, :, :], r.hot[i][:, :, :], LOWEST, left[:, :, :],
                                                      ALU.mult, ALU.add))
                if top == 2:
                    step(dve.tensor_tensor(both[:, :, :], r.hot[0][:, :, :], r.hot[1][:, :, :], ALU.add))
                else:
                    step(dve.tensor_copy(both[:, :, :], r.hot[0][:, :, :]))
                step(dve.memset(earlier[:, 0, :], 0.0))
                for i in range(BATCH):
                    step(dve.tensor_tensor(earlier[:, i + 1, :], earlier[:, i, :], both[:, i, :], ALU.add))
                dve.nop().then_inc(hot_ready, 1)
                if top == 2:
                    step(dve.tensor_tensor(b_[:, :], peak[1][:, :], peak[0][:, :], ALU.subtract))
                    dve.nop().then_inc(ask_exp, 1)
                    dve.wait_ge(exp_done, 1)
                    step(dve.tensor_scalar(c_[:, :], a[:, :], 1.0, None, ALU.add))
                    step(dve.reciprocal(r.weight[0][:, :], c_[:, :]))
                    step(dve.tensor_tensor(r.weight[1][:, :], r.weight[0][:, :], a[:, :], ALU.mult))
                else:
                    step(dve.tensor_tensor(left[:, :, :], r.logits[:, :, :], along(peak[0][:, :], E), ALU.subtract))
                    dve.nop().then_inc(ask_exp, 1)
                    dve.wait_ge(exp_done, 1)
                    step(dve.tensor_reduce(a[:, :], t[:, :, :], AX.X, ALU.add))
                    step(dve.reciprocal(r.weight[0][:, :], a[:, :]))
                dve.wait_ge(ranked, 1)
                ranks = rank[0:Q, 0:BATCH * E].rearrange("p (b e) -> p b e", e=E)
                if top == 2:
                    step(dve.tensor_copy(count[:, :], totals[0:Q, 0:E]))
                    step(dve.tensor_scalar(blocks[:, :], k.ramp[0:Q, 0:E], float(BLK), None, ALU.mult))
                    step(dve.tensor_tensor(cover[:, :, :], along(count[:, :], COUNTS0),
                                           between(blocks[:, 0:COUNTS0], E), ALU.is_gt))
                    step(dve.tensor_reduce(blocks[:, :], cover[:, :, :], AX.X, ALU.add))
                    step(dve.tensor_tensor(pairs[:, :, :], k.expert_before[0:Q, :, :], between(blocks[:, :], E), ALU.mult))
                    step(dve.tensor_reduce(start[:, :], pairs[:, :, :], AX.X, ALU.add))
                    step(dve.tensor_tensor(count[:, :], start[:, :], blocks[:, :], ALU.add))
                    step(dve.tensor_tensor(owner[:, :, :], along(k.ramp[0:Q, 0:BLOCKS0], E),
                                           between(count[:, :], BLOCKS0), ALU.is_ge))
                    step(dve.tensor_reduce(owner_of[:, :], owner[:, :, :], AX.X, ALU.add))
                    step(dve.tensor_scalar(owner_of[:, :], owner_of[:, :], float(E - 1), None, ALU.min))
                    step(dve.tensor_copy(r.block_expert[:, :], owner_of[0:1, :]))
                    step(dve.tensor_scalar(start[:, :], start[:, :], float(BLK), None, ALU.mult))
                else:
                    step(dve.tensor_scalar(start[:, :], k.ramp[0:Q, 0:E], float(BLK), None, ALU.mult))
                for i in range(top):
                    if top == 2:
                        step(dve.tensor_tensor(t[:, :, :], ranks, between(start[:, :], BATCH), ALU.add))
                        step(dve.tensor_tensor(t[:, :, :], t[:, :, :], r.hot[i][:, :, :], ALU.mult))
                        step(dve.tensor_reduce(a[:, :], t[:, :, :], AX.X, ALU.add))
                        step(dve.tensor_copy(r.slot[i][:, :], a[:, :]))
                        step(dve.tensor_copy(r.send[i][:, :], a[:, :]))
                    else:
                        step(dve.tensor_tensor(t[:, :, :], ranks, r.hot[i][:, :, :], ALU.mult))
                        step(dve.tensor_reduce(a[:, :], t[:, :, :], AX.X, ALU.add))
                        step(dve.tensor_scalar(b_[:, :], a[:, :], float(CAP1), None, ALU.is_lt))
                        step(dve.tensor_tensor(t[:, :, :], between(start[:, :], BATCH), r.hot[i][:, :, :], ALU.mult))
                        step(dve.tensor_reduce(c_[:, :], t[:, :, :], AX.X, ALU.add))
                        step(dve.tensor_tensor(a[:, :], a[:, :], c_[:, :], ALU.add))
                        step(dve.tensor_tensor(a[:, :], a[:, :], b_[:, :], ALU.mult))
                        step(dve.tensor_copy(r.slot[i][:, :], a[:, :]))
                        step(dve.tensor_scalar(token[:, :], token[:, :], float(SLOTS1), None, ALU.add))
                        step(dve.tensor_scalar(c_[:, :], b_[:, :], -1.0, 1.0, ALU.mult, ALU.add))
                        step(dve.tensor_tensor(token[:, :], token[:, :], c_[:, :], ALU.mult))
                        step(dve.tensor_tensor(a[:, :], a[:, :], token[:, :], ALU.add))
                        step(dve.tensor_copy(r.send[i][:, :], a[:, :]))
                        step(dve.tensor_tensor(r.weight[i][:, :], r.weight[i][:, :], b_[:, :], ALU.mult))


def send_rows(nc, r, h_all, slots, name, top):
    with Scope(nc, name) as s:
        sent = s.sem("sent")
        with nc.Block() as block:
            @block.gpsimd
            def _(pool):
                for b in range(BATCH):
                    for i in range(top):
                        pool.indirect_dma_start(slots, bass.IndirectOffsetOnAxis(ap=r.send[i][:, b:b + 1], axis=0),
                                                h_all[:, b, :], None).then_inc(sent, 16)
                pool.wait_ge(sent, 16 * BATCH * top)


def gather_outputs(nc, k, r, name, top, outputs, out):
    with Scope(nc, name) as s:
        got = s.sb("got", [Q, BATCH, top, D])
        stats_done = s.sem("stats_done")
        fetched, added, own, stored = s.sems("fetched", BATCH), s.sem("added"), s.sem("own"), s.sem("stored")
        with nc.Block() as block:
            @block.gpsimd
            def _(pool):
                for b in range(BATCH):
                    for i in range(top):
                        pool.indirect_dma_start(got[:, b, i, :], None, outputs,
                                                bass.IndirectOffsetOnAxis(ap=r.slot[i][:, b:b + 1], axis=0))\
                            .then_inc(fetched[b], 16)

            @block.vector
            def _(dve):
                step = Chain(dve, own)
                for b in range(BATCH):
                    dve.wait_ge(fetched[b], 16 * top)
                    for i in range(top):
                        ins = dve.scalar_tensor_tensor(k.x[:, b, :], got[:, b, i, :], r.weight[i][:, b:b + 1],
                                                       k.x[:, b, :], ALU.mult, ALU.add)
                        if i < top - 1:
                            step(ins)
                        else:
                            ins.then_inc(added, 1)
                    if out is None:
                        dve.wait_ge(added, b + 1)
                        row_stats(dve, k, b, k.x[:, b, :]).then_inc(stats_done, 1)
                dve.wait_ge(added, BATCH)
                if out is None:
                    dve.wait_ge(stats_done, BATCH)

            if out is not None:
                @block.sync
                def _(sp):
                    for b in range(BATCH):
                        sp.wait_ge(added, b + 1)
                        sp.dma_start(out[b], k.x[:, b, :]).then_inc(stored, 16)
                    sp.wait_ge(stored, 16 * BATCH)


def second_attention(nc, io, k, wu):
    SIDES = ((0, KEYS // 2 + 1), (KEYS // 2 + 1, KEYS // 2 - 1))
    assert all(n % 2 == 0 for _, n in SIDES)
    CHUNKS = 2 * DC
    OWN = 4
    TURN_AFTER = DC
    with Scope(nc, "xattn1") as s:
        masks = s.sb("masks", [Q, BATCH, KEYS], U8)
        hide = s.sb("hide", [Q, KEYS])
        ctx_t = s.sb("ctx_t", [P, 2, DC, KEYS])
        ctx_t_h, ctx_t_l = (s.sb(n, [P, DC, KEYS], F32R) for n in ("ctx_t_h", "ctx_t_l"))
        ctx = s.sb("ctx", [P, KTILES, D])
        ctx_h, ctx_l = (s.sb(n, [P, KTILES, D], F32R) for n in ("ctx_h", "ctx_l"))
        up = [s.sb(n, [P, 2, DC, Q], F32R) for n in ("up_h", "up_l")]
        uq_h, uq_l = (s.sb(n, [P, DC, KEYS], F32R) for n in ("uq_h", "uq_l"))
        masked = s.sb("masked", [Q, KEYS])
        peak, neg_peak, total, inv_total = (s.sb(n, [Q, 1]) for n in ("peak", "neg_peak", "total", "inv_total"))
        probs = s.sb("probs", [Q, KEYS])
        probs_h, probs_l = (s.sb(n, [P, KTILES, Q], F32R) for n in ("probs_h", "probs_l"))
        hid = s.ps("hid", [P, 2, D])
        scores = s.ps("scores", [P, 2, D])
        turned = s.ps("turned", [P, 2, D])
        mixed = s.ps("mixed", [P, D])
        masks_loaded, ctx_t_loaded, ctx_loaded = s.sem("masks_loaded"), s.sems("ctx_t_loaded", 2), s.sem("ctx_loaded")
        ctx_t_h_ready, ctx_t_l_ready = s.sem("ctx_t_h_ready"), s.sem("ctx_t_l_ready")
        ctx_h_ready, ctx_l_ready = s.sem("ctx_h_ready"), s.sem("ctx_l_ready")
        uq_done, uq_h_ready, uq_l_ready = s.sem("uq_done"), s.sem("uq_h_ready"), s.sem("uq_l_ready")
        up_loaded = s.sems("up_loaded", 2)
        scores_done, own, exp_done = s.sem("scores_done"), s.sem("own"), s.sem("exp_done")
        turn_done, probs_h_ready, probs_l_ready = s.sem("turn_done"), s.sem("probs_h_ready"), s.sem("probs_l_ready")
        peak_done = s.sem("peak_done")
        stats_done = s.sem("stats_done")
        mixed_done, x_added, prepared = s.sem("mixed_done"), s.sem("x_added"), s.sem("prepared")

        def steps(step, eng):
            step(-1, 1, False, True, True)
            with eng.Fori(0, BATCH // 2 - 1) as i:
                for half in range(2):
                    step(2 * i + half, half, True, True, True)
            step(BATCH - 2, 0, True, True, False)
            step(BATCH - 1, 1, True, False, False)

        def up_count(b, half):
            return 16 * (b + (2 if half == 0 else 3))

        def chunk(c):
            side, m = divmod(c, DC)
            return side, m, slice(SIDES[side][0], sum(SIDES[side]))

        with nc.Block() as block:
            @block.sync
            def _(sp):
                def load_t(b, half):
                    wait(sp, ctx_t_l_ready, 2 * b - 2)
                    sp.dma_start(ctx_t[:, half, :, :], io["ctx_t"][bass.ds(b, 1)].rearrange("a p c n -> p (a c) n"))\
                      .then_inc(ctx_t_loaded[half], 16)

                def load(b):
                    wait(sp, ctx_l_ready, b)
                    rows = io["ctx"][bass.ds(b, 1)].rearrange("a n d -> (a n) d")
                    sp.dma_start(ctx[:, 0:KTILES - 1, :],
                                 rows[0:KEYS - KLAST, :].rearrange("(t p) d -> p t d", p=P)).then_inc(ctx_loaded, 16)
                    sp.dma_start(ctx[0:KLAST, KTILES - 1, :], rows[KEYS - KLAST:KEYS, :]).then_inc(ctx_loaded, 16)

                def load_up(b, half):
                    for part in range(2):
                        sp.dma_start(up[part][:, half, :, :].bitcast(F32), io["up_parts"][part, :, :, bass.ds(b * Q, Q)])\
                          .then_inc(up_loaded[half], 16)

                load_t(0, 0)
                load_up(0, 0)
                load_t(1, 1)
                load_up(1, 1)
                sp.dma_start(masks[:, :, :].rearrange("p b n -> p (b n)"), io["mask"].partition_broadcast(Q))\
                  .then_inc(masks_loaded, 16)
                sp.wait_ge(prepared, 2)
                load(0)
                with sp.Fori(0, BATCH // 2 - 1) as i:
                    for half in range(2):
                        b = 2 * i + half
                        load_t(b + 2, half)
                        sp.wait_ge(scores_done, b + 1)
                        load_up(b + 2, half)
                        load(b + 1)
                load(BATCH - 1)

            @block.tensor
            def _(pe):
                def step(b, half, now, next_, after):
                    for c in range(CHUNKS if next_ else 0):
                        side, m, keys = chunk(c)
                        if m == 0:
                            pe.wait_ge(ctx_t_l_ready, 2 * b + (2 + side + 1))
                        pe.wait_ge(uq_l_ready, CHUNKS * b + (CHUNKS + c + 1))
                        for d in range(DC):
                            mm = times(pe, hid[:, c % 2, 0:SIDES[side][1]], [w[:, d, m * P:(m + 1) * P] for w in wu],
                                       (ctx_t_h[:, d, keys], ctx_t_l[:, d, keys]), d == 0, d == DC - 1)
                        mm.then_inc(uq_done, 1)
                        if c == TURN_AFTER and now:
                            turn(b)
                    if now:
                        if not next_:
                            turn(b)
                        pe.wait_ge(probs_l_ready, b + 1)
                        pe.wait_ge(ctx_l_ready, b + 1)
                        wait(pe, x_added, b)
                        for t in range(KTILES):
                            n = P if t < KTILES - 1 else KLAST
                            mm = times(pe, mixed[0:Q, :], (probs_h[0:n, t, :], probs_l[0:n, t, :]),
                                       (ctx_h[0:n, t, :], ctx_l[0:n, t, :]), t == 0, t == KTILES - 1)
                        mm.then_inc(mixed_done, 1)
                    if next_:
                        pe.wait_ge(uq_l_ready, CHUNKS * b + (2 * CHUNKS + 2))
                        pe.wait_ge(up_loaded[1 - half], up_count(b, half))
                        wait(pe, own, OWN * b + 2)
                        for side, (at, n) in enumerate(SIDES):
                            for d in range(DC):
                                mm = times(pe, scores[0:Q, side, 0:n], [part[:, 1 - half, d, :] for part in up],
                                           (uq_h[:, d, at:at + n], uq_l[:, d, at:at + n]), d == 0, d == DC - 1)
                        mm.then_inc(scores_done, 1)

                def turn(b):
                    pe.wait_ge(exp_done, b + 1)
                    wait(pe, probs_l_ready, b)
                    for t in range(KTILES):
                        n = P if t < KTILES - 1 else KLAST
                        mm = pe.transpose(turned[0:n, t // 3, t % 3 * Q:(t % 3 + 1) * Q],
                                          probs[:, t * P:t * P + n], k.ident[0:Q, 0:Q])
                    mm.then_inc(turn_done, 1)

                pe.wait_ge(prepared, 2)
                steps(step, pe)

            @block.gpsimd
            def _(pool):
                def step(b, half, now, next_, after):
                    if not next_:
                        return
                    pool.wait_ge(ctx_h_ready, b + 2)
                    low(pool, ctx_l[:, :, :], ctx[:, :, :], ctx_h[:, :, :]).then_inc(ctx_l_ready, 1)

                steps(step, pool)

            def raw_count(b, half):
                return 8 * (b - half) + 16

            def split_side(b, side, eng, make, loaded, ready):
                keys = slice(SIDES[side][0], sum(SIDES[side]))
                eng.wait_ge(*loaded)
                wait(eng, uq_done, CHUNKS * b + ((side + 1) * DC - CHUNKS))
                make(keys).then_inc(ready, 1)

            @block.scalar
            def _(act):
                def upper_side(b, half, side):
                    split_side(b, side, act, lambda keys: high(act, ctx_t_h[:, :, keys], ctx_t[:, half, :, keys]),
                               (ctx_t_loaded[half], raw_count(b, half)), ctx_t_h_ready)

                def step(b, half, now, next_, after):
                    for c in range(CHUNKS if next_ else 0):
                        side, m, keys = chunk(c)
                        act.wait_ge(uq_done, CHUNKS * b + (CHUNKS + c + 1))
                        high(act, uq_h[:, m, keys], hid[:, c % 2, 0:SIDES[side][1]], ACT.Relu).then_inc(uq_h_ready, 1)
                        if c == 0 and now:
                            exponentials(b)
                        if c == TURN_AFTER and now:
                            upper_probs(b)
                        if c % DC == DC - 1 and after:
                            upper_side(b + 2, half, side)
                    if now and not next_:
                        exponentials(b)
                        upper_probs(b)
                    if next_:
                        wait(act, mixed_done, b + 1)
                        act.wait_ge(ctx_loaded, 32 * b + 64)
                        high(act, ctx_h[:, :, :], ctx[:, :, :]).then_inc(ctx_h_ready, 1)

                def exponentials(b):
                    act.wait_ge(own, OWN * b + 3)
                    act.activation(probs[:, :], masked[:, :], ACT.Exp, bias=neg_peak[:, :],
                                   accum_out=total[:, :]).then_inc(exp_done, 1)

                def upper_probs(b):
                    act.wait_ge(turn_done, b + 1)
                    high(act, probs_h[:, :, :].rearrange("p (s t) q -> p s (t q)", s=2), turned[:, :, 0:3 * Q])\
                        .then_inc(probs_h_ready, 1)

                for side in range(2):
                    upper_side(0, 0, side)
                act.wait_ge(prepared, 2)
                steps(step, act)

            @block.vector
            def _(dve):
                def lower_side(b, half, side):
                    split_side(b, side, dve,
                               lambda keys: low(dve, ctx_t_l[:, :, keys], ctx_t[:, half, :, keys], ctx_t_h[:, :, keys]),
                               (ctx_t_h_ready, 2 * b + (side + 1)), ctx_t_l_ready)

                def lower_probs(b):
                    dve.wait_ge(probs_h_ready, b + 1)
                    low(dve, probs_l[:, :, :].rearrange("p (s t) q -> p s (t q)", s=2), turned[:, :, 0:3 * Q],
                        probs_h[:, :, :].rearrange("p (s t) q -> p s (t q)", s=2)).then_inc(probs_l_ready, 1)
                    dve.reciprocal(inv_total[:, :], total[:, :]).then_inc(own, 1)

                def step(b, half, now, next_, after):
                    for c in range(CHUNKS if next_ else 0):
                        side, m, keys = chunk(c)
                        dve.wait_ge(uq_h_ready, CHUNKS * b + (CHUNKS + c + 1))
                        dve.scalar_tensor_tensor(uq_l[:, m, keys], hid[:, c % 2, 0:SIDES[side][1]], 0.0,
                                                 uq_h[:, m, keys].bitcast(F32), ALU.max, ALU.subtract)\
                           .then_inc(uq_l_ready, 1)
                        if c == TURN_AFTER and now:
                            lower_probs(b)
                        if c % DC == DC - 1 and after:
                            lower_side(b + 2, half, side)
                    if now:
                        if not next_:
                            lower_probs(b)
                        dve.wait_ge(own, OWN * b + OWN)
                        dve.wait_ge(mixed_done, b + 1)
                        dve.scalar_tensor_tensor(row(k.x, b), mixed[0:Q, :], inv_total[:, :], row(k.x, b),
                                                 ALU.mult, ALU.add).then_inc(x_added, 1)
                    if next_:
                        dve.tensor_scalar(hide[:, :], row(masks, b + 1), LOWEST, None, ALU.mult).then_inc(own, 1)
                        dve.wait_ge(own, OWN * b + (OWN + 1))
                        dve.wait_ge(scores_done, b + 2)
                        wait(dve, exp_done, b + 1)
                        for side, (at, n) in enumerate(SIDES):
                            ins = dve.tensor_tensor(masked[:, at:at + n], scores[0:Q, side, 0:n], hide[:, at:at + n], ALU.add)
                        ins.then_inc(own, 1)
                        dve.wait_ge(own, OWN * b + (OWN + 2))
                        dve.tensor_reduce(peak[:, :], masked[:, :], AX.X, ALU.max).then_inc(peak_done, 1)
                        dve.wait_ge(peak_done, b + 2)
                        dve.tensor_scalar(neg_peak[:, :], peak[:, :], FLOOR, -1.0, ALU.max, ALU.mult).then_inc(own, 1)
                    if now:
                        dve.wait_ge(x_added, b + 1)
                        row_stats(dve, k, b, row(k.x, b)).then_inc(stats_done, 1)

                dve.sem_inc(uq_l_ready, 2)
                dve.memset(turned[:, :, :], 0.0).then_inc(prepared, 1)
                dve.memset(ctx[:, KTILES - 1, :], 0.0).then_inc(prepared, 1)
                for side in range(2):
                    lower_side(0, 0, side)
                dve.wait_ge(prepared, 2)
                dve.wait_ge(masks_loaded, 16)
                steps(step, dve)
                dve.wait_ge(stats_done, BATCH)


def experts(nc, io, ident, name, blocks, gated, block_expert):
    PAIRS = NW if gated else F1 // P // 2
    TILES = PAIRS if gated else 2 * PAIRS
    OUTS = TILES // 2
    CH = PAIRS + OUTS
    RING = CH if CH <= 8 else 8
    assert CH % RING == 0
    LAPS = CH // RING
    POOLS = (1, 3, 5) if gated else (1, 4, 7)
    W = 2 * D
    with Scope(nc, name) as s:
        raw = s.sb("raw", [P, RING, W])
        upper = s.sb("upper", [P, RING, W], F32R)
        lower = s.sb("lower", [P, RING, W], F32R)
        b1 = s.sb("b1", [P, blocks, 2 * PAIRS])
        b2 = s.sb("b2", [P, blocks, D])
        rows = s.sb("rows", [P, 2, D])
        rows_h, rows_l = (s.sb(n, [P, DC, BLK], F32R) for n in ("rows_h", "rows_l"))
        act_h, act_l = (s.sb(n, [P, TILES, BLK], F32R) for n in ("act_h", "act_l"))
        act_f = s.sb("act_f", [P, 2, 2 * BLK])
        y = s.sb("y", [P, 2, D])
        if gated:
            glu, lin, sig = (s.sb(n, [P, 2, BLK]) for n in ("glu", "lin", "sig"))
        hidden = s.ps("hidden", [P, 4, 2, BLK])
        turned = s.ps("turned", [P, DC, BLK])
        out = s.ps("out", [P, 2, D])
        b2_loaded = s.sem("b2_loaded")
        rows_loaded, raw_loaded = s.sem("rows_loaded"), s.sems("raw_loaded", RING)
        upper_ready, lower_ready = s.sems("upper_ready", RING), s.sems("lower_ready", RING)
        chunk_done, turn_done = s.sem("chunk_done"), s.sem("turn_done")
        rows_h_ready, rows_l_ready = s.sem("rows_h_ready"), s.sem("rows_l_ready")
        hidden_free, act_made, act_h_ready, act_ready = (
            s.sem("hidden_free"), s.sem("act_made"), s.sem("act_h_ready"), s.sem("act_ready"))
        y_ready, stored, glu_ready, sig_ready, own = (
            s.sem("y_ready"), s.sem("stored"), s.sem("glu_ready"), s.sem("sig_ready"), s.sem("own"))
        slots, results, weights, biases, out_biases = (
            io[n + name[-1]] for n in ("slots", "results", "chunks", "b1_", "b2_"))

        def used(j, c):
            return j * LAPS + (c // RING + 1)

        def ahead(j, c):
            return (j, c + RING) if c + RING < CH else (j + 1, c + RING - CH)

        def each_ahead(j, last, do):
            for c in range(CH):
                nj, nc_ = ahead(j, c)
                if not (last and nj is not j):
                    do(nj, nc_)

        with nc.Block() as block:
            @block.sync
            def _(sp):
                def load(j):
                    sp.wait_ge(turn_done, j + 1)
                    sp.dma_start(rows[:, :, :], slots[bass.ds(j * BLK, BLK), :].rearrange("(t p) d -> p t d", p=P))\
                      .then_inc(rows_loaded, 16)
                    e = j
                    if gated:
                        e = sp.value_load(block_expert[0:1, bass.ds(j, 1)], min_val=0, max_val=E - 1)
                    sp.dma_start(b1[:, bass.ds(j, 1), :].rearrange("p a f -> p (a f)"),
                                 biases[bass.ds(e, 1)].rearrange("a p f -> p (a f)")).then_inc(rows_loaded, 16)
                    for c in range(CH):
                        sp.wait_ge(lower_ready[c % RING], used(j, c))
                        sp.dma_start(raw[:, c % RING, :], weights[bass.ds(e, 1), c].rearrange("a p w -> p (a w)"))\
                          .then_inc(raw_loaded[c % RING], 16)
                    sp.dma_start(b2[:, bass.ds(j, 1), :].rearrange("p a d -> p (a d)"),
                                 out_biases[bass.ds(e, 1)].rearrange("a d -> (a d)").partition_broadcast(P))\
                      .then_inc(b2_loaded, 16)

                with sp.Fori(0, blocks) as j:
                    load(j)

            @block.tensor
            def _(pe):
                def turn(j):
                    pe.wait_ge(rows_loaded, 32 * j + 32)
                    pe.wait_ge(rows_l_ready, j + 1)
                    for t in range(2):
                        for d in range(DC):
                            mm = pe.transpose(turned[:, d, t * P:(t + 1) * P], rows[:, t, d * P:(d + 1) * P],
                                              ident[:, :])
                    mm.then_inc(turn_done, 1)

                def block_of(j, last):
                    pe.wait_ge(rows_l_ready, j + 2)
                    for c in range(PAIRS):
                        w_h, w_l = (w[:, c % RING, :].rearrange("p (s d f) -> p s d f", s=2, d=DC) for w in (upper, lower))
                        pe.wait_ge(lower_ready[c % RING], used(j, c) + 1)
                        pe.wait_ge(hidden_free, j * PAIRS + (c + 1))
                        for side in range(2):
                            for d in range(DC):
                                mm = times(pe, hidden[:, c % 4, side, :], (w_h[:, side, d, :], w_l[:, side, d, :]),
                                           (rows_h[:, d, :], rows_l[:, d, :]), d == 0, d == DC - 1)
                        mm.then_inc(chunk_done, 1)
                    if not last:
                        turn(j + 1)
                    pe.wait_ge(y_ready, 2 * j + 2)
                    for o in range(OUTS):
                        c = PAIRS + o
                        w_h, w_l = (w[:, c % RING, :].rearrange("p (s d) -> p s d", s=2) for w in (upper, lower))
                        pe.wait_ge(lower_ready[c % RING], used(j, c) + 1)
                        if not gated:
                            pe.wait_ge(act_ready, j * PAIRS + (o + 3))
                        for side in range(2):
                            f = 2 * o + side
                            if gated:
                                pe.wait_ge(act_ready, j * PAIRS + (f + 1))
                            for t in range(2):
                                cols = slice(t * P, (t + 1) * P)
                                mm = times(pe, out[:, t, :], (act_h[:, f, cols], act_l[:, f, cols]),
                                           (w_h[:, side, :], w_l[:, side, :]), f == 0, f == TILES - 1)
                        mm.then_inc(chunk_done, 1)

                pe.sem_inc(chunk_done, RING)
                pe.sem_inc(turn_done, 1)
                turn(0)
                with pe.Fori(0, blocks - 1) as j:
                    block_of(j, False)
                block_of(blocks - 1, True)

            def make_lower(eng, j, c):
                eng.wait_ge(upper_ready[c % RING], used(j, c))
                low(eng, lower[:, c % RING, :], raw[:, c % RING, :], upper[:, c % RING, :])\
                    .then_inc(lower_ready[c % RING], 1)

            @block.gpsimd
            def _(pool):
                def mine(j, c):
                    if c % RING in POOLS:
                        make_lower(pool, j, c)

                for c in POOLS:
                    pool.sem_inc(lower_ready[c], 1)
                for c in range(RING):
                    mine(0, c)
                with pool.Fori(0, blocks - 1) as j:
                    each_ahead(j, False, mine)
                each_ahead(blocks - 1, True, mine)

            @block.scalar
            def _(act):
                def make_upper(j, c):
                    act.wait_ge(raw_loaded[c % RING], 16 * used(j, c))
                    act.wait_ge(chunk_done, j * CH + (c + 1))
                    high(act, upper[:, c % RING, :], raw[:, c % RING, :]).then_inc(upper_ready[c % RING], 1)

                def copy_turned(j):
                    act.wait_ge(turn_done, j + 2)
                    high(act, rows_h[:, :, :], turned[:, :, :]).then_inc(rows_h_ready, 1)

                def chunk_of(j, c, last):
                    if c < PAIRS and gated:
                        act.wait_ge(glu_ready, j * PAIRS + (c + 1))
                        act.activation(sig[:, c % 2, :], glu[:, c % 2, :], ACT.Sigmoid, scale=ALPHA).then_inc(sig_ready, 1)
                    elif c < PAIRS:
                        act.wait_ge(chunk_done, j * CH + (c + 1 + RING))
                        act.wait_ge(act_ready, j * PAIRS + (c + 1))
                        for side in range(2):
                            f = 2 * c + side
                            act.activation(act_f[:, c % 2, side * BLK:(side + 1) * BLK], hidden[:, c % 4, side, :],
                                           ACT.Gelu, bias=b1[:, bass.ds(j, 1), f]).then_inc(act_made, 1)
                    nj, nc_ = ahead(j, c)
                    urgent = gated and c == PAIRS - 1
                    if not (last and nj is not j) and not urgent:
                        make_upper(nj, nc_)
                    if c < PAIRS and gated:
                        act.wait_ge(act_made, j * PAIRS + (c + 1))
                        high(act, act_h[:, c, :], act_f[:, c % 2, 0:BLK]).then_inc(act_h_ready, 1)
                    if not (last and nj is not j) and urgent:
                        make_upper(nj, nc_)
                    if c == PAIRS - 1 and not last:
                        copy_turned(j + 1)

                def block_of(j, next_last=False, last=False):
                    for c in range(1, CH):
                        chunk_of(j, c, last)
                    if not last:
                        chunk_of(j + 1, 0, next_last)
                    act.wait_ge(y_ready, 2 * j + 4)
                    act.dma_start(results[bass.ds(j * BLK, BLK), :].rearrange("(t p) d -> p t d", p=P), y[:, :, :])\
                       .then_inc(stored, 16)

                act.sem_inc(stored, 16)
                for c in range(RING):
                    make_upper(0, c)
                copy_turned(0)
                chunk_of(0, 0, False)
                with act.Fori(0, blocks - 2) as j:
                    block_of(j)
                block_of(blocks - 2, next_last=True)
                block_of(blocks - 1, last=True)
                act.wait_ge(stored, 16 * blocks + 16)

            @block.vector
            def _(dve):
                def mine(j, c):
                    if c % RING not in POOLS:
                        make_lower(dve, j, c)

                def split_turned(j):
                    dve.wait_ge(rows_h_ready, j + 1)
                    low(dve, rows_l[:, :, :], turned[:, :, :], rows_h[:, :, :]).then_inc(rows_l_ready, 1)

                def lower_act(j, c):
                    if gated:
                        whole, upper_part, part = act_f[:, c % 2, 0:BLK], act_h[:, c, :], act_l[:, c, :]
                    else:
                        whole = act_f[:, c % 2, :]
                        upper_part, part = (a[:, 2 * c:2 * c + 2, :].rearrange("p s n -> p (s n)") for a in (act_h, act_l))
                    dve.wait_ge(act_h_ready, j * PAIRS + (c + 1))
                    low(dve, part, whole, upper_part).then_inc(act_ready, 1)

                def block_of(j, last):
                    for c in range(CH):
                        one = c % 2
                        if c < PAIRS and gated:
                            dve.wait_ge(chunk_done, j * CH + (c + 1 + RING))
                            dve.tensor_scalar(glu[:, one, :], hidden[:, c % 4, 0, :], b1[:, bass.ds(j, 1), c], LIMIT,
                                              ALU.add, ALU.min).then_inc(glu_ready, 1)
                            dve.tensor_scalar(lin[:, one, :], hidden[:, c % 4, 1, :], b1[:, bass.ds(j, 1), PAIRS + c],
                                              LIMIT, ALU.add, ALU.min).then_inc(hidden_free, 1)
                            dve.wait_ge(hidden_free, j * PAIRS + (c + 5))
                            dve.tensor_scalar(lin[:, one, :], lin[:, one, :], -LIMIT, 1.0, ALU.max, ALU.add).then_inc(own, 1)
                            if c > 0:
                                lower_act(j, c - 1)
                            dve.wait_ge(sig_ready, j * PAIRS + (c + 1))
                            dve.tensor_tensor(glu[:, one, :], glu[:, one, :], sig[:, one, :], ALU.mult).then_inc(own, 1)
                            dve.wait_ge(own, 2 * PAIRS * j + (2 * c + 2))
                            dve.tensor_tensor(act_f[:, one, 0:BLK], glu[:, one, :], lin[:, one, :], ALU.mult)\
                               .then_inc(act_made, 1)
                        elif c < PAIRS:
                            dve.wait_ge(act_made, j * TILES + (2 * c + 2))
                            dve.sem_inc(hidden_free, 1)
                            dve.tensor_copy(act_h[:, 2 * c:2 * c + 2, :].rearrange("p s n -> p (s n)"), act_f[:, one, :])\
                               .then_inc(act_h_ready, 1)
                            lower_act(j, c)
                        if gated and c == PAIRS - 1:
                            lower_act(j, c)
                        for late in [c - 1, c] if gated and c == PAIRS - 1 else [] if gated and c == PAIRS - 2 else [c]:
                            nj, nc_ = ahead(j, late)
                            if not (last and nj is not j):
                                mine(nj, nc_)
                        if c == PAIRS - 1:
                            if not last:
                                split_turned(j + 1)
                    dve.wait_ge(stored, 16 * j + 16)
                    dve.wait_ge(b2_loaded, 16 * j + 16)
                    dve.wait_ge(chunk_done, j * CH + (CH + RING))
                    for t in range(2):
                        dve.tensor_tensor(y[:, t, :], out[:, t, :],
                                          b2[:, bass.ds(j, 1), :].rearrange("p a d -> p (a d)"), ALU.add)\
                           .then_inc(y_ready, 1)

                for c in range(RING):
                    if c not in POOLS:
                        dve.sem_inc(lower_ready[c], 1)
                dve.sem_inc(rows_l_ready, 1)
                dve.sem_inc(y_ready, 2)
                dve.sem_inc(hidden_free, 4)
                if not gated:
                    dve.sem_inc(act_ready, 2)
                for c in range(RING):
                    mine(0, c)
                split_turned(0)
                with dve.Fori(0, blocks - 1) as j:
                    block_of(j, False)
                block_of(blocks - 1, True)


class Keep:
    pass


def build(nc, io):
    with ExitStack() as whole:
        def sb(name, shape, dt=F32):
            return whole.enter_context(nc.sbuf_tensor(name, shape, dt))

        k = Keep()
        k.ident = sb("ident", [P, P])
        k.ones = sb("ones", [P, P])
        k.before = sb("before", [P, P])
        k.ramp_i = sb("ramp_i", [P, P], I32)
        k.ramp = sb("ramp", [P, P])
        k.expert_before = sb("expert_before", [P, E, E])
        k.scale_row = sb("scale_row", [P, DC])
        k.stats = sb("stats", [Q, BATCH, 6])
        load_constants(nc, io, k)

        with Scope(nc, "before0") as s:
            k.x = s.sb("x", [Q, BATCH, D])
            wq = [s.sb(f"wq{i}", [P, DC, D], F32R) for i in range(2)]
            norm_and_project(nc, io, k, "queries", "wq", wq, io["q_parts"],
                             lambda dve, out, acc, m: dve.tensor_scalar(out, acc, SCALE, None, ALU.mult), io["x"],
                             [io["slots0"], io["slots1"][0:SLOTS1, :]])
        first_attention(nc, io, k)
        k.x = sb("x", [Q, BATCH, D])
        with Scope(nc, "ffn0") as s:
            r = Routing(s, TOP0)
            with Scope(nc, "ffn0h") as sh:
                h_all = sh.sb("h_all", [Q, BATCH, D])
                norm_and_route(nc, io, k, "route_norm0", h_all, r.logits, "gate0", True, io["x1"])
                route(nc, io, k, r, "route0", TOP0, "gate_b")
                send_rows(nc, r, h_all, io["slots0"], "send0", TOP0)
            experts(nc, io, k.ident, "experts0", BLOCKS0, True, r.block_expert)
            gather_outputs(nc, k, r, "gather0", TOP0, io["results0"], None)
        with Scope(nc, "attention1") as s:
            wu = [s.sb(f"wu{i}", [P, DC, D], F32R) for i in range(2)]
            norm_and_project(nc, io, k, "up", "u", wu, io["up_parts"],
                             lambda dve, out, acc, m: dve.tensor_scalar(out, acc, 0.0, k.scale_row[:, m:m + 1],
                                                                        ALU.max, ALU.mult))
            second_attention(nc, io, k, wu)
        with Scope(nc, "ffn1") as s:
            r = Routing(s, 1)
            with Scope(nc, "ffn1h") as sh:
                h_all = sh.sb("h_all", [Q, BATCH, D])
                norm_and_route(nc, io, k, "route_norm1", h_all, r.logits, "gate1", False)
                route(nc, io, k, r, "route1", 1, None)
                send_rows(nc, r, h_all, io["slots1"], "send1", 1)
            experts(nc, io, k.ident, "experts1", E, False, None)
            gather_outputs(nc, k, r, "gather1", 1, io["results1"], io["out"])


def lay_out(a):
    def turn(w):
        return w.T.reshape(-1, P, w.shape[0]).transpose(1, 0, 2)

    def chunks(w1, w2):
        return np.concatenate([w1.reshape(E, -1, P, 2 * D), w2.reshape(E, -1, P, 2 * D)], axis=1)

    w1 = a["L0_ffn_mlp1_w"]
    return {
        "x": a["x"].transpose(1, 0, 2),
        "ctx": a["ctx_1024"],
        "ctx_t": a["ctx_1024"].transpose(0, 2, 1).reshape(BATCH, DC, P, KEYS).transpose(0, 2, 1, 3),
        "mask": a["mask_BxS2_bk1"].reshape(BATCH * KEYS),
        "wq": turn(a["L0_xattn_wq"]), "wk": turn(a["L0_xattn_wk"]), "wv": turn(a["L0_xattn_wv"]),
        "wo": turn(a["L0_xattn_wo"]), "bo": a["L0_xattn_bo"],
        "norm_w": a["L0_ffn_norm_w"], "gate0": turn(a["L0_ffn_gate_w"]), "gate_b": a["L0_ffn_gate_b"],
        "chunks0": chunks(w1.reshape(E, NW, P, 2, DC, P).transpose(0, 1, 5, 3, 4, 2),
                          a["L0_ffn_mlp2_w"].reshape(E, D, NW // 2, 2, P).transpose(0, 2, 4, 3, 1)),
        "b1_0": a["L0_ffn_mlp1_b"].reshape(E, NW, P, 2).transpose(0, 2, 3, 1).reshape(E, P, 2 * NW),
        "b2_0": a["L0_ffn_mlp2_b"],
        "u": turn(a["L1_xattn_U_w"]), "d_param": a["L1_xattn_D_param"].reshape(DC, P).T,
        "gate1": a["L1_ffn_wg"].reshape(DC, P, E).transpose(1, 0, 2),
        "chunks1": chunks(a["L1_ffn_W1"].reshape(E, DC, P, F1 // P // 2, 2, P).transpose(0, 3, 2, 4, 1, 5),
                          a["L1_ffn_W2"].reshape(E, F1 // P // 2, 2, P, D).transpose(0, 1, 3, 2, 4)),
        "b1_1": a["L1_ffn_b1"].reshape(E, F1 // P, P).transpose(0, 2, 1),
        "b2_1": a["L1_ffn_b2"],
    }


def scratch(nc):
    shapes = {"x1": [Q, BATCH, D], "q_parts": [2, P, DC, TOKENS], "up_parts": [2, P, DC, TOKENS],
              "slots0": [SLOTS0, D], "results0": [SLOTS0, D], "slots1": [SLOTS1 + TOKENS, D], "results1": [SLOTS1, D]}
    return {n: nc.dram_tensor(n, shape, F32, kind="Internal").ap() for n, shape in shapes.items()}


def kernel(**inputs):
    import concourse.bacc as bacc
    from concourse.bass_utils import run_bass_kernel_spmd as run

    arrays = {f"in_{n}": np.ascontiguousarray(v) for n, v in lay_out({n: np.asarray(v) for n, v in inputs.items()}).items()}
    nc = bacc.Bacc("TRN2", target_bir_lowering=False, num_devices=1)
    io = {n[3:]: nc.dram_tensor(n, v.shape, mybir.dt.from_np(v.dtype), kind="ExternalInput").ap() for n, v in arrays.items()}
    io.update(scratch(nc))
    io["out"] = nc.dram_tensor("out", [BATCH, Q, D], F32, kind="ExternalOutput").ap()
    build(nc, io)
    got = run(nc, [arrays], core_ids=[0])
    return got.results[0]["out"]
```
